# Optimizing a Trainium2 kernel written in Bass

```python
import numpy as np
import jax
import jax.numpy as jnp

def _softmax(x, axis=-1):
    return jax.nn.softmax(x, axis=axis)

def _gelu(x):
    return jax.nn.gelu(x, approximate=True)

def _silu(x):
    return jax.nn.silu(x)

def _sigmoid(x):
    return jax.nn.sigmoid(x)

def _layernorm(x, axis=-1, eps=1e-05):
    m = jnp.mean(x, axis=axis, keepdims=True)
    v = jnp.var(x, axis=axis, keepdims=True)
    return (x - m) / jnp.sqrt(v + eps)

def _scatter_add(tgt, idx, src, axis=0):
    return tgt.at[idx].add(src)

def _segment_sum(src, seg, n):
    return jax.ops.segment_sum(src, seg, n)
kernel_name = 'mk_xattn_ffn_d4_seqx_r8_bc3fcb'

def setup_inputs(seed: int=0):
    np.random.seed(seed)
    _w = jnp.asarray

    def _rec_inputs():
        import jax
        import jax.numpy as jnp
        _rk = jax.random.key(seed)
        x = 7.22e-05 + 1 * jax.random.normal(jax.random.fold_in(_rk, 1), (16, 64, 512), jnp.float32)
        _lenS = 64 - jax.random.randint(jax.random.fold_in(_rk, 7), (16,), 0, max(1, 64 // 4) + 1, jnp.int32)
        _lenS2 = 64 - jax.random.randint(jax.random.fold_in(_rk, 8), (16,), 0, max(1, 64 // 4) + 1, jnp.int32)
        _ctx_4096P = jax.random.normal(jax.random.fold_in(_rk, 11), (16, 16, 512), jnp.float32)
        _ctx_4096c = jax.random.dirichlet(jax.random.fold_in(_rk, 511), 0.3 * jnp.ones((16,), jnp.float32), (16, 64))
        _ctx_4096t = jnp.einsum('bsk,bkd->bsd', _ctx_4096c, _ctx_4096P)
        _ctx_4096t = _ctx_4096t * jax.lax.rsqrt(jnp.mean(jnp.square(_ctx_4096t)) + 1e-12) * 0.953939
        ctx_4096 = 4.13588e-05 + 0.999923 * (_ctx_4096t + 0.3 * jax.random.normal(jax.random.fold_in(_rk, 611), (16, 64, 512), jnp.float32))
        pos_BxS2 = jnp.broadcast_to(jnp.arange(64, dtype=jnp.int32), (16, 64))
        _validS = jnp.arange(64)[None, :] < _lenS[:, None]
        _validS2 = jnp.arange(64)[None, :] < _lenS2[:, None]
        _causal = jnp.tril(jnp.ones((64, 64), dtype=bool))
        mask_BxSxS2_ik0 = jnp.where(jnp.broadcast_to(_validS2[:, None, :], (16, 64, 64)), 0, 1).astype(jnp.int32)
        return (x, ctx_4096, pos_BxS2, mask_BxSxS2_ik0)
    x, ctx_4096, pos_BxS2, mask_BxSxS2_ik0 = _rec_inputs()

    def _L0_xattn_setup():
        import jax, jax.numpy as jnp
        import numpy as np
        HEADS = 8
        WINDOW = 16

        def _pointwise(W, b, t):
            return jnp.einsum('oc,bct->bot', W, t) + b[None, :, None]
        key = jax.random.key(seed)
        ks = jax.random.split(key, 10)
        B, C, T = (4, 64, 512)
        s = 0.02
        return {'x': jax.random.normal(ks[0], (B, C, T), jnp.float32), 'cond': jax.random.normal(ks[1], (B, C, T), jnp.float32), 'Wq': jax.random.normal(ks[2], (C, C), jnp.float32) * s, 'bq': jnp.zeros((C,), jnp.float32), 'Wk': jax.random.normal(ks[3], (C, C), jnp.float32) * s, 'bk': jnp.zeros((C,), jnp.float32), 'Wv': jax.random.normal(ks[4], (C, C), jnp.float32) * s, 'bv': jnp.zeros((C,), jnp.float32), 'Wo': jax.random.normal(ks[5], (C, C), jnp.float32) * s, 'bo': jnp.zeros((C,), jnp.float32)}
    _L0_xattn_all = _L0_xattn_setup()
    _L0_xattn_in = {k: v for k, v in _L0_xattn_all.items() if k in ('Wq', 'bq', 'Wk', 'bk', 'Wv', 'bv', 'Wo', 'bo')}
    del _L0_xattn_all

    def _L0_ffn_setup():
        import jax, jax.numpy as jnp
        import numpy as np
        TOP_K = 2
        key = jax.random.key(seed)
        k1, k2, k3 = jax.random.split(key, 3)
        B, S, H, O, E = (32, 1, 512, 512, 8)
        x = jax.random.normal(k1, (B, S, H), dtype=jnp.float32)
        gate_w = jax.random.normal(k2, (H, E), dtype=jnp.float32) * 0.02
        expert_w = jax.random.normal(k3, (E, H, O), dtype=jnp.float32) * 0.02
        return {'x': x, 'gate_w': gate_w, 'expert_w': expert_w}
    _L0_ffn_all = _L0_ffn_setup()
    _L0_ffn_in = {k: v for k, v in _L0_ffn_all.items() if k in ('gate_w', 'expert_w')}
    del _L0_ffn_all

    def _L1_xattn_setup():
        import jax, jax.numpy as jnp
        import numpy as np
        EMB_DIM = 64
        HEADS = 8
        key = jax.random.key(seed)
        kq, kk, kv = jax.random.split(key, 3)
        B, C, N = (8, EMB_DIM, 512)
        q = jax.random.normal(kq, (B, C, N), dtype=jnp.float32)
        k = jax.random.normal(kk, (B, C, N), dtype=jnp.float32)
        v = jax.random.normal(kv, (B, C, N), dtype=jnp.float32)
        return {'q': q, 'k': k, 'v': v}
    _L1_xattn_all = _L1_xattn_setup()
    _L1_xattn_in = {k: v for k, v in _L1_xattn_all.items() if k in ()}
    del _L1_xattn_all

    def _L1_ffn_setup():
        import jax, jax.numpy as jnp
        import numpy as np
        HID, INT, LAT, NE, K = (512, 1024, 256, 8, 2)
        LN_EPS = 1e-05

        def _layernorm(x, gamma, beta):
            mu = jnp.mean(x, axis=-1, keepdims=True)
            var = jnp.var(x, axis=-1, keepdims=True)
            return (x - mu) * jax.lax.rsqrt(var + LN_EPS) * gamma + beta
        key = jax.random.key(seed)
        ks = jax.random.split(key, 8)
        s = lambda d: 1.0 / np.sqrt(d)
        return {'hidden_states': jax.random.normal(ks[0], (4, 256, HID), jnp.float32), 'gate_w': jax.random.normal(ks[1], (HID, NE), jnp.float32) * s(HID), 'up_w': jax.random.normal(ks[2], (HID, INT), jnp.float32) * s(HID), 'down_w': jax.random.normal(ks[3], (INT, HID), jnp.float32) * s(INT), 'fc1_w': jax.random.normal(ks[4], (HID, LAT), jnp.float32) * s(HID), 'fc2_w': jax.random.normal(ks[5], (LAT, HID), jnp.float32) * s(LAT), 'expert_w': jax.random.normal(ks[6], (LAT, LAT), jnp.float32), 'ln_gamma': jnp.ones((HID,), jnp.float32), 'ln_beta': jnp.zeros((HID,), jnp.float32)}
    _L1_ffn_all = _L1_ffn_setup()
    _L1_ffn_in = {k: v for k, v in _L1_ffn_all.items() if k in ('gate_w', 'up_w', 'down_w', 'fc1_w', 'fc2_w', 'expert_w', 'ln_gamma', 'ln_beta')}
    del _L1_ffn_all

    def _L2_xattn_setup():
        import jax, jax.numpy as jnp
        import numpy as np
        B, S, E = (2, 256, 512)
        H, KVH, D = (32, 8, 128)
        GROUPS = H // KVH
        MAX_POS = 512
        ROPE_THETA = 10000.0

        def _rope_tables(max_pos, dim, theta):
            inv_freq = 1.0 / theta ** (jnp.arange(0, dim, 2, dtype=jnp.float32) / dim)
            t = jnp.arange(max_pos, dtype=jnp.float32)
            freqs = jnp.einsum('i,j->ij', t, inv_freq)
            emb = jnp.concatenate([freqs, freqs], axis=-1)
            return (jnp.cos(emb), jnp.sin(emb))

        def _rotate_half(x):
            x1, x2 = (x[..., :x.shape[-1] // 2], x[..., x.shape[-1] // 2:])
            return jnp.concatenate([-x2, x1], axis=-1)
        key = jax.random.key(seed)
        ks = jax.random.split(key, 8)
        scale_w = 1.0 / np.sqrt(E)
        query = jax.random.normal(ks[0], (B, S, E), dtype=jnp.float32)
        k_in = jax.random.normal(ks[1], (B, S, E), dtype=jnp.float32)
        v_in = jax.random.normal(ks[2], (B, S, E), dtype=jnp.float32)
        position_ids = jnp.broadcast_to(jnp.arange(S, dtype=jnp.int64), (B, S))
        src_mask = jnp.tril(jnp.ones((S, S), dtype=jnp.int32))
        src_mask = jnp.broadcast_to(src_mask, (B, S, S))
        Wq = jax.random.normal(ks[3], (E, H * D), dtype=jnp.float32) * scale_w
        Wk = jax.random.normal(ks[4], (E, KVH * D), dtype=jnp.float32) * scale_w
        Wv = jax.random.normal(ks[5], (E, KVH * D), dtype=jnp.float32) * scale_w
        Wo = jax.random.normal(ks[6], (H * D, E), dtype=jnp.float32) * scale_w
        return {'query': query, 'key': k_in, 'value': v_in, 'position_ids': position_ids, 'src_mask': src_mask, 'Wq': Wq, 'Wk': Wk, 'Wv': Wv, 'Wo': Wo}
    _L2_xattn_all = _L2_xattn_setup()
    _L2_xattn_in = {k: v for k, v in _L2_xattn_all.items() if k in ('Wq', 'Wk', 'Wv', 'Wo')}
    del _L2_xattn_all

    def _L2_ffn_setup():
        import jax, jax.numpy as jnp
        import numpy as np
        IN_F = 512
        OUT_F = 512
        N_CLUSTERS = 64
        THRESHOLD = 0.01
        TEMPERATURE = 0.1
        BATCH, SEQ = (4, 256)
        key = jax.random.key(seed)
        k1, k2, k3, k4, k5 = jax.random.split(key, 5)
        s = 1.0 / np.sqrt(IN_F)
        return {'input': jax.random.normal(k1, (BATCH, SEQ, IN_F), dtype=jnp.float32), 'weight': jax.random.normal(k2, (OUT_F, IN_F), dtype=jnp.float32) * s, 'bias': jax.random.uniform(k3, (OUT_F,), dtype=jnp.float32, minval=-s, maxval=s), 'centroids': jax.random.normal(k4, (N_CLUSTERS, IN_F), dtype=jnp.float32) * s, 'assignments': jax.random.randint(k5, (OUT_F,), 0, N_CLUSTERS, dtype=jnp.int32)}
    _L2_ffn_all = _L2_ffn_setup()
    _L2_ffn_in = {k: v for k, v in _L2_ffn_all.items() if k in ('weight', 'bias', 'centroids', 'assignments')}
    del _L2_ffn_all

    def _L3_xattn_setup():
        import jax, jax.numpy as jnp
        import numpy as np
        import math
        D_MODEL = 128
        NHEAD = 16
        MAX_SUP = 4
        DK = D_MODEL // NHEAD
        DM = D_MODEL * MAX_SUP
        B, S = (2, 128)
        key = jax.random.key(seed)
        ks = jax.random.split(key, 12)
        std = 0.02
        inp = {'q': jax.random.normal(ks[0], (B, S, DM), jnp.float32), 'k': jax.random.normal(ks[1], (B, S, DM), jnp.float32), 'v': jax.random.normal(ks[2], (B, S, DM), jnp.float32), 'Wq': jax.random.normal(ks[3], (DM, DM), jnp.float32) * std, 'bq': jnp.zeros((DM,), jnp.float32), 'Wk': jax.random.normal(ks[4], (DM, DM), jnp.float32) * std, 'bk': jnp.zeros((DM,), jnp.float32), 'Wv': jax.random.normal(ks[5], (DM, DM), jnp.float32) * std, 'bv': jnp.zeros((DM,), jnp.float32), 'interference': jax.random.normal(ks[6], (NHEAD, MAX_SUP, MAX_SUP), jnp.float32), 'amp': jnp.ones((1,), jnp.float32), 'Wo': jax.random.normal(ks[7], (DM, DM), jnp.float32) * std, 'bo': jnp.zeros((DM,), jnp.float32)}
        return inp
    _L3_xattn_all = _L3_xattn_setup()
    _L3_xattn_in = {k: v for k, v in _L3_xattn_all.items() if k in ('Wq', 'bq', 'Wk', 'bk', 'Wv', 'bv', 'interference', 'amp', 'Wo', 'bo')}
    del _L3_xattn_all

    def _L3_ffn_setup():
        import jax, jax.numpy as jnp
        import numpy as np
        DIM = 512
        INTER = 1792
        SPARSITY = 32
        RANK = 16
        key = jax.random.key(seed)
        ks = jax.random.split(key, 5)
        B, T = (32, 1)
        x = jax.random.normal(ks[0], (B, T, DIM), dtype=jnp.float32)
        c1_w = jax.random.normal(ks[1], (RANK, DIM), dtype=jnp.float32) * (1.0 / np.sqrt(DIM))
        c2_w = jax.random.normal(ks[2], (INTER, RANK), dtype=jnp.float32) * (1.0 / np.sqrt(RANK))
        w1 = jax.random.normal(ks[3], (INTER, DIM), dtype=jnp.float32) * (1.0 / np.sqrt(DIM))
        w2t = jax.random.normal(ks[4], (INTER, DIM), dtype=jnp.float32) * (1.0 / np.sqrt(INTER))
        return {'x': x, 'c1_w': c1_w, 'c2_w': c2_w, 'w1': w1, 'w2t': w2t}
    _L3_ffn_all = _L3_ffn_setup()
    _L3_ffn_in = {k: v for k, v in _L3_ffn_all.items() if k in ('c1_w', 'c2_w', 'w1', 'w2t')}
    del _L3_ffn_all
    return {'x': x, 'ctx_4096': ctx_4096, 'pos_BxS2': pos_BxS2, 'mask_BxSxS2_ik0': mask_BxSxS2_ik0, 'L0_xattn_Wq': _L0_xattn_in['Wq'], 'L0_xattn_bq': _L0_xattn_in['bq'], 'L0_xattn_Wk': _L0_xattn_in['Wk'], 'L0_xattn_bk': _L0_xattn_in['bk'], 'L0_xattn_Wv': _L0_xattn_in['Wv'], 'L0_xattn_bv': _L0_xattn_in['bv'], 'L0_xattn_Wo': _L0_xattn_in['Wo'], 'L0_xattn_bo': _L0_xattn_in['bo'], 'L0_ffn_gate_w': _L0_ffn_in['gate_w'], 'L0_ffn_expert_w': _L0_ffn_in['expert_w'], 'L1_ffn_gate_w': _L1_ffn_in['gate_w'], 'L1_ffn_up_w': _L1_ffn_in['up_w'], 'L1_ffn_down_w': _L1_ffn_in['down_w'], 'L1_ffn_fc1_w': _L1_ffn_in['fc1_w'], 'L1_ffn_fc2_w': _L1_ffn_in['fc2_w'], 'L1_ffn_expert_w': _L1_ffn_in['expert_w'], 'L1_ffn_ln_gamma': _L1_ffn_in['ln_gamma'], 'L1_ffn_ln_beta': _L1_ffn_in['ln_beta'], 'L2_xattn_Wq': _L2_xattn_in['Wq'], 'L2_xattn_Wk': _L2_xattn_in['Wk'], 'L2_xattn_Wv': _L2_xattn_in['Wv'], 'L2_xattn_Wo': _L2_xattn_in['Wo'], 'L2_ffn_weight': _L2_ffn_in['weight'], 'L2_ffn_bias': _L2_ffn_in['bias'], 'L2_ffn_centroids': _L2_ffn_in['centroids'], 'L2_ffn_assignments': _L2_ffn_in['assignments'], 'L3_xattn_Wq': _L3_xattn_in['Wq'], 'L3_xattn_bq': _L3_xattn_in['bq'], 'L3_xattn_Wk': _L3_xattn_in['Wk'], 'L3_xattn_bk': _L3_xattn_in['bk'], 'L3_xattn_Wv': _L3_xattn_in['Wv'], 'L3_xattn_bv': _L3_xattn_in['bv'], 'L3_xattn_interference': _L3_xattn_in['interference'], 'L3_xattn_amp': _L3_xattn_in['amp'], 'L3_xattn_Wo': _L3_xattn_in['Wo'], 'L3_xattn_bo': _L3_xattn_in['bo'], 'L3_ffn_c1_w': _L3_ffn_in['c1_w'], 'L3_ffn_c2_w': _L3_ffn_in['c2_w'], 'L3_ffn_w1': _L3_ffn_in['w1'], 'L3_ffn_w2t': _L3_ffn_in['w2t']}

def reference(x, ctx_4096, pos_BxS2, mask_BxSxS2_ik0, L0_xattn_Wq, L0_xattn_bq, L0_xattn_Wk, L0_xattn_bk, L0_xattn_Wv, L0_xattn_bv, L0_xattn_Wo, L0_xattn_bo, L0_ffn_gate_w, L0_ffn_expert_w, L1_ffn_gate_w, L1_ffn_up_w, L1_ffn_down_w, L1_ffn_fc1_w, L1_ffn_fc2_w, L1_ffn_expert_w, L1_ffn_ln_gamma, L1_ffn_ln_beta, L2_xattn_Wq, L2_xattn_Wk, L2_xattn_Wv, L2_xattn_Wo, L2_ffn_weight, L2_ffn_bias, L2_ffn_centroids, L2_ffn_assignments, L3_xattn_Wq, L3_xattn_bq, L3_xattn_Wk, L3_xattn_bk, L3_xattn_Wv, L3_xattn_bv, L3_xattn_interference, L3_xattn_amp, L3_xattn_Wo, L3_xattn_bo, L3_ffn_c1_w, L3_ffn_c2_w, L3_ffn_w1, L3_ffn_w2t):
    import jax
    import jax.numpy as jnp

    def _L0_xattn_ref(x, cond, Wq, bq, Wk, bk, Wv, bv, Wo, bo):
        import jax, jax.numpy as jnp
        import numpy as np
        HEADS = 8
        WINDOW = 16

        def _pointwise(W, b, t):
            return jnp.einsum('oc,bct->bot', W, t) + b[None, :, None]
        B, C, T = x.shape
        H, W = (HEADS, WINDOW)
        hd = C // H
        scale = hd ** (-0.5)
        pad_left = W // 2
        pad_right = W - pad_left - 1
        q = _pointwise(Wq, bq, x)
        k = _pointwise(Wk, bk, cond)
        v = _pointwise(Wv, bv, cond)
        k = jnp.pad(k, ((0, 0), (0, 0), (pad_left, pad_right)))
        v = jnp.pad(v, ((0, 0), (0, 0), (pad_left, pad_right)))
        idx = jnp.arange(T)[:, None] + jnp.arange(W)[None, :]
        k_win = k[:, :, idx].reshape(B, H, hd, T, W)
        v_win = v[:, :, idx].reshape(B, H, hd, T, W)
        qh = q.reshape(B, H, hd, T)
        dots = jnp.einsum('bhdt,bhdtw->bhtw', qh, k_win) * scale
        attn = jax.nn.softmax(dots, axis=-1)
        out = jnp.einsum('bhtw,bhdtw->bhdt', attn, v_win)
        out = out.reshape(B, C, T)
        return _pointwise(Wo, bo, out)

    def _L0_ffn_ref(x, gate_w, expert_w):
        import jax, jax.numpy as jnp
        import numpy as np
        TOP_K = 2
        E = expert_w.shape[0]
        gate_logits = jnp.einsum('bsh,he->bse', x, gate_w)
        top_vals, top_idx = jax.lax.top_k(gate_logits, TOP_K)
        probs = jax.nn.softmax(top_vals, axis=-1)
        onehot = jax.nn.one_hot(top_idx, E, dtype=x.dtype)
        w_e = jnp.einsum('bsk,bske->bse', probs, onehot)
        expert_out = jnp.einsum('bsh,eho->bseo', x, expert_w)
        out = jnp.einsum('bseo,bse->bso', expert_out, w_e)
        return out

    def _L1_xattn_ref(q, k, v):
        import jax, jax.numpy as jnp
        import numpy as np
        EMB_DIM = 64
        HEADS = 8
        B, C, N = q.shape
        H = HEADS
        dh = C // H
        qh = q.transpose(0, 2, 1).reshape(B, N, H, dh)
        kh = k.transpose(0, 2, 1).reshape(B, N, H, dh)
        vh = v.transpose(0, 2, 1).reshape(B, N, H, dh)
        qh = jax.nn.softmax(qh, axis=3)
        kh = jax.nn.softmax(kh, axis=1)
        kvs = jnp.einsum('bnhd,bnhe->bhde', kh, vh)
        out = jnp.einsum('bnhd,bhde->bnhe', qh, kvs)
        return out.transpose(0, 2, 3, 1).reshape(B, C, N)

    def _L1_ffn_ref(hidden_states, gate_w, up_w, down_w, fc1_w, fc2_w, expert_w, ln_gamma, ln_beta):
        import jax, jax.numpy as jnp
        import numpy as np
        HID, INT, LAT, NE, K = (512, 1024, 256, 8, 2)
        LN_EPS = 1e-05

        def _layernorm(x, gamma, beta):
            mu = jnp.mean(x, axis=-1, keepdims=True)
            var = jnp.var(x, axis=-1, keepdims=True)
            return (x - mu) * jax.lax.rsqrt(var + LN_EPS) * gamma + beta
        logits = jnp.einsum('bsh,he->bse', hidden_states, gate_w)
        routing_weights, selected_experts = jax.lax.top_k(logits, K)
        h = jax.nn.relu(jnp.einsum('bsh,hi->bsi', hidden_states, up_w)) ** 2
        shared_out = jnp.einsum('bsi,ih->bsh', h, down_w)
        x_latent = jnp.einsum('bsh,hl->bsl', hidden_states, fc1_w)
        expert_out = jnp.einsum('bsl,lm->bsm', x_latent, expert_w)
        moe_out = expert_out * jnp.sum(routing_weights, axis=-1, keepdims=True)
        routed_out = jnp.einsum('bsl,lh->bsh', moe_out, fc2_w)
        return _layernorm(shared_out + routed_out, ln_gamma, ln_beta)

    def _L2_xattn_ref(query, key, value, position_ids, src_mask, Wq, Wk, Wv, Wo):
        import jax, jax.numpy as jnp
        import numpy as np
        B, S, E = (2, 256, 512)
        H, KVH, D = (32, 8, 128)
        GROUPS = H // KVH
        MAX_POS = 512
        ROPE_THETA = 10000.0

        def _rope_tables(max_pos, dim, theta):
            inv_freq = 1.0 / theta ** (jnp.arange(0, dim, 2, dtype=jnp.float32) / dim)
            t = jnp.arange(max_pos, dtype=jnp.float32)
            freqs = jnp.einsum('i,j->ij', t, inv_freq)
            emb = jnp.concatenate([freqs, freqs], axis=-1)
            return (jnp.cos(emb), jnp.sin(emb))

        def _rotate_half(x):
            x1, x2 = (x[..., :x.shape[-1] // 2], x[..., x.shape[-1] // 2:])
            return jnp.concatenate([-x2, x1], axis=-1)
        nb, q_len, _ = query.shape
        q = (query @ Wq).reshape(nb, q_len, H, D).transpose(0, 2, 1, 3)
        k = (key @ Wk).reshape(nb, q_len, KVH, D).transpose(0, 2, 1, 3)
        v = (value @ Wv).reshape(nb, q_len, KVH, D).transpose(0, 2, 1, 3)
        cos_t, sin_t = _rope_tables(MAX_POS, D, ROPE_THETA)
        cos = cos_t[position_ids][:, None]
        sin = sin_t[position_ids][:, None]
        q = q * cos + _rotate_half(q) * sin
        k = k * cos + _rotate_half(k) * sin
        k = jnp.repeat(k, GROUPS, axis=1)
        v = jnp.repeat(v, GROUPS, axis=1)
        scores = jnp.einsum('bhqd,bhkd->bhqk', q, k) / jnp.sqrt(jnp.float32(D))
        mask = src_mask[:, None]
        scores = jnp.where(mask == 0, jnp.float32(-1000000000.0), scores)
        attn = jax.nn.softmax(scores, axis=-1)
        x = jnp.einsum('bhqk,bhkd->bhqd', attn, v)
        x = x.transpose(0, 2, 1, 3).reshape(nb, q_len, H * D)
        return x @ Wo

    def _L2_ffn_ref(input, weight, bias, centroids, assignments):
        import jax, jax.numpy as jnp
        import numpy as np
        IN_F = 512
        OUT_F = 512
        N_CLUSTERS = 64
        THRESHOLD = 0.01
        TEMPERATURE = 0.1
        BATCH, SEQ = (4, 256)
        shape = input.shape
        x = input.reshape(-1, shape[-1])
        dots = jax.nn.softmax(x @ centroids.T / TEMPERATURE, axis=-1)
        hits = dots > THRESHOLD
        query_sel = jnp.any(hits, axis=1)
        cluster_sel = jnp.any(hits, axis=0)
        row_sel = cluster_sel[assignments]
        dense = x @ weight.T + bias
        out = jnp.where(query_sel[:, None] & row_sel[None, :], dense, jnp.zeros((), dense.dtype))
        return out.reshape(*shape[:-1], -1)

    def _L3_xattn_ref(q, k, v, Wq, bq, Wk, bk, Wv, bv, interference, amp, Wo, bo):
        import jax, jax.numpy as jnp
        import numpy as np
        import math
        D_MODEL = 128
        NHEAD = 16
        MAX_SUP = 4
        DK = D_MODEL // NHEAD
        DM = D_MODEL * MAX_SUP
        B, S = (2, 128)
        b, s, dm = q.shape
        H, M = (interference.shape[0], interference.shape[1])
        dk = dm // (H * M)

        def proj(x, W, bias):
            y = x @ W.T + bias
            y = y.reshape(b, s, H, dk, M)
            return jnp.transpose(y, (0, 2, 1, 3, 4))
        qh = proj(q, Wq, bq)
        kh = proj(k, Wk, bk)
        vh = proj(v, Wv, bv)

        def interfere(x):
            return x + 0.1 * amp[0] * jnp.einsum('bhsdi,hij->bhsdj', x, interference)
        qh, kh, vh = (interfere(qh), interfere(kh), interfere(vh))
        scores = jnp.einsum('bhqdm,bhkdm->bhqkm', qh, kh) / math.sqrt(dk)
        weights = jax.nn.softmax(scores, axis=3)
        out = jnp.einsum('bhqkm,bhkdm->bhqdm', weights, vh)
        out = jnp.transpose(out, (0, 2, 1, 3, 4)).reshape(b, s, dm)
        return out @ Wo.T + bo

    def _L3_ffn_ref(x, c1_w, c2_w, w1, w2t):
        import jax, jax.numpy as jnp
        import numpy as np
        DIM = 512
        INTER = 1792
        SPARSITY = 32
        RANK = 16
        B, T, M = x.shape
        xf = x.reshape(B * T, M)
        inter = xf @ c1_w.T @ c2_w.T
        n_blocks = INTER // SPARSITY
        blk = inter.reshape(B * T, n_blocks, SPARSITY)
        idx = jnp.argmax(blk, axis=-1) + jnp.arange(0, INTER, SPARSITY)
        w1_g = w1[idx]
        w2_g = w2t[idx]
        h = jax.nn.relu(jnp.einsum('bkm,bm->bk', w1_g, xf))
        out = jnp.einsum('bk,bkm->bm', h, w2_g)
        return out.reshape(B, T, M)
    x = x + _L0_xattn_ref(_layernorm(x, axis=-1), ctx_4096, L0_xattn_Wq, L0_xattn_bq, L0_xattn_Wk, L0_xattn_bk, L0_xattn_Wv, L0_xattn_bv, L0_xattn_Wo, L0_xattn_bo)
    x = x + _L0_ffn_ref(_layernorm(x, axis=-1), L0_ffn_gate_w, L0_ffn_expert_w)
    x = x + _L1_xattn_ref(_layernorm(x, axis=-1), ctx_4096, ctx_4096)
    x = x + _L1_ffn_ref(_layernorm(x, axis=-1), L1_ffn_gate_w, L1_ffn_up_w, L1_ffn_down_w, L1_ffn_fc1_w, L1_ffn_fc2_w, L1_ffn_expert_w, L1_ffn_ln_gamma, L1_ffn_ln_beta)
    x = x + _L2_xattn_ref(_layernorm(x, axis=-1), ctx_4096, ctx_4096, pos_BxS2, mask_BxSxS2_ik0, L2_xattn_Wq, L2_xattn_Wk, L2_xattn_Wv, L2_xattn_Wo)
    x = x + _L2_ffn_ref(_layernorm(x, axis=-1), L2_ffn_weight, L2_ffn_bias, L2_ffn_centroids, L2_ffn_assignments)
    x = x + _L3_xattn_ref(_layernorm(x, axis=-1), ctx_4096, ctx_4096, L3_xattn_Wq, L3_xattn_bq, L3_xattn_Wk, L3_xattn_bk, L3_xattn_Wv, L3_xattn_bv, L3_xattn_interference, L3_xattn_amp, L3_xattn_Wo, L3_xattn_bo)
    x = x + _L3_ffn_ref(_layernorm(x, axis=-1), L3_ffn_c1_w, L3_ffn_c2_w, L3_ffn_w1, L3_ffn_w2t)
    return x

_drawn_inputs = setup_inputs


def setup_inputs(seed=0):
    import zlib

    import numpy as np

    out = dict(_drawn_inputs(seed))
    spreads = {'L0_xattn_bq': (0.0, 0.8),
     'L0_xattn_bk': (0.0, 0.8),
     'L0_xattn_bv': (0.0, 0.8),
     'L0_xattn_bo': (0.0, 0.1),
     'L1_ffn_ln_gamma': (1.0, 0.2),
     'L1_ffn_ln_beta': (0.0, 0.1),
     'L3_xattn_bq': (0.0, 0.8),
     'L3_xattn_bk': (0.0, 0.8),
     'L3_xattn_bv': (0.0, 0.409),
     'L3_xattn_bo': (0.0, 0.1)}
    factors = {'L0_xattn_Wq': 8.0,
     'L0_xattn_Wk': 8.0,
     'L0_xattn_Wv': 2.869,
     'L0_xattn_Wo': 2.788,
     'L2_ffn_bias': 4.917,
     'L3_xattn_Wq': 8.0,
     'L3_xattn_Wk': 8.0,
     'L3_xattn_interference': 5.261}
    for name, (base, spread) in spreads.items():
        noise = np.random.default_rng([zlib.crc32(name.encode()), seed]).standard_normal(out[name].shape)
        drawn = base * np.exp(spread * noise) if base else spread * noise
        out[name] = jnp.asarray(drawn.astype(out[name].dtype))
    for name, factor in factors.items():
        out[name] = (out[name] * factor).astype(out[name].dtype)
    return out
```

```python
from contextlib import ExitStack

import numpy as np

import concourse.bass as bass
from concourse import mybir

F32 = mybir.dt.float32
I32 = mybir.dt.int32
U32 = mybir.dt.uint32
ALU = mybir.AluOpType
ACT = mybir.ActivationFunctionType
AX = mybir.AxisListType.X

P = 128
B, S, D = 16, 64, 512
NT = B * S // P
DC = D // P
N = B * S
HALF = N // 2
EPS = 1e-5
NEG = -1e9

H0, WIN = 8, 16
HD0 = S // H0
PADL = WIN // 2
KW = D + WIN - 1
E0 = 8
INT1, LAT1 = 1024, 256
G2, QH2, D2 = 8, 4, 128
WG = DC * QH2 * D2 + 2 * DC * D2 + QH2 * D
MAXPOS = 512
NCL = 64
M3 = 4
INTER, BLK, RANK = 1792, 32, 16
NI = INTER // P


class Step:

    def __init__(self, line, n, turn=None, per=0):
        self.line, self.n, self.turn, self.per = line, n, turn, per

    def value(self):
        return self.n if self.turn is None or not self.per else self.turn * self.per + self.n

    def before(self):
        assert self.n - self.per >= 0
        return Step(self.line, self.n - self.per, self.turn, self.per)


class Line:

    def __init__(self, engine, sem, step=1):
        self.e, self.sem, self.step = engine, sem, step
        self.n, self.turn, self.per, self.known = 0, None, 0, {}

    def go(self, ins):
        ins.then_inc(self.sem, self.step)
        self.n += self.step
        return self.at(self.n)

    def at(self, n):
        return Step(self, n, self.turn, self.per)

    def last(self):
        return self.at(self.n)

    def need(self, *steps):
        for s in steps:
            if s is None or s.n == 0:
                continue
            key = (id(s.line), s.turn is not None and s.per > 0)
            if self.known.get(key, -1) >= s.n:
                continue
            self.known[key] = s.n
            self.e.wait_ge(s.line.sem, s.value())


def chunked(w):
    k, n = w.shape
    return np.ascontiguousarray(w.reshape(k // P, P, n).transpose(1, 0, 2).reshape(P, -1))


def constants():
    k = np.arange(P)
    parts = {
        "ident": np.eye(P),
        "selw": (np.arange(2 * P - 16)[None, :] == (P - 16 + k // S * H0 + k % S // HD0)[:, None]),
        "selt": np.concatenate([(k[:, None] == 16 * p + (k // S * H0 + k % S // HD0)[None, :])
                                for p in range(NT)], 1),
        "block8": np.kron(np.eye(P // 8), np.ones((8, 8))),
        "block4": np.kron(np.eye(P // 4), np.ones((4, 4))),
        "iota8": np.tile(np.arange(8), (P, 1)),
        "posid": k[:, None] + P * np.arange(MAXPOS // P)[None, :],
        "down32": np.tile(BLK - np.arange(BLK), (P, 1)),
        "is_m": k[:, None] % M3 == np.arange(M3)[None, :],
        "is_odd": k[:, None] % 2 == np.arange(2)[None, :],
        "m_half": np.arange(M3)[None, :] // 2 == (k // S)[:, None],
    }
    at, cols = {}, 0
    for name, a in parts.items():
        at[name] = (cols, cols + a.shape[1])
        cols += a.shape[1]
    return np.concatenate([a.astype(np.float32) for a in parts.values()], 1), at


def rope_tables():
    inv = (1.0 / 10000.0 ** (np.arange(0, D2, 2, dtype=np.float32) / np.float32(D2))).astype(np.float32)
    f = np.arange(MAXPOS, dtype=np.float32)[:, None] * inv[None, :]
    cos = np.concatenate([np.cos(f), np.cos(f)], 1)
    sin = np.concatenate([-np.sin(f), np.sin(f)], 1)
    return chunked(np.concatenate([cos, sin], 1).astype(np.float32))


def lay_out(i):
    f = {n: np.asarray(a) for n, a in i.items()}
    x, c = f["x"].reshape(N, D), f["ctx_4096"].reshape(N, D)

    def twice(w):
        z = np.zeros((P, P), w.dtype)
        z[:S, :S] = w.T
        z[S:, S:] = w.T
        return z

    def rows(v):
        return np.broadcast_to(v[None, :], (P, v.shape[0]))

    a = {"x": chunked(x), "c": chunked(c), "ct": chunked(c.T), "const": constants()[0]}
    a["w0"] = np.concatenate([twice(f[f"L0_xattn_{n}"]) for n in ("Wq", "Wk", "Wv", "Wo")]
                             + [np.tile(f[f"L0_xattn_{n}"], 2)[:, None] for n in ("bq", "bk", "bv", "bo")], 1)
    a["gate0"] = chunked(f["L0_ffn_gate_w"])
    a["expert0"] = np.concatenate([chunked(w) for w in f["L0_ffn_expert_w"]], 1)
    a["ffn1"] = np.concatenate([chunked(f[f"L1_ffn_{n}"]) for n in ("up_w", "fc1_w", "expert_w", "fc2_w", "down_w",
                                                                    "gate_w")], 1)
    a["ln1"] = np.concatenate([rows(f["L1_ffn_ln_gamma"]), rows(f["L1_ffn_ln_beta"])], 1)
    q, k, v, o = (f[f"L2_xattn_W{n}"] for n in "qkvo")
    w = QH2 * D2
    a["attn2"] = np.stack([np.concatenate([chunked(q[:, g * w:(g + 1) * w]), chunked(k[:, g * D2:(g + 1) * D2]),
                                           chunked(v[:, g * D2:(g + 1) * D2]), chunked(o[g * w:(g + 1) * w])], 1)
                           for g in range(G2)])
    a["pos"] = rows(f["pos_BxS2"].reshape(-1))
    m = f["mask_BxSxS2_ik0"].transpose(1, 0, 2).reshape(S, -1)
    a["mask"] = np.concatenate([m, m], 0)
    a["rope"] = rope_tables()
    a["ffn2"] = np.concatenate([chunked(f["L2_ffn_weight"].T), chunked(f["L2_ffn_centroids"].T),
                                rows(f["L2_ffn_bias"])], 1)
    a["assign"] = rows(f["L2_ffn_assignments"])
    a["attn3"] = np.concatenate([chunked(f[f"L3_xattn_W{n}"]) for n in "qkv"], 1)
    a["wo3"] = chunked(f["L3_xattn_Wo"].T)
    inter = f["L3_xattn_interference"].reshape(DC, 4, 1, M3, M3)
    inter = np.broadcast_to(inter, (DC, 4, P // 16, M3, M3)).reshape(DC, P, M3).transpose(1, 0, 2).reshape(P, -1)
    a["small3"] = np.concatenate([f[f"L3_xattn_b{n}"].reshape(DC, P).T for n in "qkv"]
                                 + [inter, rows(f["L3_xattn_amp"]), rows(f["L3_xattn_bo"])], 1)
    a["c1"] = chunked(f["L3_ffn_c1_w"].T)
    a["c2"] = f["L3_ffn_c2_w"].T
    a["w1"] = chunked(f["L3_ffn_w1"].T)
    a["w2"] = chunked(f["L3_ffn_w2t"])
    return {n: np.ascontiguousarray(v) for n, v in a.items()}


PER2 = (168, 38, 14, 36)
X, XT, CT, C, CONST = 0, 4096, 8192, 12288, 16384
CONST_AT = constants()[1]
NCONST = max(b for _, b in CONST_AT.values())
SMALL = CONST + NCONST
R = SMALL + 1024
WORDS = R + 30720


def program(nc, dram, out):
    with ExitStack() as ctx:
        A = ctx.enter_context(nc.sbuf_tensor("arena", [P, WORDS], F32))
        bank = ctx.enter_context(nc.psum_tensor("banks", [P, 8, 512], F32))

        def sem(name):
            return ctx.enter_context(nc.semaphore(name))

        PE, V, G, AC = (Line(e, sem(n)) for e, n in ((nc.tensor, "pe_steps"), (nc.vector, "vector_steps"),
                                                      (nc.gpsimd, "pool_steps"), (nc.scalar, "act_steps")))
        SP = Line(nc.sync, sem("sp_steps"))
        engines = (PE, V, G, AC)
        pe, v, g, act = nc.tensor, nc.vector, nc.gpsimd, nc.scalar

        def a(at, n, *shape):
            t = A[:, bass.ds(at, n)]
            if len(shape) == 2:
                return t.rearrange("p (a b) -> p a b", a=shape[0], b=shape[1])
            if len(shape) == 3:
                return t.rearrange("p (a b c) -> p a b c", a=shape[0], b=shape[1], c=shape[2])
            return t

        def const(name):
            lo, hi = CONST_AT[name]
            return A[:, CONST + lo:CONST + hi]

        def load(name, to, src, *after, line=None, part=P):
            line = line or Line(nc.sync, sem(name), 16)
            SP.need(*after)
            return line.go(nc.sync.dma_start(A[0:part, bass.ds(to, src.shape[-1])], src))

        class Turns:

            def __init__(self, turns, per):
                self.turns, self.per = turns, per

            def __enter__(self):
                self.ctx = nc.Fori(0, self.turns)
                self.i = self.ctx.__enter__()
                self.base = {ln: ln.n for ln in self.per}
                for ln in self.per:
                    ln.turn, ln.per = self.i, self.per[ln]
                for ln in engines + (SP,):
                    ln.known = {key: n for key, n in ln.known.items() if not key[1]}
                return self.i

            def __exit__(self, *exc):
                if exc[0]:
                    return False
                moved = [ln.n - self.base[ln] for ln in self.per]
                assert all(ln.n - self.base[ln] == self.per[ln] for ln in self.per), moved
                self.ctx.__exit__(None, None, None)
                for ln in self.per:
                    ln.n = self.base[ln] + self.turns * self.per[ln]
                    ln.turn, ln.per = None, 0
                for ln in engines + (SP,):
                    ln.known = {}
                return False

        def boundary():
            for ln in engines + (SP,):
                ln.need(*(o.last() for o in engines if o is not ln))

        def mm(dst, lhsT, rhs, k=0, n=1, **kw):
            return pe.matmul(dst, lhsT=lhsT, rhs=rhs, start=(k == 0), stop=(k == n - 1), **kw)

        STAT = SMALL
        HALVES = SMALL + 80
        g_half = G.go(g.memset(a(HALVES, 1), -0.5))

        def normalise(src, dst, t, *after):
            st = STAT + 10 * t
            V.need(*after)
            s = V.go(v.bn_stats(a(st, 6), src))
            V.need(s)
            s = V.go(v.bn_aggr(a(st + 6, 2), a(st, 6)))
            V.need(s)
            s = V.go(v.tensor_scalar(a(st + 7, 1), a(st + 7, 1), EPS, None, ALU.add))
            G.need(s, g_half)
            s = G.go(g.tensor_tensor(a(st + 8, 1), a(st + 7, 1), a(HALVES, 1), ALU.pow))
            V.need(s)
            return V.go(v.tensor_scalar(dst, src, a(st + 6, 1), a(st + 8, 1), ALU.subtract, ALU.mult))

        def transposed(src, dst, t, b, free, *after):
            PE.need(free, *after)
            for c in range(DC):
                s = PE.go(pe.transpose(bank[:, b, c * P:(c + 1) * P], src[:, c * P:(c + 1) * P], const("ident")))
            AC.need(s)
            return AC.go(act.activation(a(dst, DC * N, DC, N)[:, :, t * P:(t + 1) * P],
                                        bank[:, b, :].rearrange("p (c n) -> p c n", c=DC), ACT.Copy))

        def norm_all(xn, ready=(), with_t=True):
            free = [None, None]
            ns = []
            for t in range(NT):
                s = normalise(a(X + t * D, D), a(xn + t * D, D), t, *ready)
                ns.append(s)
                if with_t:
                    free[t % 2] = transposed(a(xn + t * D, D), XT, t, t % 2, free[t % 2], s)
            return ns, free[1]

        x_in = load("x_in", X, dram["x"])
        const_in = load("const_in", CONST, dram["const"])
        c_in = load("c_in", C, dram["c"])

        Q0, K0, V0 = R, R + 4096, R + 4096 + NT * KW
        DOTS = V0 + NT * KW
        PROD = DOTS + WIN * D
        assert PROD + 8 * D <= R + 30720
        W0 = SMALL + 96
        XN0 = XT
        w0_in = load("w0_in", W0, dram["w0"])
        ct_in = load("ct_in", CT, dram["ct"])
        scale0 = HD0 ** -0.5

        pads = []
        for at in (K0, V0):
            kv = a(at, NT * KW, NT, KW)
            pads.append(G.go(g.memset(kv[:, :, 0:PADL], 0.0)))
            pads.append(G.go(g.memset(kv[:, :, PADL + D:KW], 0.0)))
        norms, _ = norm_all(XN0, (x_in,), with_t=False)
        PE.need(w0_in, c_in, const_in)
        AC.need(w0_in)
        bias0 = a(W0 + 4 * P, 4)
        free = [None] * 8
        n = 0
        for t in range(NT):
            for j, (src, dst) in enumerate(((XN0, Q0 + t * D), (C, K0 + t * KW + PADL), (C, V0 + t * KW + PADL))):
                PE.need(free[n % 8], norms[t] if j == 0 else None)
                s = PE.go(mm(bank[:, n % 8, :], a(W0 + j * P, P), a(src + t * D, D)))
                AC.need(s)
                free[n % 8] = AC.go(act.activation(a(dst, D), bank[:, n % 8, :], ACT.Identity,
                                                   bias=bias0[:, j:j + 1]))
                n += 1
        qkv = AC.last()
        lo = CONST_AT["selw"][0] + CONST
        PE.need(qkv)
        with Turns(WIN // 2, {PE: 16, V: 10, G: 6, AC: 2}) as i:
            done = []
            for u in range(2):
                prods = []
                for t in range(NT):
                    ln = G if t % 3 == 2 and t < 8 and (t != 8) else V
                    ln = G if t in (1, 4, 6) else V
                    ln.need(qkv, pads[-1], done[t] if u else PE.at(PE.n + NT + t + 1).before())
                    prods.append(ln.go(ln.e.tensor_tensor(
                        a(PROD + t * D, D), a(Q0 + t * D, D),
                        A[:, bass.ds(K0 + t * KW + i * 2 + u, D)], ALU.mult)))
                if not u:
                    PE.need(AC.at(AC.n + 1).before())
                else:
                    PE.need(AC.at(AC.n + 1).before())
                new = []
                for t in range(NT):
                    PE.need(prods[t])
                    new.append(PE.go(mm(bank[:, u, :], A[:, lo + P - 16 - 16 * t:lo + 2 * P - 16 - 16 * t],
                                        a(PROD + t * D, D), t, NT)))
                done = new
                AC.need(new[-1])
                AC.go(act.activation(A[:, bass.ds(DOTS + i * 2 * D + u * D, D)], bank[:, u, :], ACT.Copy))
        TOP, SUM = PROD, PROD + D
        dots = a(DOTS, WIN * D, WIN, D)
        V.need(AC.last(), PE.last())
        G.need(AC.last())
        atts = []
        for c in range(4):
            cut = slice(c * P, (c + 1) * P)
            part = dots[:, :, cut]
            by_t = part.rearrange("p w t -> p t w")

            def over_w(at):
                return a(at, D)[:, cut].unsqueeze(1).broadcast_to([P, WIN, P])

            s = V.go(v.tensor_reduce(a(TOP, D)[:, cut], by_t, axis=AX, op=ALU.max))
            G.need(s)
            s = G.go(g.tensor_tensor(part, part, over_w(TOP), ALU.subtract))
            AC.need(s)
            s = AC.go(act.activation(part, part, ACT.Exp, scale=scale0))
            V.need(s)
            s = V.go(v.tensor_reduce(a(SUM, D)[:, cut], by_t, axis=AX, op=ALU.add))
            V.need(s)
            s = V.go(v.reciprocal(a(SUM, D)[:, cut], a(SUM, D)[:, cut]))
            V.need(s)
            atts.append(V.go(v.tensor_tensor(part, part, over_w(SUM), ALU.mult)))
        SELT = XT
        AV, AVN = Q0, 8
        PE.need(atts[-1])
        AC.need(atts[-1])
        V.need(atts[-1])
        s_bo = None
        with Turns(NT, {PE: WIN + 4, V: WIN + 1, G: 12, AC: 1}) as i:
            AC.need(PE.at(PE.n + WIN + 4).before())
            sel = AC.go(act.activation(a(SELT, P), A[:, bass.ds(CONST + CONST_AT["selt"][0] + i * P, P)], ACT.Copy))
            spread, avs, out_mm = [], [], None
            quads = []
            PE0, V0n, G0 = PE.n, V.n, G.n

            def to_out(k):
                PE.need(quads[k])
                if k == 0:
                    PE.need(V.at(V0n + WIN + 1).before())
                return PE.go(mm(bank[:, 4, :], a(W0 + 3 * P, P), a(AV + (4 * k % AVN) * D, D), k, 4))

            outs = []
            for w in range(WIN):
                PE.need(sel)
                PE.need(avs[w - 4] if w >= 4 else V.at(V0n + WIN - 3 + w).before())
                s = PE.go(mm(bank[:, w % 4, :], a(SELT, P), A[:, DOTS + w * D:DOTS + (w + 1) * D]))
                V.need(s)
                if w >= AVN:
                    V.need(quads[w // 4 - 2], outs[w // 4 - 2] if w % 4 == 0 else None)
                else:
                    V.need(G.at(G0 + 3 * (w // 4 + 2) + 3).before(),
                           PE.at(PE0 + WIN + w // 4 + 3).before() if w % 4 == 0 else None)
                avs.append(V.go(v.tensor_tensor(a(AV + w % AVN * D, D), bank[:, w % 4, :],
                                                A[:, bass.ds(V0 + i * KW + w, D)], ALU.mult)))
                if w % 4 == 3:
                    b0 = AV + (w - 3) % AVN * D
                    G.need(avs[w])
                    s1 = G.go(g.tensor_tensor(a(b0, D), a(b0, D), a(b0 + D, D), ALU.add))
                    s2 = G.go(g.tensor_tensor(a(b0 + 2 * D, D), a(b0 + 2 * D, D), a(b0 + 3 * D, D), ALU.add))
                    G.need(s2)
                    quads.append(G.go(g.tensor_tensor(a(b0, D), a(b0, D), a(b0 + 2 * D, D), ALU.add)))
                if w % 4 == 3 and w > 4:
                    outs.append(to_out(w // 4 - 1))
            outs.append(to_out(3))
            V.need(outs[-1])
            V.go(v.scalar_tensor_tensor(A[:, bass.ds(X + i * D, D)], bank[:, 4, :], bias0[:, 3:4],
                                        A[:, bass.ds(X + i * D, D)], ALU.add, ALU.add))
        boundary()

        XN = R
        EXP = R + 28672
        WREP, WCOL = R + 4096, R + 4096 + 64
        GATE = R + 4096 + 128
        LOG = GATE + 32
        TOP8, IDX = LOG + 64, LOG + 128
        TMP = LOG + 192
        gate_in = load("gate_in", GATE, dram["gate0"])
        exp_line = Line(nc.sync, sem("expert_in"), 16)
        for e in range(E0):
            exp_in = load("", EXP - e * 2048, dram["expert0"][:, e * 2048:(e + 1) * 2048], exp_line.last(),
                          line=exp_line)
        norms, xt_done = norm_all(XN)
        PE.need(xt_done, gate_in)
        last_banks = (AC.last(),)

        def logits(gate_at, b):
            for t in range(NT):
                for c in range(DC):
                    s = PE.go(mm(bank[:, b, t * 8:(t + 1) * 8], a(XT + c * N + t * P, P), a(gate_at + c * 8, 8), c, DC))
            return s

        s = logits(GATE, 7)
        V.need(s)
        V.need(V.go(v.tensor_copy(a(LOG, 64), bank[:, 7, 0:64])))
        for t in range(NT):
            V.go(v.max(a(TOP8 + 8 * t, 8), a(LOG + 8 * t, 8)))
        V.need(V.last())
        for t in range(NT):
            V.go(v.max_index(a(IDX + 8 * t, 8).bitcast(U32), a(TOP8 + 8 * t, 8), a(LOG + 8 * t, 8)))
        top = a(TOP8, 64, NT, 8)
        s = V.go(v.tensor_tensor(a(TMP, NT), top[:, :, 1], top[:, :, 0], ALU.subtract))
        AC.need(s)
        s = AC.go(act.activation(a(TMP, NT), a(TMP, NT), ACT.Exp))
        V.need(s)
        V.need(V.go(v.tensor_scalar(a(TMP + 8, NT), a(TMP, NT), 1.0, None, ALU.add)))
        V.need(V.go(v.reciprocal(a(TMP + 8, NT), a(TMP + 8, NT))))
        V.need(V.go(v.tensor_tensor(a(TMP, NT), a(TMP, NT), a(TMP + 8, NT), ALU.mult)))
        V.need(V.go(v.tensor_copy(a(TMP + 16, 64), a(IDX, 64).bitcast(U32))))
        idx = a(TMP + 16, 64, NT, 8)
        pick = [a(TMP + 80 + 64 * j, 64, E0, NT) for j in range(2)]
        for j, weight in ((0, TMP + 8), (1, TMP)):
            V.need(V.go(v.tensor_tensor(pick[j], const("iota8").unsqueeze(2).broadcast_to([P, E0, NT]),
                                        idx[:, :, j].unsqueeze(1).broadcast_to([P, E0, NT]), ALU.is_equal)))
            V.need(V.go(v.tensor_tensor(pick[j], pick[j], a(weight, NT).unsqueeze(1).broadcast_to([P, E0, NT]),
                                        ALU.mult)))
        V.need(V.go(v.tensor_tensor(a(WREP, 64, E0, NT), pick[0], pick[1], ALU.add)))
        V.go(v.memset(a(TMP, 1), 0.0))
        PE.need(V.last())
        with Turns(E0, {PE: NT * DC, V: NT + 1}) as e:
            V.need(V.last())
            col = V.go(v.tensor_copy(a(WCOL, NT), A[:, bass.ds(WREP + e * NT, NT)]))
            PE.need(Step(exp_line, 16, e, 16))
            for t in range(NT):
                PE.need(V.at(V.n + 1).before() if t == 0 else V.at(V.n + 1).before())
                for c in range(DC):
                    s = PE.go(mm(bank[:, t, :], a(XT + c * N + t * P, P),
                                 A[:, bass.ds(EXP - e * 2048 + c * D, D)], c, DC))
                V.need(s, col)
                V.go(v.scalar_tensor_tensor(a(X + t * D, D), bank[:, t, :], a(WCOL + t, 1), a(X + t * D, D),
                                            ALU.mult, ALU.add))
        boundary()

        F1 = R + 14336
        f1_in = load("ffn1_in", F1, dram["ffn1"])
        KE, KET, KV = R + 4096, F1 - 0 + 10784, R + 8192
        NMAX, KSUM = R + 13312, R + 13320
        assert KET + 4096 <= R + 30720
        ke = []
        for t in range(NT):
            V.need(None)
            s = V.go(v.tensor_reduce(a(NMAX + t, 1), a(C + t * D, D), axis=AX, op=ALU.max, negate=True))
            AC.need(s)
            ke.append(AC.go(act.activation(a(KE + t * D, D), a(C + t * D, D), ACT.Exp, bias=a(NMAX + t, 1),
                                           accum_out=a(KSUM + t, 1))))
        V.need(ke[-1])
        ksum = V.go(v.reciprocal(a(KSUM, NT), a(KSUM, NT)))
        norms, _ = norm_all(XN, with_t=False)
        free = [None] * 8
        for t in range(NT):
            free[t % 2] = transposed(a(KE + t * D, D), KET, t, t % 2, free[t % 2], ke[t])
        for t in range(NT):
            PE.need(free[0], free[1], free[2 + t % 2])
            for c in range(DC):
                s = PE.go(mm(bank[:, 2 + t % 2, 0:P], a(KET + c * N + t * P, P), a(CT + c * N + t * P, P), c, DC))
            V.need(s, ksum)
            free[2 + t % 2] = V.go(v.scalar_tensor_tensor(a(KV + t * P, P), bank[:, 2 + t % 2, 0:P], a(KSUM + t, 1),
                                                          const("block8"), ALU.mult, ALU.mult))
        for t in range(NT):
            AC.need(norms[t])
            xq = a(XN + t * D, D)
            s = AC.go(act.activation(xq, xq, ACT.Exp))
            b = 4 + t % 2
            PE.need(s, free[b])
            s = PE.go(mm(bank[:, b, :], const("block8"), xq))
            V.need(s)
            s = V.go(v.reciprocal(a(KE + t * D, D), bank[:, b, :]))
            free[b] = s
            G.need(s)
            s = G.go(g.tensor_tensor(xq, xq, a(KE + t * D, D), ALU.mult))
            PE.need(s, free[2], free[3], free[6 + t % 2])
            s = PE.go(mm(bank[:, 6 + t % 2, :], a(KV + t * P, P), xq))
            V.need(s)
            free[6 + t % 2] = V.go(v.tensor_tensor(a(X + t * D, D), bank[:, 6 + t % 2, :], a(X + t * D, D), ALU.add))
        boundary()

        UP = F1
        FC1 = UP + DC * INT1
        EX1 = FC1 + DC * LAT1
        FC2 = EX1 + LAT1 // P * LAT1
        DOWN = FC2 + LAT1 // P * D
        GATE1 = DOWN + INT1 // P * D
        XN1 = C
        HT = R + 5120
        LT, LE, LN1 = R + 25120, R + 27168, R + 29216
        G_OFF = LN1 + 1024
        slot = [R, R + 14336]
        a2_line = [Line(nc.sync, sem(f"group_in{j}"), 16) for j in range(2)]
        ln1_in = load("ln1_in", LN1, dram["ln1"])
        load("", slot[0], dram["attn2"][0], line=a2_line[0])
        norms, xt_done = norm_all(XN1)
        PE.need(xt_done, f1_in)
        s = logits(GATE1, 7)
        V.need(s)
        V.need(V.go(v.tensor_copy(a(G_OFF, 64), bank[:, 7, 0:64])))
        for t in range(NT):
            V.go(v.max(a(G_OFF + 64 + 8 * t, 8), a(G_OFF + 8 * t, 8)))
        V.need(V.last())
        top = a(G_OFF + 64, 64, NT, 8)
        RW = G_OFF + 128
        rw = V.go(v.tensor_tensor(a(RW, NT), top[:, :, 0], top[:, :, 1], ALU.add))
        G.need(ln1_in, norms[-1])
        for t in range(NT):
            G.go(g.tensor_tensor(a(X + t * D, D), a(X + t * D, D), a(LN1 + D, D), ALU.add))
        free = [None] * 8
        n = 0

        def product(dst, w_at, cols, j, src, k, h, evac):
            nonlocal n
            b = n % 7
            n += 1
            PE.need(free[b])
            for c in range(k):
                s = PE.go(mm(bank[:, b, :], a(w_at + c * cols + j * P, P), a(src + c * N + h * HALF, HALF), c, k))
            free[b] = evac(dst + j * N + h * HALF, b, s)

        def copied(to, b, s):
            AC.need(s)
            return AC.go(act.activation(a(to, HALF), bank[:, b, :], ACT.Copy))

        def relu_squared(to, b, s):
            AC.need(s)
            s = AC.go(act.activation(a(to, HALF), bank[:, b, :], ACT.Relu))
            V.need(s)
            return V.go(v.tensor_tensor(a(to, HALF), a(to, HALF), bank[:, b, :], ALU.mult))

        for j in range(LAT1 // P):
            for h in range(2):
                product(LT, FC1, LAT1, j, XT, DC, h, copied)
        lt_done = AC.last()
        for j in range(INT1 // P):
            for h in range(2):
                product(HT, UP, INT1, j, XT, DC, h, relu_squared)
        PE.need(lt_done)
        for j in range(LAT1 // P):
            for h in range(2):
                product(LE, EX1, LAT1, j, LT, LAT1 // P, h, copied)
        PE.need(V.last(), AC.last())
        free = [None] * 8
        for t in range(NT):
            b, y = 2 * (t % 4), a(XN1 + t * D, D)
            PE.need(free[b])
            for k in range(LAT1 // P):
                s = PE.go(mm(bank[:, b + 1, :], a(LE + k * N + t * P, P), a(FC2 + k * D, D), k, LAT1 // P))
            for k in range(INT1 // P):
                s = PE.go(mm(bank[:, b, :], a(HT + k * N + t * P, P), a(DOWN + k * D, D), k, INT1 // P))
            AC.need(s)
            s = AC.go(act.activation(y, bank[:, b, :], ACT.Copy))
            V.need(s, rw)
            free[b] = s = V.go(v.scalar_tensor_tensor(y, bank[:, b + 1, :], a(RW + t, 1), y, ALU.mult, ALU.add))
            s = normalise(y, y, t, s)
            G.need(s)
            s = G.go(g.tensor_tensor(y, y, a(LN1, D), ALU.mult))
            V.need(s)
            V.go(v.tensor_tensor(a(X + t * D, D), y, a(X + t * D, D), ALU.add))
        boundary()

        QT, AT = R + 19456, R + 23552
        SC, VN = R + 27648, R + 29696
        PT, COS, SIN = R + 5120, R + 7168, R + 8192
        MK, MNEG, KT = R + 9216, R + 10240, R + 11264
        WT2, CENT2 = R + 12288, C + 2048
        ROT, QC = C, C + 1024
        scale2 = D2 ** -0.5
        w2_in = load("weight2_in", WT2, dram["ffn2"][:, 0:DC * D])
        rope_in = load("rope_in", QT, dram["rope"])
        sem_i = Line(nc.sync, sem("int_in"), 16)
        sem_i.go(nc.sync.dma_start(a(SC, N).bitcast(I32), dram["pos"]))
        sem_m = Line(nc.sync, sem("mask_in"), 16)
        sem_m.go(nc.sync.dma_start(a(MK, N).bitcast(I32), dram["mask"]))
        norms, xt_done = norm_all(C)
        V.need(sem_m.last(), sem_i.last())
        s = V.go(v.tensor_scalar(a(MNEG, N), a(MK, N).bitcast(I32), 0.0, None, ALU.is_equal))
        V.need(s)
        V.need(V.go(v.tensor_scalar(a(MK, N), a(MNEG, N), -1.0, 1.0, ALU.mult, ALU.add)))
        V.go(v.tensor_scalar(a(MNEG, N), a(MNEG, N), NEG / scale2, None, ALU.mult))
        V.go(v.tensor_copy(a(SC, N), a(SC, N).bitcast(I32)))
        V.need(V.last())
        V.need(V.go(v.tensor_scalar(a(VN, N), a(SC, N), 0.0, float(MAXPOS), ALU.is_lt, ALU.mult)))
        V.need(V.go(v.tensor_tensor(a(SC, N), a(SC, N), a(VN, N), ALU.add)))
        V.need(V.go(v.tensor_scalar(a(SC, N), a(SC, N), 0.0, float(MAXPOS - 1), ALU.max, ALU.min)))
        for c in range(MAXPOS // P):
            V.go(v.tensor_scalar(a(AT + c * N, N), a(SC, N), const("posid")[:, c:c + 1], None, ALU.is_equal))
        PE.need(V.last(), rope_in)
        for j, to in ((0, COS), (1, SIN)):
            for h in range(2):
                b = 2 * j + h
                for c in range(MAXPOS // P):
                    s = PE.go(mm(bank[:, 4 + b, :], a(QT + c * 2 * D2 + j * D2, D2), a(AT + c * N + h * HALF, HALF),
                                 c, MAXPOS // P))
                AC.need(s)
                AC.go(act.activation(a(to + h * HALF, HALF), bank[:, 4 + b, :], ACT.Copy))
        boundary()
        cent_in = load("cent_in", CENT2, dram["ffn2"][:, DC * D:])

        NB = 4

        def group(w, arrived, free, tfree, rot_free):
            WQ, WK = w, w + DC * QH2 * D2
            WV, WO = WK + DC * D2, WK + 2 * DC * D2
            n = r = 0
            PE.need(arrived)

            def take():
                nonlocal n
                n += 1
                PE.need(*free[(n - 1) % NB])
                return (n - 1) % NB

            def rotary(b, s, to, h):
                nonlocal r
                rot, qc = a(ROT + r % 2 * HALF, HALF), a(QC + r % 2 * HALF, HALF)
                AC.need(s, rot_free[r % 2])
                AC.go(act.activation(rot[0:64, :], bank[64:P, b, :], ACT.Copy))
                s1 = AC.go(act.activation(rot[64:P, :], bank[0:64, b, :], ACT.Copy))
                V.need(s1)
                s2 = V.go(v.tensor_tensor(qc, bank[:, b, :], a(COS + h * HALF, HALF), ALU.mult))
                G.need(s1)
                s3 = G.go(g.tensor_tensor(rot, rot, a(SIN + h * HALF, HALF), ALU.mult))
                V.need(s3, s2)
                if len(to.shape) == 3:
                    qc, rot = (x.rearrange("p (b s) -> p b s", b=8) for x in (qc, rot))
                rot_free[r % 2] = s = V.go(v.tensor_tensor(to, qc, rot, ALU.add))
                free[b] = (s2,)
                r += 1
                return s

            def project(h):
                b = take()
                for c in range(DC):
                    s = PE.go(mm(bank[:, b, :], a(WK + c * D2, D2), a(XCT + c * N + h * HALF, HALF), c, DC))
                s = rotary(b, s, a(KT + h * HALF, HALF), h)
                for q in range(QH2):
                    b = take()
                    for c in range(DC):
                        s = PE.go(mm(bank[:, b, :], a(WQ + c * QH2 * D2 + q * D2, D2), a(XT + c * N + h * HALF, HALF),
                                     c, DC))
                    s = rotary(b, s, a(QT + h * QH2 * HALF, QH2 * HALF, 8, QH2, S)[:, :, q, :], h)
                b = take()
                for t in range(4):
                    for c in range(DC):
                        m = PE.go(mm(bank[:, b, t * P:(t + 1) * P], a(XCT + c * N + (4 * h + t) * P, P),
                                     a(WV + c * D2, D2), c, DC))
                AC.need(m)
                m = AC.go(act.activation(a(VN + h * HALF, HALF), bank[:, b, :], ACT.Copy))
                free[b] = (m,)
                return s, m

            def scores(h, ready, after):
                PE.need(ready, after)
                for bb in range(8):
                    for hp in range(2):
                        at = (bb // 2 * 4 + hp * 2 + bb % 2) * 64
                        s = PE.go(mm(bank[:, 4 + at // 512, at % 512:at % 512 + 64],
                                     a(QT + ((8 * h + bb) * QH2 + 2 * hp) * S, 2 * S),
                                     a(KT + (8 * h + bb) * S, S)))
                sc = SC + h * 1024
                mk, mn = (a(at + h * HALF, HALF, 4, P).unsqueeze(2).broadcast_to([P, 4, 2, P]) for at in (MK, MNEG))
                s4 = a(sc, 1024).rearrange("p (b h k) -> p b h k", b=4, h=2)
                V.need(s)
                s = read = V.go(v.tensor_tensor(s4, bank[:, 4:6, :].rearrange("p a (b h k) -> p (a b) h k", b=2, h=2),
                                                mk, ALU.mult))
                G.need(s)
                s = G.go(g.tensor_tensor(s4, s4, mn, ALU.add))
                rows = a(sc, 1024, 16, 64)
                top, tot = SOFT + 32 * h, SOFT + 32 * h + 16

                def wide(at):
                    return a(at, 16).unsqueeze(2).broadcast_to([P, 16, 64])

                V.need(s)
                V.need(V.go(v.tensor_reduce(a(top, 16), rows, axis=AX, op=ALU.max)))
                s = V.go(v.tensor_tensor(rows, rows, wide(top), ALU.subtract))
                AC.need(s)
                s = AC.go(act.activation(rows, rows, ACT.Exp, scale=scale2))
                V.need(s)
                V.need(V.go(v.tensor_reduce(a(tot, 16), rows, axis=AX, op=ALU.add)))
                s = V.go(v.reciprocal(a(tot, 16), a(tot, 16)))
                G.need(s)
                return G.go(g.tensor_tensor(rows, rows, wide(tot), ALU.mult)), read

            def attend(h, att, v_ready):
                for k in range(2):
                    PE.need(att, tfree[k])
                    for j in range(4):
                        s = PE.go(pe.transpose(bank[:, 6 + k, j * P:(j + 1) * P],
                                               a(SC + h * 1024 + (4 * k + j) * P, P), const("ident")))
                    AC.need(s)
                    tfree[k] = AC.go(act.activation(a(PT + h * 1024 + k * 512, 512), bank[:, 6 + k, :], ACT.Copy))
                PE.need(v_ready, *tfree)
                for k in range(2):
                    pair = (take(), take())
                    for bp in (2 * k, 2 * k + 1):
                        for b2, b in enumerate(pair):
                            rows = slice(b2 * 64, b2 * 64 + 64)
                            s = PE.go(mm(bank[:, b, (bp % 2) * 256:(bp % 2 + 1) * 256],
                                         a(VN + (4 * h + bp) * P, P)[rows, :],
                                         a(PT + h * 1024 + bp * 256, 256)[rows, :]))
                    AC.need(s)
                    cols = slice((4 * h + 2 * k) * P, (4 * h + 2 * k + 2) * P)
                    for b2, b in enumerate(pair):
                        to = a(AT, QH2 * N, QH2, N)[:, :, cols].rearrange("p h (b c q) -> p b h c q", b=2, c=2)
                        s = AC.go(act.activation(to[:, :, :, b2, :],
                                                 bank[:, b, :].rearrange("p (b h q) -> p b h q", b=2, h=QH2), ACT.Copy))
                        free[b] = (s,)
                PE.need(s)
                for t in range(4):
                    b = take()
                    for q in range(QH2):
                        s = PE.go(mm(bank[:, b, :], a(AT + q * N + (4 * h + t) * P, P), a(WO + q * D, D), q, QH2))
                    x = a(X + (4 * h + t) * D, D)
                    V.need(s)
                    free[b] = (V.go(v.tensor_tensor(x, bank[:, b, :], x, ALU.add)),)
                return s

            k0, v0 = project(0)
            att0, read = scores(0, k0, None)
            k1, v1 = project(1)
            att1, _ = scores(1, k1, read)
            attend(0, att0, v0)
            return attend(1, att1, v1)

        XCT = CT
        SOFT = SMALL + 700
        before = {ln: ln.n for ln in engines}
        per = PER2
        with Turns(G2 // 2, {PE: 2 * per[0], V: 2 * per[1], G: 2 * per[2], AC: 2 * per[3], a2_line[0]: 16,
                             a2_line[1]: 16}) as i:
            free, tfree, rot_free = [()] * NB, [None, None], [None, None]
            SP.need(PE.last())
            a2 = dram["attn2"]
            in1 = a2_line[1].go(nc.sync.dma_start(a(slot[1], WG), a2[bass.ds(2 * i + 1, 1)].rearrange("a p n -> (a p) n")))
            after = nc.sync.snap((2 * i + 2) % G2, min_val=0, max_val=G2 - 1)
            done0 = group(slot[0], Step(a2_line[0], a2_line[0].n, i, 16), free, tfree, rot_free)
            SP.need(done0)
            nxt = a2[bass.ds(after, 1)]
            a2_line[0].go(nc.sync.dma_start(a(slot[0], WG), nxt.rearrange("a p n -> (a p) n")))
            group(slot[1], in1, free, tfree, rot_free)
            PE.need(V.last(), AC.last(), G.last())
        SP.need(a2_line[0].last())
        boundary()

        W3, WO3, SM3 = R, R + 9248, R + 8192
        XN2 = R + 19456
        DT, ASG, AHOT, RSEL, ONES, YD, QSEL = (R + 14336 + 512 * j for j in range(7))
        w3_in = load("attn3_in", W3, dram["attn3"])
        wo3_in = load("wo3_in", WO3, dram["wo3"])
        sm3_in = load("small3_in", SM3, dram["small3"])
        asg_line = Line(nc.sync, sem("assign_in"), 16)
        asg_in = asg_line.go(nc.sync.dma_start(a(ASG, D).bitcast(I32), dram["assign"]))
        norms, xt_done = norm_all(XN2)
        V.need(asg_in)
        V.go(v.memset(a(ONES, P), 1.0))
        V.need(V.go(v.tensor_copy(a(ASG, D), a(ASG, D).bitcast(I32))))
        V.need(V.go(v.tensor_scalar(a(AHOT, D), a(ASG, D), 0.0, float(NCL), ALU.is_lt, ALU.mult)))
        V.need(V.go(v.tensor_tensor(a(ASG, D), a(ASG, D), a(AHOT, D), ALU.add)))
        V.need(V.go(v.tensor_scalar(a(ASG, D), a(ASG, D), 0.0, float(NCL - 1), ALU.max, ALU.min)))
        ahot = V.go(v.tensor_scalar(a(AHOT, D), a(ASG, D), const("posid")[:, 0:1], None, ALU.is_equal))
        PE.need(xt_done, cent_in, w2_in)
        for t in range(NT):
            for c in range(DC):
                s = PE.go(mm(bank[:, 7, t * NCL:(t + 1) * NCL], a(XT + c * N + t * P, P), a(CENT2 + c * NCL, NCL),
                             c, DC))
        dt, top8 = a(DT, 512, NT, NCL), a(QSEL, NT)
        wide8 = top8.unsqueeze(2).broadcast_to([P, NT, NCL])
        b7 = bank[:, 7, :].rearrange("p (t n) -> p t n", t=NT)
        V.need(s)
        V.need(V.go(v.tensor_reduce(top8, b7, axis=AX, op=ALU.max)))
        s = V.go(v.tensor_tensor(dt, b7, wide8, ALU.subtract))
        AC.need(s)
        s = AC.go(act.activation(dt, dt, ACT.Exp, scale=10.0))
        V.need(s)
        V.need(V.go(v.tensor_reduce(top8, dt, axis=AX, op=ALU.add)))
        V.need(V.go(v.reciprocal(top8, top8)))
        V.need(V.go(v.tensor_tensor(dt, dt, wide8, ALU.mult)))
        hit = V.go(v.tensor_scalar(dt, dt, 0.01, None, ALU.is_gt))
        V.need(hit)
        qsel = V.go(v.tensor_reduce(top8, dt, axis=AX, op=ALU.max))
        PE.need(hit)
        for t in range(NT):
            s = PE.go(mm(bank[0:NCL, 6, 0:1], a(DT + t * NCL, NCL), a(ONES, 1), t, NT))
        V.need(s)
        s = V.go(v.tensor_scalar(a(QSEL + 16, 1)[0:NCL, :], bank[0:NCL, 6, 0:1], 0.0, None, ALU.is_gt))
        V.need(s)
        s = V.go(v.tensor_scalar(a(QSEL + 32, P)[0:NCL, :], a(ONES, P)[0:NCL, :], a(QSEL + 16, 1)[0:NCL, :], None,
                                 ALU.mult))
        PE.need(s, ahot)
        s = PE.go(mm(bank[:, 5, :], a(QSEL + 32, P)[0:NCL, :], a(AHOT, D)[0:NCL, :]))
        AC.need(s)
        rsel = AC.go(act.activation(a(RSEL, D), bank[:, 5, :], ACT.Copy))
        free = [None] * 4
        yfree = [None, None]
        YS = [YD, QSEL + 256]
        for t in range(NT):
            b, y = t % 4, a(YS[t % 2], D)
            PE.need(free[b])
            for c in range(DC):
                s = PE.go(mm(bank[:, b, :], a(XT + c * N + t * P, P), a(WT2 + c * D, D), c, DC))
            V.need(s)
            s = free[b] = V.go(v.tensor_tensor(y, bank[:, b, :], a(CENT2 + DC * NCL, D), ALU.add))
            G.need(s, rsel)
            s = G.go(g.tensor_tensor(y, y, a(RSEL, D), ALU.mult))
            V.need(s, qsel)
            x = a(X + t * D, D)
            V.go(v.scalar_tensor_tensor(x, y, a(QSEL + t, 1), x, ALU.mult, ALU.add))
        FW, MIX, SI, BQK, BVB, BVS = R + 24576, R + 11296, R + 8736, R + 8760, R + 6144, R + 6656
        V.need(sm3_in)
        V.need(V.go(v.tensor_scalar(a(SI, 16), a(SM3 + 12, 16), 0.1, a(SM3 + 28, 1), ALU.mult, ALU.mult)))
        for T in range(DC):
            mix = a(MIX + T * P, P)
            s = V.go(v.tensor_tensor(mix.rearrange("p (a b) -> p a b", b=M3),
                                     const("block4").rearrange("p (a b) -> p a b", b=M3),
                                     a(SI + 4 * T, M3).unsqueeze(1).broadcast_to([P, P // M3, M3]), ALU.mult))
            V.need(s)
            V.go(v.tensor_tensor(mix, mix, const("ident"), ALU.add))
            V.go(v.tensor_scalar(a(BVB + T * P, P), a(ONES, P), a(SM3 + 8 + T, 1), None, ALU.mult))
        PE.need(V.last(), w3_in)
        free = [V.last()] * 8
        n = 0
        for w in range(3):
            for c in range(DC):
                PE.need(free[n % 4])
                for T in range(DC):
                    s = PE.go(mm(bank[:, n % 4, T * P:(T + 1) * P], a(W3 + w * 2048 + T * D + c * P, P),
                                 a(MIX + T * P, P)))
                AC.need(s)
                free[n % 4] = AC.go(act.activation(a(FW + w * 2048 + c * D, D), bank[:, n % 4, :], ACT.Copy))
                n += 1
        for j in range(8):
            s = PE.go(mm(bank[:, 6, j:j + 1], a(MIX + j % DC * P, P), a(SM3 + j, 1)))
        for T in range(DC):
            s = PE.go(mm(bank[:, 7, T * P:(T + 1) * P], a(BVB + T * P, P), a(MIX + T * P, P)))
        AC.need(s)
        AC.go(act.activation(a(BQK, 8), bank[:, 6, 0:8], ACT.Copy))
        AC.go(act.activation(a(BVS, D), bank[:, 7, :], ACT.Copy))
        boundary()

        QT3, KT3, VN3, OT = R + 12288, R + 16384, C, R + 20480
        XN3 = R + 20480
        VX, PT3, QX, PR = R + 24576, R + 26624, R + 28672, CT
        VD, KTF = XT, XT + 2048
        W1 = R
        scale3 = 8 ** -0.5
        free = [None] * 8
        n = 0

        def feature_rows(w, src, dst):
            nonlocal n
            for T in range(DC):
                for h in range(2):
                    b = n % 8
                    n += 1
                    PE.need(free[b])
                    for c in range(DC):
                        s = PE.go(mm(bank[:, b, :], a(FW + w * 2048 + c * D + T * P, P), a(src + c * N + h * HALF, HALF),
                                     c, DC))
                    AC.need(s)
                    free[b] = AC.go(act.activation(a(dst + T * N + h * HALF, HALF), bank[:, b, :], ACT.Identity,
                                                   bias=a(BQK + 4 * w + T, 1)))

        norm3 = [normalise(a(X + t * D, D), a(XN3 + t * D, D), t) for t in range(NT)]
        feature_rows(1, CT, KT3)
        for t in range(NT):
            b = n % 8
            n += 1
            PE.need(free[b])
            for c in range(DC):
                s = PE.go(mm(bank[:, b, :], a(CT + c * N + t * P, P), a(FW + 4096 + c * D, D), c, DC))
            V.need(s)
            free[b] = V.go(v.tensor_tensor(a(VN3 + t * D, D), bank[:, b, :], a(BVS, D), ALU.add))
        vn_done = V.last()
        for t in range(NT):
            b = n % 8
            n += 1
            free[b] = transposed(a(XN3 + t * D, D), XT, t, b, free[b], norm3[t])
            G.need(norm3[t])
            G.go(g.tensor_tensor(a(X + t * D, D), a(X + t * D, D), a(SM3 + 29, D), ALU.add))
        PE.need(AC.last())
        feature_rows(0, XT, QT3)
        boundary()
        w1_in = load("w1_in", W1, dram["w1"])
        vd_line = Line(nc.sync, sem("v_copies"), 16)
        with Turns(DC, {PE: 4 * 64, V: 4 * 6, G: 4 * 2 + 1, AC: 4 * 5 + 1, vd_line: 64}) as T:
            SP.need(G.last(), PE.last())
            for rep in range(2):
                for b2 in range(2):
                    dst = a(VD, 16 * P, NT, 2, P)[rep * S:(rep + 1) * S, :, b2, :]
                    src = A[b2 * S:(b2 + 1) * S, VN3:VN3 + NT * D].rearrange("p (t f) -> p t f", t=NT)
                    vd_in = vd_line.go(nc.sync.dma_start(dst, src[:, :, bass.ds(T * P, P)]))
            G.need(PE.last())
            AC.need(PE.last())
            ktf = AC.go(act.activation(a(KTF, N), A[:, bass.ds(KT3 + T * N, N)], ACT.Copy))

            def score(q):
                qx = a(QX + q % 2 * 1024, 1024)
                G.need(tails.get(q - 2), masked.get(q - 2))
                src = A[:, bass.ds(QT3 + T * N + q * 256, 256)].rearrange("p (b r) -> p b r", b=4)
                s = G.go(g.tensor_tensor(qx.rearrange("p (b m r) -> p b m r", b=4, m=M3),
                                         src.unsqueeze(2).broadcast_to([P, 4, M3, S]),
                                         const("is_m").unsqueeze(1).unsqueeze(3).broadcast_to([P, 4, M3, S]), ALU.mult))
                PE.need(s, ktf, score_read.get(q - 1))
                for b in range(4):
                    for mp in range(2):
                        for h in range(4):
                            rows = slice(32 * h, 32 * h + 32)
                            s = PE.go(mm(bank[:, h, (2 * b + mp) * S:(2 * b + mp + 1) * S],
                                         qx[rows, (2 * b + mp) * P:(2 * b + mp + 1) * P],
                                         a(KTF + (4 * q + b) * S, S)[rows, :]))
                scored[q] = s
                at = PR + q % 2 * 2048
                pr = a(at, 2048, 32, S)
                scores4 = bank[:, 0:4, :].rearrange("p h (g k) -> p (h g) k", k=S)
                top, tot = SOFT, SOFT + 32

                def wide(at):
                    return a(at, 32).unsqueeze(2).broadcast_to([P, 32, S])

                V.need(s)
                V.need(V.go(v.tensor_reduce(a(top, 32), scores4, axis=AX, op=ALU.max)), turned.get(q - 2))
                s = score_read[q] = V.go(v.tensor_tensor(pr, scores4, wide(top), ALU.subtract))
                AC.need(s)
                s = AC.go(act.activation(pr, pr, ACT.Exp, scale=scale3))
                V.need(s)
                V.need(V.go(v.tensor_reduce(a(tot, 32), pr, axis=AX, op=ALU.add)))
                s = V.go(v.reciprocal(a(tot, 32), a(tot, 32)))
                G.need(s)
                masked[q] = G.go(g.tensor_tensor(pr, pr, wide(tot), ALU.mult))
                V.need(masked[q])

            def attend3(q):
                for h in range(4):
                    b = 4 + h % 2
                    PE.need(masked[q], tcopied[b])
                    for bb in range(4):
                        s = PE.go(pe.transpose(bank[:, b, bb * P:(bb + 1) * P],
                                               a(PR + q % 2 * 2048 + (h * 4 + bb) * P, P), const("ident")))
                    turned[q] = s
                    AC.need(s, tails.get(q - 1))
                    tcopied[b] = AC.go(act.activation(a(PT3 + h * 512, 512), bank[:, b, :], ACT.Copy))
                PE.need(AC.last(), vx, kept.get(q - 2))
                ob = 6 + q % 2
                for bb in range(4):
                    for h in range(4):
                        rows = slice(32 * h, 32 * h + 32)
                        s = PE.go(mm(bank[rows, ob, bb * P:(bb + 1) * P],
                                     a(VX + (4 * q + bb) * P + 32 * h, 32), a(PT3 + (h * 4 + bb) * P, P)))
                tails[q] = s
                o2 = bank[:, ob, :].rearrange("p (b m r) -> p b m r", b=4, m=2)
                to = A[:, bass.ds(OT + T * N + q * 256, 256)].rearrange("p (b r) -> p b r", b=4)
                V.need(s)
                odd = const("is_odd")
                V.need(V.go(v.tensor_scalar(to, o2[:, :, 0, :], odd[:, 0:1], None, ALU.mult)))
                kept[q] = V.go(v.scalar_tensor_tensor(to, o2[:, :, 1, :], odd[:, 1:2], to, ALU.mult, ALU.add))

            scored, score_read, masked, turned, tails, kept = {}, {}, {}, {}, {}, {}
            tcopied = {4: None, 5: None}
            score(0)
            G.need(vd_in)
            vx = G.go(g.tensor_tensor(a(VX, 2048).rearrange("p (f m) -> p f m", m=M3),
                                      a(VD, 2048).rearrange("p (f m) -> p f m", m=M3),
                                      const("m_half").unsqueeze(1).broadcast_to([P, 512, M3]), ALU.mult))
            for q in range(1, 4):
                score(q)
                attend3(q - 1)
            attend3(3)
            PE.need(V.last(), AC.last())
        PE.need(V.last(), wo3_in)
        G.need(G.last())
        V.need(G.last())
        free = [None] * 4
        for t in range(NT):
            b = t % 4
            PE.need(free[b])
            for c in range(DC):
                s = PE.go(mm(bank[:, b, :], a(OT + c * N + t * P, P), a(WO3 + c * D, D), c, DC))
            V.need(s)
            x = a(X + t * D, D)
            free[b] = V.go(v.tensor_tensor(x, bank[:, b, :], x, ALU.add))
        boundary()

        C1, C2, W2, LOW = R + 7168, R + 9248, R + 12288, R + 19456
        RING = 3
        EQ, HS, HTS, TOPS = R + 20480, R + 20480 + RING * D, R + 20480 + 2 * RING * D, R + 20480 + 3 * RING * D
        c1_in = load("c1_in", C1, dram["c1"])
        c2_in = load("c2_in", C2, dram["c2"], part=RANK)
        w2_in = load("w2_in", W2, dram["w2"])
        norms, xt_done = norm_all(C)
        PE.need(xt_done, c1_in)
        for h in range(2):
            for c in range(DC):
                s = PE.go(mm(bank[0:RANK, 2 + h, :], a(C1 + c * RANK, RANK), a(XT + c * N + h * HALF, HALF), c, DC))
            AC.need(s)
            s = AC.go(act.activation(a(LOW + h * HALF, HALF)[0:RANK, :], bank[0:RANK, 2 + h, :], ACT.Copy))
        PE.need(s, c2_in, w1_in, w2_in)
        units = [(t, j) for t in range(NT) for j in range(4)]
        inter_read, h_read, hs_done, picked, turned, hts, outed = {}, {}, {}, {}, {}, {}, {}
        eq_done = {}
        stored = sem("stored")
        for u in range(len(units) + 2):
            if u < len(units):
                t, j = units[u]
                wd = min(D, INTER - j * D)
                nb = wd // BLK
                bi, bh, ring = u % 2, 2 + u % 2, u % RING
                eq = a(EQ + ring * D, wd)
                blocks = eq.rearrange("p (n k) -> p n k", k=BLK)
                tops = a(TOPS + ring * 32, nb)
                PE.need(inter_read.get(u - 2))
                s1 = PE.go(mm(bank[:, bi, 0:wd], a(LOW + t * P, P)[0:RANK, :], a(C2 + j * D, wd)[0:RANK, :]))
                PE.need(h_read.get(u - 2))
                for c in range(DC):
                    s2 = PE.go(mm(bank[:, bh, 0:wd], a(XT + c * N + t * P, P), a(W1 + c * INTER + j * D, wd), c, DC))
                hs_done[u] = s2
                inter = bank[:, bi, 0:wd].rearrange("p (n k) -> p n k", k=BLK)
                V.need(s1)
                V.need(V.go(v.tensor_reduce(tops, inter, axis=AX, op=ALU.max)))
                s = inter_read[u] = V.go(v.tensor_tensor(blocks, inter, tops.unsqueeze(2).broadcast_to([P, nb, BLK]),
                                                         ALU.is_equal))
                G.need(s)
                eq_done[u] = G.go(g.tensor_tensor(blocks, blocks, const("down32").unsqueeze(1)
                                                  .broadcast_to([P, nb, BLK]), ALU.mult))
            if 0 <= u - 1 < len(units):
                w = u - 1
                t, j = units[w]
                wd = min(D, INTER - j * D)
                nb = wd // BLK
                ring = w % RING
                eq = a(EQ + ring * D, wd)
                blocks = eq.rearrange("p (n k) -> p n k", k=BLK)
                tops = a(TOPS + ring * 32, nb)
                V.need(eq_done[w])
                V.need(V.go(v.tensor_reduce(tops, blocks, axis=AX, op=ALU.max)))
                s = V.go(v.tensor_tensor(blocks, blocks, tops.unsqueeze(2).broadcast_to([P, nb, BLK]), ALU.is_equal))
                V.need(s, hs_done[w], turned.get(w - RING))
                h_read[w] = V.go(v.scalar_tensor_tensor(a(HS + ring * D, wd), bank[:, 2 + w % 2, 0:wd], 0.0, eq,
                                                        ALU.max, ALU.mult))
            if 0 <= u - 2 < len(units):
                w = u - 2
                t, j = units[w]
                wd = min(D, INTER - j * D)
                ring = w % RING
                b = 4 + w % 2
                PE.need(h_read[w], hts.get(w - 2))
                for k in range(wd // P):
                    s = PE.go(pe.transpose(bank[:, b, k * P:(k + 1) * P], a(HS + ring * D + k * P, P), const("ident")))
                turned[w] = s
                AC.need(s, outed.get(w - RING))
                hts[w] = s = AC.go(act.activation(a(HTS + ring * D, wd), bank[:, b, 0:wd], ACT.Copy))
                PE.need(s)
                ob = 6 + t % 2
                if j == 0:
                    PE.need(outed.get(("x", t - 2)))
                for k in range(wd // P):
                    f = j * 4 + k
                    s = PE.go(mm(bank[:, ob, :], a(HTS + ring * D + k * P, P), a(W2 + f * D, D), f, NI))
                outed[w] = s
                if j == 3:
                    x = a(X + t * D, D)
                    V.need(s)
                    s = outed[("x", t)] = V.go(v.tensor_tensor(x, bank[:, ob, :], x, ALU.add))
                    SP.need(s)
                    nc.sync.dma_start(out[t * P:(t + 1) * P, :], x).then_inc(stored, 16)
        nc.sync.wait_ge(stored, 16 * NT)


def kernel(**inputs):
    import concourse.bacc as _bacc
    from concourse.bass_utils import run_bass_kernel_spmd as _run

    nc = _bacc.Bacc("TRN2", target_bir_lowering=False, num_devices=1)
    arrays = lay_out(inputs)
    dram = {n: nc.dram_tensor(f"in_{n}", v.shape, mybir.dt.from_np(v.dtype), kind="ExternalInput").ap()
            for n, v in arrays.items()}
    out = nc.dram_tensor("out", (N, D), F32, kind="ExternalOutput").ap()
    program(nc, dram, out)
    r = _run(nc, [{f"in_{n}": v for n, v in arrays.items()}], core_ids=[0])
    return r.results[0]["out"].reshape(B, S, D)
```

```python
from contextlib import ExitStack

import numpy as np

import concourse.bass as bass
from concourse import mybir

F32 = mybir.dt.float32
I32 = mybir.dt.int32
U32 = mybir.dt.uint32
ALU = mybir.AluOpType
ACT = mybir.ActivationFunctionType
AX = mybir.AxisListType.X

P = 128
B, S, D = 16, 64, 512
NT = B * S // P
DC = D // P
N = B * S
HALF = N // 2
EPS = 1e-5
NEG = -1e9

H0, WIN = 8, 16
HD0 = S // H0
PADL = WIN // 2
KW = D + WIN - 1
E0 = 8
INT1, LAT1 = 1024, 256
G2, QH2, D2 = 8, 4, 128
WG = DC * QH2 * D2 + 2 * DC * D2 + QH2 * D
MAXPOS = 512
NCL = 64
M3 = 4
INTER, BLK, RANK = 1792, 32, 16
NI = INTER // P


class Step:

    def __init__(self, line, n, turn=None, per=0):
        self.line, self.n, self.turn, self.per = line, n, turn, per

    def value(self):
        return self.n if self.turn is None or not self.per else self.turn * self.per + self.n

    def before(self):
        assert self.n - self.per >= 0
        return Step(self.line, self.n - self.per, self.turn, self.per)


class Line:

    def __init__(self, engine, sem, step=1):
        self.e, self.sem, self.step = engine, sem, step
        self.n, self.turn, self.per, self.known = 0, None, 0, {}

    def go(self, ins):
        ins.then_inc(self.sem, self.step)
        self.n += self.step
        return self.at(self.n)

    def at(self, n):
        return Step(self, n, self.turn, self.per)

    def last(self):
        return self.at(self.n)

    def need(self, *steps):
        for s in steps:
            if s is None or s.n == 0:
                continue
            key = (id(s.line), s.turn is not None and s.per > 0)
            if self.known.get(key, -1) >= s.n:
                continue
            self.known[key] = s.n
            self.e.wait_ge(s.line.sem, s.value())


def chunked(w):
    k, n = w.shape
    return np.ascontiguousarray(w.reshape(k // P, P, n).transpose(1, 0, 2).reshape(P, -1))


def constants():
    k = np.arange(P)
    parts = {
        "ident": np.eye(P),
        "selw": (np.arange(2 * P - 16)[None, :] == (P - 16 + k // S * H0 + k % S // HD0)[:, None]),
        "selt": np.concatenate([(k[:, None] == 16 * p + (k // S * H0 + k % S // HD0)[None, :])
                                for p in range(NT)], 1),
        "block8": np.kron(np.eye(P // 8), np.ones((8, 8))),
        "block4": np.kron(np.eye(P // 4), np.ones((4, 4))),
        "iota8": np.tile(np.arange(8), (P, 1)),
        "posid": k[:, None] + P * np.arange(MAXPOS // P)[None, :],
        "down32": np.tile(BLK - np.arange(BLK), (P, 1)),
        "is_m": k[:, None] % M3 == np.arange(M3)[None, :],
        "is_h": k[:, None] // 32 == np.arange(4)[None, :],
        "is_odd": k[:, None] % 2 == np.arange(2)[None, :],
        "m_half": np.arange(M3)[None, :] // 2 == (k // S)[:, None],
    }
    at, cols = {}, 0
    for name, a in parts.items():
        at[name] = (cols, cols + a.shape[1])
        cols += a.shape[1]
    return np.concatenate([a.astype(np.float32) for a in parts.values()], 1), at


def rope_tables():
    inv = (1.0 / 10000.0 ** (np.arange(0, D2, 2, dtype=np.float32) / np.float32(D2))).astype(np.float32)
    f = np.arange(MAXPOS, dtype=np.float32)[:, None] * inv[None, :]
    cos = np.concatenate([np.cos(f), np.cos(f)], 1)
    sin = np.concatenate([-np.sin(f), np.sin(f)], 1)
    return chunked(np.concatenate([cos, sin], 1).astype(np.float32))


def lay_out(i):
    f = {n: np.asarray(a) for n, a in i.items()}
    x, c = f["x"].reshape(N, D), f["ctx_4096"].reshape(N, D)

    def twice(w):
        z = np.zeros((P, P), w.dtype)
        z[:S, :S] = w.T
        z[S:, S:] = w.T
        return z

    def rows(v):
        return np.broadcast_to(v[None, :], (P, v.shape[0]))

    a = {"x": chunked(x), "c": chunked(c), "ct": chunked(c.T), "const": constants()[0]}
    a["w0"] = np.concatenate([twice(f[f"L0_xattn_{n}"]) for n in ("Wq", "Wk", "Wv", "Wo")]
                             + [np.tile(f[f"L0_xattn_{n}"], 2)[:, None] for n in ("bq", "bk", "bv", "bo")], 1)
    a["gate0"] = chunked(f["L0_ffn_gate_w"])
    a["expert0"] = np.concatenate([chunked(w) for w in f["L0_ffn_expert_w"]], 1)
    a["ffn1"] = np.concatenate([chunked(f[f"L1_ffn_{n}"]) for n in ("up_w", "fc1_w", "expert_w", "fc2_w", "down_w",
                                                                    "gate_w")], 1)
    a["ln1"] = np.concatenate([rows(f["L1_ffn_ln_gamma"]), rows(f["L1_ffn_ln_beta"])], 1)
    q, k, v, o = (f[f"L2_xattn_W{n}"] for n in "qkvo")
    w = QH2 * D2
    a["attn2"] = np.stack([np.concatenate([chunked(q[:, g * w:(g + 1) * w]), chunked(k[:, g * D2:(g + 1) * D2]),
                                           chunked(v[:, g * D2:(g + 1) * D2]), chunked(o[g * w:(g + 1) * w])], 1)
                           for g in range(G2)])
    a["pos"] = rows(f["pos_BxS2"].reshape(-1))
    m = f["mask_BxSxS2_ik0"].transpose(1, 0, 2).reshape(S, -1)
    a["mask"] = np.concatenate([m, m], 0)
    a["rope"] = rope_tables()
    a["ffn2"] = np.concatenate([chunked(f["L2_ffn_weight"].T), chunked(f["L2_ffn_centroids"].T),
                                rows(f["L2_ffn_bias"])], 1)
    a["assign"] = rows(f["L2_ffn_assignments"])
    a["attn3"] = np.concatenate([chunked(f[f"L3_xattn_W{n}"]) for n in "qkv"], 1)
    a["wo3"] = chunked(f["L3_xattn_Wo"].T)
    inter = f["L3_xattn_interference"].reshape(DC, 4, 1, M3, M3)
    inter = np.broadcast_to(inter, (DC, 4, P // 16, M3, M3)).reshape(DC, P, M3).transpose(1, 0, 2).reshape(P, -1)
    a["small3"] = np.concatenate([f[f"L3_xattn_b{n}"].reshape(DC, P).T for n in "qkv"]
                                 + [inter, rows(f["L3_xattn_amp"]), rows(f["L3_xattn_bo"])], 1)
    a["c1"] = chunked(f["L3_ffn_c1_w"].T)
    a["c2"] = f["L3_ffn_c2_w"].T
    a["w1"] = chunked(f["L3_ffn_w1"].T)
    a["w2"] = chunked(f["L3_ffn_w2t"])
    return {n: np.ascontiguousarray(v) for n, v in a.items()}


PER2 = (168, 38, 14, 36)
X, XT, CT, C, CONST = 0, 4096, 8192, 12288, 16384
CONST_AT = constants()[1]
NCONST = max(b for _, b in CONST_AT.values())
SMALL = CONST + NCONST
R = SMALL + 1024
WORDS = R + 30720


def program(nc, dram, out):
    with ExitStack() as ctx:
        A = ctx.enter_context(nc.sbuf_tensor("arena", [P, WORDS], F32))
        bank = ctx.enter_context(nc.psum_tensor("banks", [P, 8, 512], F32))

        def sem(name):
            return ctx.enter_context(nc.semaphore(name))

        PE, V, G, AC = (Line(e, sem(n)) for e, n in ((nc.tensor, "pe_steps"), (nc.vector, "vector_steps"),
                                                      (nc.gpsimd, "pool_steps"), (nc.scalar, "act_steps")))
        SP = Line(nc.sync, sem("sp_steps"))
        engines = (PE, V, G, AC)
        pe, v, g, act = nc.tensor, nc.vector, nc.gpsimd, nc.scalar

        def a(at, n, *shape):
            t = A[:, bass.ds(at, n)]
            if len(shape) == 2:
                return t.rearrange("p (a b) -> p a b", a=shape[0], b=shape[1])
            if len(shape) == 3:
                return t.rearrange("p (a b c) -> p a b c", a=shape[0], b=shape[1], c=shape[2])
            return t

        def const(name):
            lo, hi = CONST_AT[name]
            return A[:, CONST + lo:CONST + hi]

        def load(name, to, src, *after, line=None, part=P):
            line = line or Line(nc.sync, sem(name), 16)
            SP.need(*after)
            return line.go(nc.sync.dma_start(A[0:part, bass.ds(to, src.shape[-1])], src))

        class Turns:

            def __init__(self, turns, per):
                self.turns, self.per = turns, per

            def __enter__(self):
                self.ctx = nc.Fori(0, self.turns)
                self.i = self.ctx.__enter__()
                self.base = {ln: ln.n for ln in self.per}
                for ln in self.per:
                    ln.turn, ln.per = self.i, self.per[ln]
                for ln in engines + (SP,):
                    ln.known = {key: n for key, n in ln.known.items() if not key[1]}
                return self.i

            def __exit__(self, *exc):
                if exc[0]:
                    return False
                moved = [ln.n - self.base[ln] for ln in self.per]
                assert all(ln.n - self.base[ln] == self.per[ln] for ln in self.per), moved
                self.ctx.__exit__(None, None, None)
                for ln in self.per:
                    ln.n = self.base[ln] + self.turns * self.per[ln]
                    ln.turn, ln.per = None, 0
                for ln in engines + (SP,):
                    ln.known = {}
                return False

        def boundary():
            for ln in engines + (SP,):
                ln.need(*(o.last() for o in engines))

        def mm(dst, lhsT, rhs, k=0, n=1, **kw):
            return pe.matmul(dst, lhsT=lhsT, rhs=rhs, start=(k == 0), stop=(k == n - 1), **kw)

        STAT, MEAN, RSTD = SMALL, SMALL + 48, SMALL + 64
        HALVES = SMALL + 72
        g_half = G.go(g.memset(a(HALVES, NT), -0.5))

        def moments(src, t):
            V.need(V.go(v.bn_stats(a(STAT + 6 * t, 6), src)))
            return V.go(v.bn_aggr(a(MEAN + 2 * t, 2), a(STAT + 6 * t, 6)))

        def root(t, n):
            V.need(V.last())
            var = a(MEAN + 2 * t, 2 * n, n, 2)[:, :, 1]
            s = V.go(v.tensor_scalar(a(RSTD + t, n), var, EPS, None, ALU.add))
            G.need(s, g_half)
            return G.go(g.tensor_tensor(a(RSTD + t, n), a(RSTD + t, n), a(HALVES, n), ALU.pow))

        def scaled(src, dst, t):
            return V.go(v.tensor_scalar(dst, src, a(MEAN + 2 * t, 1), a(RSTD + t, 1), ALU.subtract, ALU.mult))

        def normalise(src, dst, t, *after):
            V.need(*after)
            moments(src, t)
            V.need(root(t, 1))
            return scaled(src, dst, t)

        def norms_of(xn, ready=()):
            V.need(*ready)
            for t in range(4):
                moments(a(X + t * D, D), t)
            r0 = root(0, 4)
            for t in range(4, NT):
                moments(a(X + t * D, D), t)
            r1 = root(4, 4)
            out = []
            for t in range(NT):
                V.need(r0 if t < 4 else r1)
                out.append(scaled(a(X + t * D, D), a(xn + t * D, D), t))
            return out

        def transposed(src, dst, t, b, free, *after):
            PE.need(free, *after)
            for c in range(DC):
                s = PE.go(pe.transpose(bank[:, b, c * P:(c + 1) * P], src[:, c * P:(c + 1) * P], const("ident")))
            AC.need(s)
            return AC.go(act.activation(a(dst, DC * N, DC, N)[:, :, t * P:(t + 1) * P],
                                        bank[:, b, :].rearrange("p (c n) -> p c n", c=DC), ACT.Copy))

        def norm_all(xn, ready=(), with_t=True):
            free = [None] * 4
            ns = norms_of(xn, ready)
            if with_t:
                for t in range(NT):
                    free[t % 4] = transposed(a(xn + t * D, D), XT, t, t % 4, free[t % 4], ns[t])
            return ns, free[3]

        x_in = load("x_in", X, dram["x"])
        const_in = load("const_in", CONST, dram["const"])
        c_in = load("c_in", C, dram["c"])

        Q0, K0, V0 = R, R + 4096, R + 4096 + NT * KW
        DOTS = V0 + NT * KW
        PROD = DOTS + WIN * D
        assert PROD + 8 * D <= R + 30720
        W0 = SMALL + 96
        XN0 = XT
        w0_in = load("w0_in", W0, dram["w0"])
        ct_in = load("ct_in", CT, dram["ct"])
        scale0 = HD0 ** -0.5

        pads = []
        for at in (K0, V0):
            kv = a(at, NT * KW, NT, KW)
            pads.append(G.go(g.memset(kv[:, :, 0:PADL], 0.0)))
            pads.append(G.go(g.memset(kv[:, :, PADL + D:KW], 0.0)))
        norms, _ = norm_all(XN0, (x_in,), with_t=False)
        PE.need(w0_in, c_in, const_in)
        AC.need(w0_in)
        bias0 = a(W0 + 4 * P, 4)
        free = [None] * 8
        n = 0
        for t in range(NT):
            for j, (src, dst) in enumerate(((XN0, Q0 + t * D), (C, K0 + t * KW + PADL), (C, V0 + t * KW + PADL))):
                PE.need(free[n % 8], norms[t] if j == 0 else None)
                s = PE.go(mm(bank[:, n % 8, :], a(W0 + j * P, P), a(src + t * D, D)))
                AC.need(s)
                free[n % 8] = AC.go(act.activation(a(dst, D), bank[:, n % 8, :], ACT.Identity,
                                                   bias=bias0[:, j:j + 1]))
                n += 1
        qkv = AC.last()
        lo = CONST_AT["selw"][0] + CONST
        PE.need(qkv)
        with Turns(WIN // 2, {PE: 16, V: 10, G: 6, AC: 2}) as i:
            done = []
            for u in range(2):
                prods = []
                for t in range(NT):
                    ln = G if t % 3 == 2 and t < 8 and (t != 8) else V
                    ln = G if t in (1, 4, 6) else V
                    ln.need(qkv, pads[-1], done[t] if u else PE.at(PE.n + NT + t + 1).before())
                    prods.append(ln.go(ln.e.tensor_tensor(
                        a(PROD + t * D, D), a(Q0 + t * D, D),
                        A[:, bass.ds(K0 + t * KW + i * 2 + u, D)], ALU.mult)))
                if not u:
                    PE.need(AC.at(AC.n + 1).before())
                else:
                    PE.need(AC.at(AC.n + 1).before())
                new = []
                for t in range(NT):
                    PE.need(prods[t])
                    new.append(PE.go(mm(bank[:, u, :], A[:, lo + P - 16 - 16 * t:lo + 2 * P - 16 - 16 * t],
                                        a(PROD + t * D, D), t, NT)))
                done = new
                AC.need(new[-1])
                AC.go(act.activation(A[:, bass.ds(DOTS + i * 2 * D + u * D, D)], bank[:, u, :], ACT.Copy))
        TOP, SUM = PROD, PROD + D
        dots = a(DOTS, WIN * D, WIN, D)
        V.need(AC.last(), PE.last())
        G.need(AC.last())
        atts = []
        for c in range(4):
            cut = slice(c * P, (c + 1) * P)
            part = dots[:, :, cut]
            by_t = part.rearrange("p w t -> p t w")

            def over_w(at):
                return a(at, D)[:, cut].unsqueeze(1).broadcast_to([P, WIN, P])

            s = V.go(v.tensor_reduce(a(TOP, D)[:, cut], by_t, axis=AX, op=ALU.max))
            G.need(s)
            s = G.go(g.tensor_tensor(part, part, over_w(TOP), ALU.subtract))
            AC.need(s)
            s = AC.go(act.activation(part, part, ACT.Exp, scale=scale0))
            V.need(s)
            s = V.go(v.tensor_reduce(a(SUM, D)[:, cut], by_t, axis=AX, op=ALU.add))
            V.need(s)
            s = V.go(v.reciprocal(a(SUM, D)[:, cut], a(SUM, D)[:, cut]))
            V.need(s)
            atts.append(V.go(v.tensor_tensor(part, part, over_w(SUM), ALU.mult)))
        SELT = XT
        AV, AVN = Q0, 8
        PE.need(atts[-1])
        AC.need(atts[-1])
        V.need(atts[-1])
        s_bo = None
        with Turns(NT, {PE: WIN + 4, V: WIN + 1, G: 12, AC: 1}) as i:
            AC.need(PE.at(PE.n + WIN + 4).before())
            sel = AC.go(act.activation(a(SELT, P), A[:, bass.ds(CONST + CONST_AT["selt"][0] + i * P, P)], ACT.Copy))
            spread, avs, out_mm = [], [], None
            quads = []
            PE0, V0n, G0 = PE.n, V.n, G.n

            def to_out(k):
                PE.need(quads[k])
                if k == 0:
                    PE.need(V.at(V0n + WIN + 1).before())
                return PE.go(mm(bank[:, 4, :], a(W0 + 3 * P, P), a(AV + (4 * k % AVN) * D, D), k, 4))

            outs = []
            for w in range(WIN):
                PE.need(sel)
                PE.need(avs[w - 4] if w >= 4 else V.at(V0n + WIN - 3 + w).before())
                s = PE.go(mm(bank[:, w % 4, :], a(SELT, P), A[:, DOTS + w * D:DOTS + (w + 1) * D]))
                V.need(s)
                if w >= AVN:
                    V.need(quads[w // 4 - 2], outs[w // 4 - 2] if w % 4 == 0 else None)
                else:
                    V.need(G.at(G0 + 3 * (w // 4 + 2) + 3).before(),
                           PE.at(PE0 + WIN + w // 4 + 3).before() if w % 4 == 0 else None)
                avs.append(V.go(v.tensor_tensor(a(AV + w % AVN * D, D), bank[:, w % 4, :],
                                                A[:, bass.ds(V0 + i * KW + w, D)], ALU.mult)))
                if w % 4 == 3:
                    b0 = AV + (w - 3) % AVN * D
                    G.need(avs[w])
                    s1 = G.go(g.tensor_tensor(a(b0, D), a(b0, D), a(b0 + D, D), ALU.add))
                    s2 = G.go(g.tensor_tensor(a(b0 + 2 * D, D), a(b0 + 2 * D, D), a(b0 + 3 * D, D), ALU.add))
                    G.need(s2)
                    quads.append(G.go(g.tensor_tensor(a(b0, D), a(b0, D), a(b0 + 2 * D, D), ALU.add)))
                if w % 4 == 3 and w > 4:
                    outs.append(to_out(w // 4 - 1))
            outs.append(to_out(3))
            V.need(outs[-1])
            V.go(v.scalar_tensor_tensor(A[:, bass.ds(X + i * D, D)], bank[:, 4, :], bias0[:, 3:4],
                                        A[:, bass.ds(X + i * D, D)], ALU.add, ALU.add))
        boundary()

        XN = R
        EXP = R + 28672
        WREP, WCOL = R + 4096, R + 4096 + 64
        GATE = R + 4096 + 128
        LOG = GATE + 32
        TOP8, IDX = LOG + 64, LOG + 128
        TMP = LOG + 192
        gate_in = load("gate_in", GATE, dram["gate0"])
        exp_line = Line(nc.sync, sem("expert_in"), 16)
        for e in range(E0):
            exp_in = load("", EXP - e * 2048, dram["expert0"][:, e * 2048:(e + 1) * 2048], exp_line.last(),
                          line=exp_line)
        norms, xt_done = norm_all(XN)
        PE.need(xt_done, gate_in)
        last_banks = (AC.last(),)

        def logits(gate_at, b):
            for t in range(NT):
                for c in range(DC):
                    s = PE.go(mm(bank[:, b, t * 8:(t + 1) * 8], a(XT + c * N + t * P, P), a(gate_at + c * 8, 8), c, DC))
            return s

        s = logits(GATE, 7)
        V.need(s)
        V.need(V.go(v.tensor_copy(a(LOG, 64), bank[:, 7, 0:64])))
        for t in range(NT):
            V.go(v.max(a(TOP8 + 8 * t, 8), a(LOG + 8 * t, 8)))
        V.need(V.last())
        for t in range(NT):
            V.go(v.max_index(a(IDX + 8 * t, 8).bitcast(U32), a(TOP8 + 8 * t, 8), a(LOG + 8 * t, 8)))
        top = a(TOP8, 64, NT, 8)
        s = V.go(v.tensor_tensor(a(TMP, NT), top[:, :, 1], top[:, :, 0], ALU.subtract))
        AC.need(s)
        s = AC.go(act.activation(a(TMP, NT), a(TMP, NT), ACT.Exp))
        V.need(s)
        V.need(V.go(v.tensor_scalar(a(TMP + 8, NT), a(TMP, NT), 1.0, None, ALU.add)))
        V.need(V.go(v.reciprocal(a(TMP + 8, NT), a(TMP + 8, NT))))
        V.need(V.go(v.tensor_tensor(a(TMP, NT), a(TMP, NT), a(TMP + 8, NT), ALU.mult)))
        V.need(V.go(v.tensor_copy(a(TMP + 16, 64), a(IDX, 64).bitcast(U32))))
        idx = a(TMP + 16, 64, NT, 8)
        pick = [a(TMP + 80 + 64 * j, 64, E0, NT) for j in range(2)]
        for j, weight in ((0, TMP + 8), (1, TMP)):
            V.need(V.go(v.tensor_tensor(pick[j], const("iota8").unsqueeze(2).broadcast_to([P, E0, NT]),
                                        idx[:, :, j].unsqueeze(1).broadcast_to([P, E0, NT]), ALU.is_equal)))
            V.need(V.go(v.tensor_tensor(pick[j], pick[j], a(weight, NT).unsqueeze(1).broadcast_to([P, E0, NT]),
                                        ALU.mult)))
        V.need(V.go(v.tensor_tensor(a(WREP, 64, E0, NT), pick[0], pick[1], ALU.add)))
        V.go(v.memset(a(TMP, 1), 0.0))
        PE.need(V.last())
        with Turns(E0, {PE: NT * DC, V: NT + 1}) as e:
            V.need(V.last())
            col = V.go(v.tensor_copy(a(WCOL, NT), A[:, bass.ds(WREP + e * NT, NT)]))
            PE.need(Step(exp_line, 16, e, 16))
            for t in range(NT):
                PE.need(V.at(V.n + 1).before() if t == 0 else V.at(V.n + 1).before())
                for c in range(DC):
                    s = PE.go(mm(bank[:, t, :], a(XT + c * N + t * P, P),
                                 A[:, bass.ds(EXP - e * 2048 + c * D, D)], c, DC))
                V.need(s, col)
                V.go(v.scalar_tensor_tensor(a(X + t * D, D), bank[:, t, :], a(WCOL + t, 1), a(X + t * D, D),
                                            ALU.mult, ALU.add))
        boundary()

        F1 = R + 14336
        f1_in = load("ffn1_in", F1, dram["ffn1"])
        KE, KET, KV = R + 4096, F1 - 0 + 10784, R + 8192
        NMAX, KSUM = R + 13312, R + 13320
        assert KET + 4096 <= R + 30720
        ke = []
        for t in range(NT):
            V.need(None)
            s = V.go(v.tensor_reduce(a(NMAX + t, 1), a(C + t * D, D), axis=AX, op=ALU.max, negate=True))
            AC.need(s)
            ke.append(AC.go(act.activation(a(KE + t * D, D), a(C + t * D, D), ACT.Exp, bias=a(NMAX + t, 1),
                                           accum_out=a(KSUM + t, 1))))
        V.need(ke[-1])
        ksum = V.go(v.reciprocal(a(KSUM, NT), a(KSUM, NT)))
        norms, _ = norm_all(XN, with_t=False)
        free = [None] * 8
        for t in range(NT):
            free[t % 2] = transposed(a(KE + t * D, D), KET, t, t % 2, free[t % 2], ke[t])
        for t in range(NT):
            PE.need(free[0], free[1], free[2 + t % 2])
            for c in range(DC):
                s = PE.go(mm(bank[:, 2 + t % 2, 0:P], a(KET + c * N + t * P, P), a(CT + c * N + t * P, P), c, DC))
            V.need(s, ksum)
            free[2 + t % 2] = V.go(v.scalar_tensor_tensor(a(KV + t * P, P), bank[:, 2 + t % 2, 0:P], a(KSUM + t, 1),
                                                          const("block8"), ALU.mult, ALU.mult))
        for t in range(NT):
            AC.need(norms[t])
            xq = a(XN + t * D, D)
            s = AC.go(act.activation(xq, xq, ACT.Exp))
            b = 4 + t % 2
            PE.need(s, free[b])
            s = PE.go(mm(bank[:, b, :], const("block8"), xq))
            V.need(s)
            s = V.go(v.reciprocal(a(KE + t * D, D), bank[:, b, :]))
            free[b] = s
            G.need(s)
            s = G.go(g.tensor_tensor(xq, xq, a(KE + t * D, D), ALU.mult))
            PE.need(s, free[2], free[3], free[6 + t % 2])
            s = PE.go(mm(bank[:, 6 + t % 2, :], a(KV + t * P, P), xq))
            V.need(s)
            free[6 + t % 2] = V.go(v.tensor_tensor(a(X + t * D, D), bank[:, 6 + t % 2, :], a(X + t * D, D), ALU.add))
        boundary()

        UP = F1
        FC1 = UP + DC * INT1
        EX1 = FC1 + DC * LAT1
        FC2 = EX1 + LAT1 // P * LAT1
        DOWN = FC2 + LAT1 // P * D
        GATE1 = DOWN + INT1 // P * D
        XN1 = C
        HT = R + 5120
        LT, LE, LN1 = R + 25120, R + 27168, R + 29216
        G_OFF = LN1 + 1024
        slot = [R, R + 14336]
        a2_line = [Line(nc.sync, sem(f"group_in{j}"), 16) for j in range(2)]
        ln1_in = load("ln1_in", LN1, dram["ln1"])
        load("", slot[0], dram["attn2"][0], line=a2_line[0])
        norms, xt_done = norm_all(XN1)
        PE.need(xt_done, f1_in)
        s = logits(GATE1, 7)
        V.need(s)
        V.need(V.go(v.tensor_copy(a(G_OFF, 64), bank[:, 7, 0:64])))
        for t in range(NT):
            V.go(v.max(a(G_OFF + 64 + 8 * t, 8), a(G_OFF + 8 * t, 8)))
        V.need(V.last())
        top = a(G_OFF + 64, 64, NT, 8)
        RW = G_OFF + 128
        rw = V.go(v.tensor_tensor(a(RW, NT), top[:, :, 0], top[:, :, 1], ALU.add))
        G.need(ln1_in, norms[-1])
        for t in range(NT):
            G.go(g.tensor_tensor(a(X + t * D, D), a(X + t * D, D), a(LN1 + D, D), ALU.add))
        free = [None] * 8
        n = 0

        def product(dst, w_at, cols, j, src, k, h, evac):
            nonlocal n
            b = n % 7
            n += 1
            PE.need(free[b])
            for c in range(k):
                s = PE.go(mm(bank[:, b, :], a(w_at + c * cols + j * P, P), a(src + c * N + h * HALF, HALF), c, k))
            free[b] = evac(dst + j * N + h * HALF, b, s)

        def copied(to, b, s):
            AC.need(s)
            return AC.go(act.activation(a(to, HALF), bank[:, b, :], ACT.Copy))

        def relu_squared(to, b, s):
            AC.need(s)
            s = AC.go(act.activation(a(to, HALF), bank[:, b, :], ACT.Relu))
            V.need(s)
            return V.go(v.tensor_tensor(a(to, HALF), a(to, HALF), bank[:, b, :], ALU.mult))

        for j in range(LAT1 // P):
            for h in range(2):
                product(LT, FC1, LAT1, j, XT, DC, h, copied)
        lt_done = AC.last()
        for j in range(INT1 // P):
            for h in range(2):
                product(HT, UP, INT1, j, XT, DC, h, relu_squared)
        PE.need(lt_done)
        for j in range(LAT1 // P):
            for h in range(2):
                product(LE, EX1, LAT1, j, LT, LAT1 // P, h, copied)
        PE.need(V.last(), AC.last())
        free = [None] * 8
        for t in range(NT):
            b, y = 2 * (t % 4), a(XN1 + t * D, D)
            PE.need(free[b])
            for k in range(LAT1 // P):
                s = PE.go(mm(bank[:, b + 1, :], a(LE + k * N + t * P, P), a(FC2 + k * D, D), k, LAT1 // P))
            for k in range(INT1 // P):
                s = PE.go(mm(bank[:, b, :], a(HT + k * N + t * P, P), a(DOWN + k * D, D), k, INT1 // P))
            AC.need(s)
            s = AC.go(act.activation(y, bank[:, b, :], ACT.Copy))
            V.need(s, rw)
            free[b] = s = V.go(v.scalar_tensor_tensor(y, bank[:, b + 1, :], a(RW + t, 1), y, ALU.mult, ALU.add))
            s = normalise(y, y, t, s)
            G.need(s)
            s = G.go(g.tensor_tensor(y, y, a(LN1, D), ALU.mult))
            V.need(s)
            V.go(v.tensor_tensor(a(X + t * D, D), y, a(X + t * D, D), ALU.add))
        boundary()

        QT, AT = R + 19456, R + 23552
        SC, VN = R + 27648, R + 29696
        PT, COS, SIN = R + 5120, R + 7168, R + 8192
        MK, MNEG, KT = R + 9216, R + 10240, R + 11264
        WT2, CENT2 = R + 12288, C + 2048
        ROT, QC = C, C + 1024
        scale2 = D2 ** -0.5
        w2_in = load("weight2_in", WT2, dram["ffn2"][:, 0:DC * D])
        rope_in = load("rope_in", QT, dram["rope"])
        sem_i = Line(nc.sync, sem("int_in"), 16)
        sem_i.go(nc.sync.dma_start(a(SC, N).bitcast(I32), dram["pos"]))
        sem_m = Line(nc.sync, sem("mask_in"), 16)
        sem_m.go(nc.sync.dma_start(a(MK, N).bitcast(I32), dram["mask"]))
        norms, xt_done = norm_all(C)
        V.need(sem_m.last(), sem_i.last())
        s = V.go(v.tensor_scalar(a(MNEG, N), a(MK, N).bitcast(I32), 0.0, None, ALU.is_equal))
        V.need(s)
        V.need(V.go(v.tensor_scalar(a(MK, N), a(MNEG, N), -1.0, 1.0, ALU.mult, ALU.add)))
        V.go(v.tensor_scalar(a(MNEG, N), a(MNEG, N), NEG / scale2, None, ALU.mult))
        V.go(v.tensor_copy(a(SC, N), a(SC, N).bitcast(I32)))
        V.need(V.last())
        V.need(V.go(v.tensor_scalar(a(VN, N), a(SC, N), 0.0, float(MAXPOS), ALU.is_lt, ALU.mult)))
        V.need(V.go(v.tensor_tensor(a(SC, N), a(SC, N), a(VN, N), ALU.add)))
        V.need(V.go(v.tensor_scalar(a(SC, N), a(SC, N), 0.0, float(MAXPOS - 1), ALU.max, ALU.min)))
        for c in range(MAXPOS // P):
            V.go(v.tensor_scalar(a(AT + c * N, N), a(SC, N), const("posid")[:, c:c + 1], None, ALU.is_equal))
        PE.need(V.last(), rope_in)
        for j, to in ((0, COS), (1, SIN)):
            for h in range(2):
                b = 2 * j + h
                for c in range(MAXPOS // P):
                    s = PE.go(mm(bank[:, 4 + b, :], a(QT + c * 2 * D2 + j * D2, D2), a(AT + c * N + h * HALF, HALF),
                                 c, MAXPOS // P))
                AC.need(s)
                AC.go(act.activation(a(to + h * HALF, HALF), bank[:, 4 + b, :], ACT.Copy))
        boundary()
        cent_in = load("cent_in", CENT2, dram["ffn2"][:, DC * D:])

        NB = 4

        def group(w, arrived, free, tfree, rot_free):
            WQ, WK = w, w + DC * QH2 * D2
            WV, WO = WK + DC * D2, WK + 2 * DC * D2
            n = r = 0
            PE.need(arrived)

            def take():
                nonlocal n
                n += 1
                PE.need(*free[(n - 1) % NB])
                return (n - 1) % NB

            def rotary(b, s, to, h):
                nonlocal r
                rot, qc = a(ROT + r % 2 * HALF, HALF), a(QC + r % 2 * HALF, HALF)
                AC.need(s, rot_free[r % 2])
                AC.go(act.activation(rot[0:64, :], bank[64:P, b, :], ACT.Copy))
                s1 = AC.go(act.activation(rot[64:P, :], bank[0:64, b, :], ACT.Copy))
                V.need(s1)
                s2 = V.go(v.tensor_tensor(qc, bank[:, b, :], a(COS + h * HALF, HALF), ALU.mult))
                G.need(s1)
                s3 = G.go(g.tensor_tensor(rot, rot, a(SIN + h * HALF, HALF), ALU.mult))
                V.need(s3, s2)
                if len(to.shape) == 3:
                    qc, rot = (x.rearrange("p (b s) -> p b s", b=8) for x in (qc, rot))
                rot_free[r % 2] = s = V.go(v.tensor_tensor(to, qc, rot, ALU.add))
                free[b] = (s2,)
                r += 1
                return s

            def project(h):
                b = take()
                for c in range(DC):
                    s = PE.go(mm(bank[:, b, :], a(WK + c * D2, D2), a(XCT + c * N + h * HALF, HALF), c, DC))
                s = rotary(b, s, a(KT + h * HALF, HALF), h)
                for q in range(QH2):
                    b = take()
                    for c in range(DC):
                        s = PE.go(mm(bank[:, b, :], a(WQ + c * QH2 * D2 + q * D2, D2), a(XT + c * N + h * HALF, HALF),
                                     c, DC))
                    s = rotary(b, s, a(QT + h * QH2 * HALF, QH2 * HALF, 8, QH2, S)[:, :, q, :], h)
                b = take()
                for t in range(4):
                    for c in range(DC):
                        m = PE.go(mm(bank[:, b, t * P:(t + 1) * P], a(XCT + c * N + (4 * h + t) * P, P),
                                     a(WV + c * D2, D2), c, DC))
                AC.need(m)
                m = AC.go(act.activation(a(VN + h * HALF, HALF), bank[:, b, :], ACT.Copy))
                free[b] = (m,)
                return s, m

            def scores(h, ready, after):
                PE.need(ready, after)
                for bb in range(8):
                    for hp in range(2):
                        at = (bb // 2 * 4 + hp * 2 + bb % 2) * 64
                        s = PE.go(mm(bank[:, 4 + at // 512, at % 512:at % 512 + 64],
                                     a(QT + ((8 * h + bb) * QH2 + 2 * hp) * S, 2 * S),
                                     a(KT + (8 * h + bb) * S, S)))
                sc = SC + h * 1024
                mk, mn = (a(at + h * HALF, HALF, 4, P).unsqueeze(2).broadcast_to([P, 4, 2, P]) for at in (MK, MNEG))
                s4 = a(sc, 1024).rearrange("p (b h k) -> p b h k", b=4, h=2)
                V.need(s)
                s = read = V.go(v.tensor_tensor(s4, bank[:, 4:6, :].rearrange("p a (b h k) -> p (a b) h k", b=2, h=2),
                                                mk, ALU.mult))
                G.need(s)
                s = G.go(g.tensor_tensor(s4, s4, mn, ALU.add))
                rows = a(sc, 1024, 16, 64)
                top, tot = SOFT + 32 * h, SOFT + 32 * h + 16

                def wide(at):
                    return a(at, 16).unsqueeze(2).broadcast_to([P, 16, 64])

                V.need(s)
                V.need(V.go(v.tensor_reduce(a(top, 16), rows, axis=AX, op=ALU.max)))
                s = V.go(v.tensor_tensor(rows, rows, wide(top), ALU.subtract))
                AC.need(s)
                s = AC.go(act.activation(rows, rows, ACT.Exp, scale=scale2))
                V.need(s)
                V.need(V.go(v.tensor_reduce(a(tot, 16), rows, axis=AX, op=ALU.add)))
                s = V.go(v.reciprocal(a(tot, 16), a(tot, 16)))
                G.need(s)
                return G.go(g.tensor_tensor(rows, rows, wide(tot), ALU.mult)), read

            def attend(h, att, v_ready):
                for k in range(2):
                    PE.need(att, tfree[k])
                    for j in range(4):
                        s = PE.go(pe.transpose(bank[:, 6 + k, j * P:(j + 1) * P],
                                               a(SC + h * 1024 + (4 * k + j) * P, P), const("ident")))
                    AC.need(s)
                    tfree[k] = AC.go(act.activation(a(PT + h * 1024 + k * 512, 512), bank[:, 6 + k, :], ACT.Copy))
                PE.need(v_ready, *tfree)
                for k in range(2):
                    pair = (take(), take())
                    for bp in (2 * k, 2 * k + 1):
                        for b2, b in enumerate(pair):
                            rows = slice(b2 * 64, b2 * 64 + 64)
                            s = PE.go(mm(bank[:, b, (bp % 2) * 256:(bp % 2 + 1) * 256],
                                         a(VN + (4 * h + bp) * P, P)[rows, :],
                                         a(PT + h * 1024 + bp * 256, 256)[rows, :]))
                    AC.need(s)
                    cols = slice((4 * h + 2 * k) * P, (4 * h + 2 * k + 2) * P)
                    for b2, b in enumerate(pair):
                        to = a(AT, QH2 * N, QH2, N)[:, :, cols].rearrange("p h (b c q) -> p b h c q", b=2, c=2)
                        s = AC.go(act.activation(to[:, :, :, b2, :],
                                                 bank[:, b, :].rearrange("p (b h q) -> p b h q", b=2, h=QH2), ACT.Copy))
                        free[b] = (s,)
                PE.need(s)
                for t in range(4):
                    b = take()
                    for q in range(QH2):
                        s = PE.go(mm(bank[:, b, :], a(AT + q * N + (4 * h + t) * P, P), a(WO + q * D, D), q, QH2))
                    x = a(X + (4 * h + t) * D, D)
                    V.need(s)
                    free[b] = (V.go(v.tensor_tensor(x, bank[:, b, :], x, ALU.add)),)
                return s

            k0, v0 = project(0)
            att0, read = scores(0, k0, None)
            k1, v1 = project(1)
            att1, _ = scores(1, k1, read)
            attend(0, att0, v0)
            return attend(1, att1, v1)

        XCT = CT
        SOFT = SMALL + 700
        before = {ln: ln.n for ln in engines}
        per = PER2
        with Turns(G2 // 2, {PE: 2 * per[0], V: 2 * per[1], G: 2 * per[2], AC: 2 * per[3], a2_line[0]: 16,
                             a2_line[1]: 16}) as i:
            free, tfree, rot_free = [()] * NB, [None, None], [None, None]
            SP.need(PE.last())
            a2 = dram["attn2"]
            in1 = a2_line[1].go(nc.sync.dma_start(a(slot[1], WG), a2[bass.ds(2 * i + 1, 1)].rearrange("a p n -> (a p) n")))
            after = nc.sync.snap((2 * i + 2) % G2, min_val=0, max_val=G2 - 1)
            done0 = group(slot[0], Step(a2_line[0], a2_line[0].n, i, 16), free, tfree, rot_free)
            SP.need(done0)
            nxt = a2[bass.ds(after, 1)]
            a2_line[0].go(nc.sync.dma_start(a(slot[0], WG), nxt.rearrange("a p n -> (a p) n")))
            group(slot[1], in1, free, tfree, rot_free)
            PE.need(V.last(), AC.last(), G.last())
        SP.need(a2_line[0].last())
        boundary()

        W3, WO3, SM3 = R, R + 9248, R + 8192
        XN2 = R + 19456
        DT, ASG, AHOT, RSEL, ONES, YD, QSEL = (R + 14336 + 512 * j for j in range(7))
        w3_in = load("attn3_in", W3, dram["attn3"])
        wo3_in = load("wo3_in", WO3, dram["wo3"])
        sm3_in = load("small3_in", SM3, dram["small3"])
        asg_line = Line(nc.sync, sem("assign_in"), 16)
        asg_in = asg_line.go(nc.sync.dma_start(a(ASG, D).bitcast(I32), dram["assign"]))
        norms, xt_done = norm_all(XN2)
        V.need(asg_in)
        V.go(v.memset(a(ONES, P), 1.0))
        V.need(V.go(v.tensor_copy(a(ASG, D), a(ASG, D).bitcast(I32))))
        V.need(V.go(v.tensor_scalar(a(AHOT, D), a(ASG, D), 0.0, float(NCL), ALU.is_lt, ALU.mult)))
        V.need(V.go(v.tensor_tensor(a(ASG, D), a(ASG, D), a(AHOT, D), ALU.add)))
        V.need(V.go(v.tensor_scalar(a(ASG, D), a(ASG, D), 0.0, float(NCL - 1), ALU.max, ALU.min)))
        ahot = V.go(v.tensor_scalar(a(AHOT, D), a(ASG, D), const("posid")[:, 0:1], None, ALU.is_equal))
        PE.need(xt_done, cent_in, w2_in)
        for t in range(NT):
            for c in range(DC):
                s = PE.go(mm(bank[:, 7, t * NCL:(t + 1) * NCL], a(XT + c * N + t * P, P), a(CENT2 + c * NCL, NCL),
                             c, DC))
        dt, top8 = a(DT, 512, NT, NCL), a(QSEL, NT)
        wide8 = top8.unsqueeze(2).broadcast_to([P, NT, NCL])
        b7 = bank[:, 7, :].rearrange("p (t n) -> p t n", t=NT)
        V.need(s)
        V.need(V.go(v.tensor_reduce(top8, b7, axis=AX, op=ALU.max)))
        s = V.go(v.tensor_tensor(dt, b7, wide8, ALU.subtract))
        AC.need(s)
        s = AC.go(act.activation(dt, dt, ACT.Exp, scale=10.0))
        V.need(s)
        V.need(V.go(v.tensor_reduce(top8, dt, axis=AX, op=ALU.add)))
        V.need(V.go(v.reciprocal(top8, top8)))
        V.need(V.go(v.tensor_tensor(dt, dt, wide8, ALU.mult)))
        hit = V.go(v.tensor_scalar(dt, dt, 0.01, None, ALU.is_gt))
        V.need(hit)
        qsel = V.go(v.tensor_reduce(top8, dt, axis=AX, op=ALU.max))
        PE.need(hit)
        for t in range(NT):
            s = PE.go(mm(bank[0:NCL, 6, 0:1], a(DT + t * NCL, NCL), a(ONES, 1), t, NT))
        V.need(s)
        s = V.go(v.tensor_scalar(a(QSEL + 16, 1)[0:NCL, :], bank[0:NCL, 6, 0:1], 0.0, None, ALU.is_gt))
        V.need(s)
        s = V.go(v.tensor_scalar(a(QSEL + 32, P)[0:NCL, :], a(ONES, P)[0:NCL, :], a(QSEL + 16, 1)[0:NCL, :], None,
                                 ALU.mult))
        PE.need(s, ahot)
        s = PE.go(mm(bank[:, 5, :], a(QSEL + 32, P)[0:NCL, :], a(AHOT, D)[0:NCL, :]))
        AC.need(s)
        rsel = AC.go(act.activation(a(RSEL, D), bank[:, 5, :], ACT.Copy))
        free = [None] * 4
        yfree = [None, None]
        YS = [YD, QSEL + 256]
        for t in range(NT):
            b, y = t % 4, a(YS[t % 2], D)
            PE.need(free[b])
            for c in range(DC):
                s = PE.go(mm(bank[:, b, :], a(XT + c * N + t * P, P), a(WT2 + c * D, D), c, DC))
            V.need(s)
            s = free[b] = V.go(v.tensor_tensor(y, bank[:, b, :], a(CENT2 + DC * NCL, D), ALU.add))
            G.need(s, rsel)
            s = G.go(g.tensor_tensor(y, y, a(RSEL, D), ALU.mult))
            V.need(s, qsel)
            x = a(X + t * D, D)
            V.go(v.scalar_tensor_tensor(x, y, a(QSEL + t, 1), x, ALU.mult, ALU.add))
        FW, MIX, SI, BQK, BVB, BVS = R + 24576, R + 11296, R + 8736, R + 8760, R + 6144, R + 6656
        V.need(sm3_in)
        V.need(V.go(v.tensor_scalar(a(SI, 16), a(SM3 + 12, 16), 0.1, a(SM3 + 28, 1), ALU.mult, ALU.mult)))
        for T in range(DC):
            mix = a(MIX + T * P, P)
            s = V.go(v.tensor_tensor(mix.rearrange("p (a b) -> p a b", b=M3),
                                     const("block4").rearrange("p (a b) -> p a b", b=M3),
                                     a(SI + 4 * T, M3).unsqueeze(1).broadcast_to([P, P // M3, M3]), ALU.mult))
            V.need(s)
            V.go(v.tensor_tensor(mix, mix, const("ident"), ALU.add))
            V.go(v.tensor_scalar(a(BVB + T * P, P), a(ONES, P), a(SM3 + 8 + T, 1), None, ALU.mult))
        PE.need(V.last(), w3_in)
        free = [V.last()] * 8
        n = 0
        for w in range(3):
            for c in range(DC):
                PE.need(free[n % 4])
                for T in range(DC):
                    s = PE.go(mm(bank[:, n % 4, T * P:(T + 1) * P], a(W3 + w * 2048 + T * D + c * P, P),
                                 a(MIX + T * P, P)))
                AC.need(s)
                free[n % 4] = AC.go(act.activation(a(FW + w * 2048 + c * D, D), bank[:, n % 4, :], ACT.Copy))
                n += 1
        for j in range(8):
            s = PE.go(mm(bank[:, 6, j:j + 1], a(MIX + j % DC * P, P), a(SM3 + j, 1)))
        for T in range(DC):
            s = PE.go(mm(bank[:, 7, T * P:(T + 1) * P], a(BVB + T * P, P), a(MIX + T * P, P)))
        AC.need(s)
        AC.go(act.activation(a(BQK, 8), bank[:, 6, 0:8], ACT.Copy))
        AC.go(act.activation(a(BVS, D), bank[:, 7, :], ACT.Copy))
        boundary()

        QT3, KT3, VN3, OT = R + 12288, R + 16384, C, R + 20480
        XN3 = R + 20480
        VX, PT3, QX, PR = R + 24576, R + 26624, R + 28672, CT
        VD = XT
        W1 = R
        scale3 = 8 ** -0.5
        free = [None] * 8
        n = 0

        def feature_rows(w, src, dst):
            nonlocal n
            for T in range(DC):
                for h in range(2):
                    b = n % 8
                    n += 1
                    PE.need(free[b])
                    for c in range(DC):
                        s = PE.go(mm(bank[:, b, :], a(FW + w * 2048 + c * D + T * P, P), a(src + c * N + h * HALF, HALF),
                                     c, DC))
                    AC.need(s)
                    free[b] = AC.go(act.activation(a(dst + T * N + h * HALF, HALF), bank[:, b, :], ACT.Identity,
                                                   bias=a(BQK + 4 * w + T, 1)))

        norm3 = norms_of(XN3)
        feature_rows(1, CT, KT3)
        for t in range(NT):
            b = n % 8
            n += 1
            PE.need(free[b])
            for c in range(DC):
                s = PE.go(mm(bank[:, b, :], a(CT + c * N + t * P, P), a(FW + 4096 + c * D, D), c, DC))
            V.need(s)
            free[b] = V.go(v.tensor_tensor(a(VN3 + t * D, D), bank[:, b, :], a(BVS, D), ALU.add))
        vn_done = V.last()
        for t in range(NT):
            b = n % 8
            n += 1
            free[b] = transposed(a(XN3 + t * D, D), XT, t, b, free[b], norm3[t])
            G.need(norm3[t])
            G.go(g.tensor_tensor(a(X + t * D, D), a(X + t * D, D), a(SM3 + 29, D), ALU.add))
        PE.need(AC.last())
        feature_rows(0, XT, QT3)
        boundary()
        w1_in = load("w1_in", W1, dram["w1"])
        vd_line = Line(nc.sync, sem("v_copies"), 16)
        UN = 8

        def copy_v(T):
            for rep in range(2):
                for b2 in range(2):
                    dst = a(VD, 16 * P, NT, 2, P)[rep * S:(rep + 1) * S, :, b2, :]
                    src = A[b2 * S:(b2 + 1) * S, VN3:VN3 + NT * D].rearrange("p (t f) -> p t f", t=NT)
                    s = vd_line.go(nc.sync.dma_start(dst, src[:, :, bass.ds(T * P, P)]))
            return s

        def v_masked(q, vd_in, *after):
            G.need(vd_in, *after)
            return G.go(g.tensor_tensor(a(VX + q * D, D).rearrange("p (f m) -> p f m", m=M3),
                                        a(VD + q * D, D).rearrange("p (f m) -> p f m", m=M3),
                                        const("m_half").unsqueeze(1).broadcast_to([P, P, M3]), ALU.mult))

        class Unit:

            def __init__(self, u):
                self.u = u
                self.pr = PR + u % 4 * 1024
                self.qx, self.kx = QX + u % 2 * 1024, QX + u % 2 * 1024 + 512
                self.top, self.tot = SOFT + u % 2 * 16, SOFT + 32 + u % 2 * 16

            def wide(self, at):
                return a(at, 16).unsqueeze(2).broadcast_to([P, 16, S])

            def prepare(self, T, *after):
                AC.need(*after)
                G.need(*after)
                q, k = (A[:, bass.ds(at + T * N + self.u * P, P)].rearrange("p (b r) -> p b r", b=2)
                        for at in (QT3, KT3))
                for m in range(M3):
                    self.qx_done = AC.go(act.activation(a(self.qx, 512, 2, M3, S)[:, :, m, :], q, ACT.Copy,
                                                        scale=const("is_m")[:, m:m + 1]))
                self.kx_done = G.go(g.tensor_tensor(
                    a(self.kx, 512, 2, 4, S), k.unsqueeze(2).broadcast_to([P, 2, 4, S]),
                    const("is_h").unsqueeze(1).unsqueeze(3).broadcast_to([P, 2, 4, S]), ALU.mult))

            def score(self, *after):
                b = self.u % 2 * 2
                PE.need(*after)
                for b2 in range(2):
                    for mp in range(2):
                        to = bank[:, b + b2, :].rearrange("p (h m k) -> p h m k", h=4, m=2)[:, :, mp, :]
                        s = PE.go(mm(to, a(self.qx + (b2 * 4 + 2 * mp) * S, P), a(self.kx + b2 * 256, 256, 4, S)))
                self.scored = s
                scores = bank[:, b:b + 2, :].rearrange("p h (g k) -> p (h g) k", k=S)
                pr = a(self.pr, 1024, 16, S)
                V.need(s)
                V.need(V.go(v.tensor_reduce(a(self.top, 16), scores, axis=AX, op=ALU.max)))
                s = self.read = V.go(v.tensor_tensor(pr, scores, self.wide(self.top), ALU.subtract))
                AC.need(s)
                self.exp = AC.go(act.activation(pr, pr, ACT.Exp, scale=scale3))

            def divide(self, before):
                pr = a(self.pr, 1024, 16, S)
                V.need(self.exp, before)
                V.need(V.go(v.tensor_reduce(a(self.tot, 16), pr, axis=AX, op=ALU.add)))
                s = V.go(v.reciprocal(a(self.tot, 16), a(self.tot, 16)))
                G.need(s)
                self.done = G.go(g.tensor_tensor(pr, pr, self.wide(self.tot), ALU.mult))

            def turn(self, evac):
                for k in range(2):
                    PE.need(self.done, evac)
                    for h in range(4):
                        s = PE.go(pe.transpose(bank[:, 4 + k, h * P:(h + 1) * P],
                                               a(self.pr + (k * 4 + h) * P, P), const("ident")))
                    AC.need(s)
                    self.copied = AC.go(act.activation(a(PT3 + self.u % 2 * 1024 + k * 512, 512),
                                                       bank[:, 4 + k, :], ACT.Copy))

            def times_v(self, *after):
                PE.need(self.copied, *after)
                for b2 in range(2):
                    for h in range(4):
                        s = PE.go(mm(bank[32 * h:32 * h + 32, 6 + self.u % 2, b2 * P:(b2 + 1) * P],
                                     a(VX + (2 * self.u + b2) * P + 32 * h, 32),
                                     a(PT3 + self.u % 2 * 1024 + (b2 * 4 + h) * P, P)))
                return s

            def keep(self, T, s):
                o2 = bank[:, 6 + self.u % 2, 0:256].rearrange("p (b m r) -> p b m r", b=2, m=2)
                to = A[:, bass.ds(OT + T * N + self.u * P, P)].rearrange("p (b r) -> p b r", b=2)
                odd = const("is_odd")
                V.need(s)
                V.need(V.go(v.tensor_scalar(to, o2[:, :, 0, :], odd[:, 0:1], None, ALU.mult)))
                self.kept = V.go(v.scalar_tensor_tensor(to, o2[:, :, 1, :], odd[:, 1:2], to, ALU.mult, ALU.add))

        vd_in = copy_v(0)
        first = [Unit(0), Unit(1), Unit(2)]
        first[0].prepare(0)
        first[1].prepare(0)
        for q in range(3):
            v_masked(q, vd_in)
        first[0].score(first[0].qx_done, first[0].kx_done)
        first[0].divide(None)
        first[2].prepare(0, first[0].scored)
        first[1].score(first[1].qx_done, first[1].kx_done)
        v_masked(3, vd_in)
        with Turns(DC, {PE: 20 * UN, V: 6 * UN, G: 2 * UN + 4, AC: 7 * UN, vd_line: 64}) as T:
            nxt = (T + 1) % DC
            SP.need(G.last())
            vd_in = copy_v(nxt)
            v_start, ac_start, g_start = V.last(), AC.last(), G.last()
            units = dict(enumerate(first))
            units[0].done, units[1].exp = G.at(G.n - 2), ac_start
            units[2].qx_done, units[2].kx_done = ac_start, G.at(G.n - 1)
            vx = [G.at(G.n - 2)] * 3 + [g_start]
            for u in range(UN):
                w = u + 2
                units[u].turn(units[u - 1].copied if u else ac_start)
                units[u + 1].divide(units[u - 1].done if u else g_start)
                units[w + 1] = Unit((w + 1) % UN)
                units[w + 1].prepare(T if w + 1 < UN else nxt, units[u + 1].scored if u else PE.last())
                units[w].score(units[w].qx_done, units[w].kx_done, units[u].read if u > 1 else v_start)
                s = units[u].times_v(vx[u // 2], units[u - 2].kept if u > 1 else None)
                units[u].keep(T, s)
                if u % 2:
                    v_masked(u // 2, vd_in, s)
        PE.need(V.last(), wo3_in)
        G.need(G.last())
        V.need(G.last())
        free = [None] * 4
        for t in range(NT):
            b = t % 4
            PE.need(free[b])
            for c in range(DC):
                s = PE.go(mm(bank[:, b, :], a(OT + c * N + t * P, P), a(WO3 + c * D, D), c, DC))
            V.need(s)
            x = a(X + t * D, D)
            free[b] = V.go(v.tensor_tensor(x, bank[:, b, :], x, ALU.add))
        boundary()

        C1, C2, W2, LOW = R + 7168, R + 9248, R + 12288, R + 19456
        RING = 3
        EQ, HS, HTS, TOPS = R + 20480, R + 20480 + RING * D, R + 20480 + 2 * RING * D, R + 20480 + 3 * RING * D
        c1_in = load("c1_in", C1, dram["c1"])
        c2_in = load("c2_in", C2, dram["c2"], part=RANK)
        w2_in = load("w2_in", W2, dram["w2"])
        norms, xt_done = norm_all(C)
        PE.need(xt_done, c1_in)
        for h in range(2):
            for c in range(DC):
                s = PE.go(mm(bank[0:RANK, 2 + h, :], a(C1 + c * RANK, RANK), a(XT + c * N + h * HALF, HALF), c, DC))
            AC.need(s)
            s = AC.go(act.activation(a(LOW + h * HALF, HALF)[0:RANK, :], bank[0:RANK, 2 + h, :], ACT.Copy))
        PE.need(s, c2_in, w1_in, w2_in)
        units = [(t, j) for t in range(NT) for j in range(4)]
        inter_read, h_read, hs_done, picked, turned, hts, outed = {}, {}, {}, {}, {}, {}, {}
        eq_done = {}
        stored = sem("stored")
        for u in range(len(units) + 2):
            if u < len(units):
                t, j = units[u]
                wd = min(D, INTER - j * D)
                nb = wd // BLK
                bi, bh, ring = u % 2, 2 + u % 2, u % RING
                eq = a(EQ + ring * D, wd)
                blocks = eq.rearrange("p (n k) -> p n k", k=BLK)
                tops = a(TOPS + ring * 32, nb)
                PE.need(inter_read.get(u - 2))
                s1 = PE.go(mm(bank[:, bi, 0:wd], a(LOW + t * P, P)[0:RANK, :], a(C2 + j * D, wd)[0:RANK, :]))
                PE.need(h_read.get(u - 2))
                for c in range(DC):
                    s2 = PE.go(mm(bank[:, bh, 0:wd], a(XT + c * N + t * P, P), a(W1 + c * INTER + j * D, wd), c, DC))
                hs_done[u] = s2
                inter = bank[:, bi, 0:wd].rearrange("p (n k) -> p n k", k=BLK)
                V.need(s1)
                V.need(V.go(v.tensor_reduce(tops, inter, axis=AX, op=ALU.max)))
                s = inter_read[u] = V.go(v.tensor_tensor(blocks, inter, tops.unsqueeze(2).broadcast_to([P, nb, BLK]),
                                                         ALU.is_equal))
                G.need(s)
                eq_done[u] = G.go(g.tensor_tensor(blocks, blocks, const("down32").unsqueeze(1)
                                                  .broadcast_to([P, nb, BLK]), ALU.mult))
            if 0 <= u - 1 < len(units):
                w = u - 1
                t, j = units[w]
                wd = min(D, INTER - j * D)
                nb = wd // BLK
                ring = w % RING
                eq = a(EQ + ring * D, wd)
                blocks = eq.rearrange("p (n k) -> p n k", k=BLK)
                tops = a(TOPS + ring * 32, nb)
                V.need(eq_done[w])
                V.need(V.go(v.tensor_reduce(tops, blocks, axis=AX, op=ALU.max)))
                s = V.go(v.tensor_tensor(blocks, blocks, tops.unsqueeze(2).broadcast_to([P, nb, BLK]), ALU.is_equal))
                V.need(s, hs_done[w], turned.get(w - RING))
                h_read[w] = V.go(v.scalar_tensor_tensor(a(HS + ring * D, wd), bank[:, 2 + w % 2, 0:wd], 0.0, eq,
                                                        ALU.max, ALU.mult))
            if 0 <= u - 2 < len(units):
                w = u - 2
                t, j = units[w]
                wd = min(D, INTER - j * D)
                ring = w % RING
                b = 4 + w % 2
                PE.need(h_read[w], hts.get(w - 2))
                for k in range(wd // P):
                    s = PE.go(pe.transpose(bank[:, b, k * P:(k + 1) * P], a(HS + ring * D + k * P, P), const("ident")))
                turned[w] = s
                AC.need(s, outed.get(w - RING))
                hts[w] = s = AC.go(act.activation(a(HTS + ring * D, wd), bank[:, b, 0:wd], ACT.Copy))
                PE.need(s)
                ob = 6 + t % 2
                if j == 0:
                    PE.need(outed.get(("x", t - 2)))
                for k in range(wd // P):
                    f = j * 4 + k
                    s = PE.go(mm(bank[:, ob, :], a(HTS + ring * D + k * P, P), a(W2 + f * D, D), f, NI))
                outed[w] = s
                if j == 3:
                    x = a(X + t * D, D)
                    V.need(s)
                    s = outed[("x", t)] = V.go(v.tensor_tensor(x, bank[:, ob, :], x, ALU.add))
                    SP.need(s)
                    nc.sync.dma_start(out[t * P:(t + 1) * P, :], x).then_inc(stored, 16)
        nc.sync.wait_ge(stored, 16 * NT)


def kernel(**inputs):
    import concourse.bacc as _bacc
    from concourse.bass_utils import run_bass_kernel_spmd as _run

    nc = _bacc.Bacc("TRN2", target_bir_lowering=False, num_devices=1)
    arrays = lay_out(inputs)
    dram = {n: nc.dram_tensor(f"in_{n}", v.shape, mybir.dt.from_np(v.dtype), kind="ExternalInput").ap()
            for n, v in arrays.items()}
    out = nc.dram_tensor("out", (N, D), F32, kind="ExternalOutput").ap()
    program(nc, dram, out)
    r = _run(nc, [{f"in_{n}": v for n, v in arrays.items()}], core_ids=[0])
    return r.results[0]["out"].reshape(B, S, D)
```

```python
from contextlib import ExitStack

import numpy as np

import concourse.bass as bass
from concourse import mybir

F32 = mybir.dt.float32
F32R = mybir.dt.float32r
I32 = mybir.dt.int32
U32 = mybir.dt.uint32
ALU = mybir.AluOpType
ACT = mybir.ActivationFunctionType
AX = mybir.AxisListType.X

P = 128
B, S, D = 16, 64, 512
NT = B * S // P
DC = D // P
N = B * S
HALF = N // 2
EPS = 1e-5
NEG = -1e9

H0, WIN = 8, 16
HD0 = S // H0
PADL = WIN // 2
KW = D + WIN - 1
E0 = 8
INT1, LAT1 = 1024, 256
G2, QH2, D2 = 8, 4, 128
WG = DC * QH2 * D2 + 2 * DC * D2 + QH2 * D
MAXPOS = 512
NCL = 64
M3 = 4
INTER, BLK, RANK = 1792, 32, 16
NI = INTER // P


class Step:

    def __init__(self, line, n, turn=None, per=0):
        self.line, self.n, self.turn, self.per = line, n, turn, per

    def value(self):
        return self.n if self.turn is None or not self.per else self.turn * self.per + self.n

    def before(self):
        assert self.n > self.per
        return Step(self.line, self.n - self.per, self.turn, self.per)


class Line:

    def __init__(self, engine, sem, step=1):
        self.e, self.sem, self.step = engine, sem, step
        self.n, self.turn, self.per, self.known = 0, None, 0, {}

    def go(self, ins):
        ins.then_inc(self.sem, self.step)
        self.n += self.step
        return self.at(self.n)

    def at(self, n):
        return Step(self, n, self.turn, self.per)

    def last(self):
        return self.at(self.n)

    def need(self, *steps):
        for s in steps:
            if s is None or s.n == 0:
                continue
            key = (id(s.line), s.turn is not None and s.per > 0)
            if self.known.get(key, -1) >= s.n:
                continue
            self.known[key] = s.n
            self.e.wait_ge(s.line.sem, s.value())


def chunked(w):
    k, n = w.shape
    return np.ascontiguousarray(w.reshape(k // P, P, n).transpose(1, 0, 2).reshape(P, -1))


def constants():
    k = np.arange(P)
    parts = {
        "ident": np.eye(P),
        "selw": (np.arange(2 * P - 16)[None, :] == (P - 16 + k // S * H0 + k % S // HD0)[:, None]),
        "selt": np.concatenate([(k[:, None] == 16 * p + (k // S * H0 + k % S // HD0)[None, :])
                                for p in range(NT)], 1),
        "block8": np.kron(np.eye(P // 8), np.ones((8, 8))),
        "block4": np.kron(np.eye(P // 4), np.ones((4, 4))),
        "iota8": np.tile(np.arange(8), (P, 1)),
        "posid": k[:, None] + P * np.arange(MAXPOS // P)[None, :],
        "down32": np.tile(BLK - np.arange(BLK), (P, 1)),
        "is_m": k[:, None] % M3 == np.arange(M3)[None, :],
        "is_h": k[:, None] // 32 == np.arange(4)[None, :],
        "is_odd": k[:, None] % 2 == np.arange(2)[None, :],
        "m_half": np.arange(M3)[None, :] // 2 == (k // S)[:, None],
    }
    at, cols = {}, 0
    for name, a in parts.items():
        at[name] = (cols, cols + a.shape[1])
        cols += a.shape[1]
    return np.concatenate([a.astype(np.float32) for a in parts.values()], 1), at


def rope_tables():
    inv = (1.0 / 10000.0 ** (np.arange(0, D2, 2, dtype=np.float32) / np.float32(D2))).astype(np.float32)
    f = np.arange(MAXPOS, dtype=np.float32)[:, None] * inv[None, :]
    cos = np.concatenate([np.cos(f), np.cos(f)], 1)
    sin = np.concatenate([-np.sin(f), np.sin(f)], 1)
    return chunked(np.concatenate([cos, sin], 1).astype(np.float32))


def lay_out(i):
    f = {n: np.asarray(a) for n, a in i.items()}
    x, c = f["x"].reshape(N, D), f["ctx_4096"].reshape(N, D)

    def twice(w):
        z = np.zeros((P, P), w.dtype)
        z[:S, :S] = w.T
        z[S:, S:] = w.T
        return z

    def rows(v):
        return np.broadcast_to(v[None, :], (P, v.shape[0]))

    a = {"x": chunked(x), "c": chunked(c), "ct": chunked(c.T), "const": constants()[0]}
    a["w0"] = np.concatenate([twice(f[f"L0_xattn_{n}"]) for n in ("Wq", "Wk", "Wv", "Wo")]
                             + [np.tile(f[f"L0_xattn_{n}"], 2)[:, None] for n in ("bq", "bk", "bv", "bo")], 1)
    a["gate0"] = chunked(f["L0_ffn_gate_w"])
    a["expert0"] = np.concatenate([chunked(w) for w in f["L0_ffn_expert_w"]], 1)
    a["ffn1"] = np.concatenate([chunked(f[f"L1_ffn_{n}"]) for n in ("up_w", "fc1_w", "expert_w", "fc2_w", "down_w",
                                                                    "gate_w")], 1)
    a["ln1"] = np.concatenate([rows(f["L1_ffn_ln_gamma"]), rows(f["L1_ffn_ln_beta"])], 1)
    q, k, v, o = (f[f"L2_xattn_W{n}"] for n in "qkvo")
    w = QH2 * D2
    a["attn2"] = np.stack([np.concatenate([chunked(q[:, g * w:(g + 1) * w]), chunked(k[:, g * D2:(g + 1) * D2]),
                                           chunked(v[:, g * D2:(g + 1) * D2]), chunked(o[g * w:(g + 1) * w])], 1)
                           for g in range(G2)])
    a["pos"] = rows(f["pos_BxS2"].reshape(-1))
    m = f["mask_BxSxS2_ik0"].transpose(1, 0, 2).reshape(S, -1)
    a["mask"] = np.concatenate([m, m], 0)
    a["rope"] = rope_tables()
    a["ffn2"] = np.concatenate([chunked(f["L2_ffn_weight"].T), chunked(f["L2_ffn_centroids"].T),
                                rows(f["L2_ffn_bias"])], 1)
    a["assign"] = rows(f["L2_ffn_assignments"])
    a["attn3"] = np.concatenate([chunked(f[f"L3_xattn_W{n}"]) for n in "qkv"], 1)
    a["wo3"] = chunked(f["L3_xattn_Wo"].T)
    inter = f["L3_xattn_interference"].reshape(DC, 4, 1, M3, M3)
    inter = np.broadcast_to(inter, (DC, 4, P // 16, M3, M3)).reshape(DC, P, M3).transpose(1, 0, 2).reshape(P, -1)
    a["small3"] = np.concatenate([f[f"L3_xattn_b{n}"].reshape(DC, P).T for n in "qkv"]
                                 + [inter, rows(f["L3_xattn_amp"]), rows(f["L3_xattn_bo"])], 1)
    a["c1"] = chunked(f["L3_ffn_c1_w"].T)
    a["c2"] = f["L3_ffn_c2_w"].T
    a["w1"] = chunked(f["L3_ffn_w1"].T)
    a["w2"] = chunked(f["L3_ffn_w2t"])
    return {n: np.ascontiguousarray(v) for n, v in a.items()}


GROUP_MARKS = (592, 98, 26, 76)
X, XT, CT, C, CONST = 0, 4096, 8192, 12288, 16384
CONST_AT = constants()[1]
NCONST = max(b for _, b in CONST_AT.values())
SMALL = CONST + NCONST
R = SMALL + 1024


def program(nc, dram, out):
    with ExitStack() as ctx:
        A = ctx.enter_context(nc.sbuf_tensor("arena", [P, R], F32))
        stage_words = ctx.enter_context(ExitStack())
        region = {}

        def use(name, words, split=0):
            stage_words.close()
            assert R + words + split <= 53248
            region["f32"] = stage_words.enter_context(nc.sbuf_tensor(name, [P, words], F32))
            region["split"] = (stage_words.enter_context(nc.sbuf_tensor(f"{name}_split", [P, split], F32R))
                               if split else None)

        bank = ctx.enter_context(nc.psum_tensor("banks", [P, 8, 512], F32))

        def sem(name):
            return ctx.enter_context(nc.semaphore(name))

        PE, V, G, AC = (Line(e, sem(n)) for e, n in ((nc.tensor, "pe_steps"), (nc.vector, "vector_steps"),
                                                      (nc.gpsimd, "pool_steps"), (nc.scalar, "act_steps")))
        SP = Line(nc.sync, sem("sp_steps"))
        engines = (PE, V, G, AC)
        pe, v, g, act = nc.tensor, nc.vector, nc.gpsimd, nc.scalar

        def shaped(t, shape):
            names = "abc"[:len(shape)]
            if not names:
                return t
            return t.rearrange(f"p ({' '.join(names)}) -> p {' '.join(names)}", **dict(zip(names, shape)))

        def a(at, n, *shape, off=0):
            t = A[:, bass.ds(at + off, n)] if at < R else region["f32"][:, bass.ds(at - R + off, n)]
            return shaped(t, shape)

        def parts(at, part, lot, n, *shape):
            return shaped(region["split"][:, at[0] + part * lot + at[1]:at[0] + part * lot + at[1] + n], shape)

        def mm3(dst, lhsT, rhs, k, n):
            for x, (i, j) in enumerate(((0, 0), (0, 1), (1, 0))):
                s = PE.go(pe.matmul(dst, lhsT=lhsT(i), rhs=rhs(j), start=(k == 0 and x == 0),
                                    stop=(k == n - 1 and x == 2)))
            return s

        def split(hi, lo, src, *after, low=None):
            low = low or V
            AC.need(*after)
            s = AC.go(act.activation(hi, src, ACT.Copy))
            low.need(s)
            return low.go(low.e.tensor_tensor(lo, src, hi.bitcast(F32), ALU.subtract))

        def const(name):
            lo, hi = CONST_AT[name]
            return A[:, CONST + lo:CONST + hi]

        def load(name, to, src, *after, line=None, part=P):
            line = line or Line(nc.sync, sem(name), 16)
            SP.need(*after)
            return line.go(nc.sync.dma_start(a(to, src.shape[-1])[0:part, :], src))

        class Turns:

            def __init__(self, turns, per):
                self.turns, self.per = turns, per

            def __enter__(self):
                self.ctx = nc.Fori(0, self.turns)
                self.i = self.ctx.__enter__()
                self.base = {ln: ln.n for ln in self.per}
                for ln in self.per:
                    ln.turn, ln.per = self.i, self.per[ln]
                for ln in engines + (SP,):
                    ln.known = {key: n for key, n in ln.known.items() if not key[1]}
                return self.i

            def __exit__(self, *exc):
                if exc[0]:
                    return False
                moved = [ln.n - self.base[ln] for ln in self.per]
                assert all(ln.n - self.base[ln] == self.per[ln] for ln in self.per), moved
                self.ctx.__exit__(None, None, None)
                for ln in self.per:
                    ln.n = self.base[ln] + self.turns * self.per[ln]
                    ln.turn, ln.per = None, 0
                for ln in engines + (SP,):
                    ln.known = {}
                return False

        def boundary():
            for ln in engines + (SP,):
                ln.need(*(o.last() for o in engines))

        def mm(dst, lhsT, rhs, k=0, n=1, **kw):
            return pe.matmul(dst, lhsT=lhsT, rhs=rhs, start=(k == 0), stop=(k == n - 1), **kw)

        STAT, MEAN, RSTD = SMALL, SMALL + 48, SMALL + 64
        HALVES = SMALL + 72
        g_half = G.go(g.memset(a(HALVES, NT), -0.5))

        def moments(src, t):
            V.need(V.go(v.bn_stats(a(STAT + 6 * t, 6), src)))
            return V.go(v.bn_aggr(a(MEAN + 2 * t, 2), a(STAT + 6 * t, 6)))

        def root(t, n):
            V.need(V.last())
            var = a(MEAN + 2 * t, 2 * n, n, 2)[:, :, 1]
            s = V.go(v.tensor_scalar(a(RSTD + t, n), var, EPS, None, ALU.add))
            G.need(s, g_half)
            return G.go(g.tensor_tensor(a(RSTD + t, n), a(RSTD + t, n), a(HALVES, n), ALU.pow))

        def scaled(src, dst, t):
            return V.go(v.tensor_scalar(dst, src, a(MEAN + 2 * t, 1), a(RSTD + t, 1), ALU.subtract, ALU.mult))

        def normalise(src, dst, t, *after):
            V.need(*after)
            moments(src, t)
            V.need(root(t, 1))
            return scaled(src, dst, t)

        def turned_split(src, to, t, b, free, *after):
            PE.need(free, *after)
            for c in range(DC):
                s = PE.go(pe.transpose(bank[:, b, c * P:(c + 1) * P], src[:, c * P:(c + 1) * P], const("ident")))
            hi, lo = (parts(to, x, DC * N, DC * N, DC, N)[:, :, t * P:(t + 1) * P] for x in (0, 1))
            return split(hi, lo, bank[:, b, :].rearrange("p (c n) -> p c n", c=DC), s)

        roots = []

        def measured(t):
            V.need(V.last())
            moments(a(X + t * D, D), t)
            if t % 4 == 3:
                roots.append(root(t - 3, 4))

        def norms_of(xn, ready=()):
            V.need(*ready)
            if not roots:
                for t in range(NT):
                    measured(t)
            out = []
            for t in range(NT):
                V.need(roots[t // 4])
                out.append(scaled(a(X + t * D, D), a(xn + t * D, D), t))
            roots.clear()
            return out

        def transposed(src, dst, t, b, free, *after):
            PE.need(free, *after)
            for c in range(DC):
                s = PE.go(pe.transpose(bank[:, b, c * P:(c + 1) * P], src[:, c * P:(c + 1) * P], const("ident")))
            AC.need(s)
            return AC.go(act.activation(a(dst, DC * N, DC, N)[:, :, t * P:(t + 1) * P],
                                        bank[:, b, :].rearrange("p (c n) -> p c n", c=DC), ACT.Copy))

        def norm_all(xn, ready=(), with_t=True):
            free = [None] * 4
            ns = norms_of(xn, ready)
            if with_t:
                for t in range(NT):
                    free[t % 4] = transposed(a(xn + t * D, D), XT, t, t % 4, free[t % 4], ns[t])
            return ns, free[3]

        Q0, K0, V0 = XT, R, R + NT * KW
        TOP, PROD = V0 + NT * KW, CT
        DOTS = TOP + D
        ATT, SELT = (0, 0), (2 * WIN * D, 0)
        use("window", 2 * NT * KW + (1 + WIN) * D, 2 * WIN * D + 2 * P)
        W0 = SMALL + 96
        w0_in = load("w0_in", W0, dram["w0"])
        x_in = load("x_in", X, dram["x"])
        c_in = load("c_in", C, dram["c"])
        const_in = load("const_in", CONST, dram["const"])

        XN0 = XT
        scale0 = HD0 ** -0.5

        pads = []
        for at in (K0, V0):
            kv = a(at, NT * KW, NT, KW)
            pads.append(G.go(g.memset(kv[:, :, 0:PADL], 0.0)))
            pads.append(G.go(g.memset(kv[:, :, PADL + D:KW], 0.0)))
        norms, _ = norm_all(XN0, (x_in,), with_t=False)
        PE.need(w0_in, c_in)
        AC.need(w0_in)
        bias0 = a(W0 + 4 * P, 4)
        free = [None] * 8
        todo = [(j, t) for t in range(NT) for j in (1, 2)] + [(0, t) for t in range(NT)]
        for n, (j, t) in enumerate(todo):
            src, dst = ((XN0, Q0 + t * D), (C, K0 + t * KW + PADL), (C, V0 + t * KW + PADL))[j]
            PE.need(free[n % 8], norms[t] if j == 0 else None)
            s = PE.go(mm(bank[:, n % 8, :], a(W0 + j * P, P), a(src + t * D, D)))
            AC.need(s)
            free[n % 8] = AC.go(act.activation(a(dst, D), bank[:, n % 8, :], ACT.Identity, bias=bias0[:, j:j + 1]))
        qkv = AC.last()
        lo = CONST_AT["selw"][0] + CONST
        PE.need(const_in)
        PE.need(qkv)
        V.need(V.go(v.memset(a(TOP, D), -3e38)))
        with Turns(WIN // 2, {PE: 16, V: 12, G: 6, AC: 2}) as i:
            done, copied_at = [], AC.n
            for u in range(2):
                prods = []
                for t in range(NT):
                    ln = G if t in (1, 4, 6) else V
                    ln.need(qkv, pads[-1], done[t] if u else PE.at(PE.n + NT + t + 1).before())
                    prods.append(ln.go(ln.e.tensor_tensor(
                        a(PROD + t * D, D), a(Q0 + t * D, D),
                        a(K0 + t * KW + u, D, off=i * 2), ALU.mult)))
                PE.need(AC.at(AC.n + 1).before())
                new = []
                for t in range(NT):
                    PE.need(prods[t])
                    at = lo + P - 16 - 16 * (t % 2)
                    new.append(PE.go(mm(bank[t // 2 * 32:t // 2 * 32 + 32, u, :], A[:, at:at + 32],
                                        a(PROD + t * D, D), t % 2, 2)))
                done = new
                AC.need(new[-1])
                AC.go(act.activation(a(DOTS + u * D, D, off=i * 2 * D), bank[:, u, :], ACT.Copy))
                if u:
                    for k in (0, 1):
                        V.need(AC.at(copied_at + 1) if k else AC.at(copied_at + 2).before(), V.last())
                        V.go(v.tensor_tensor(a(TOP, D), a(TOP, D), a(DOTS + (k - 1) * D, D, off=i * 2 * D), ALU.max))
        SUM = PROD
        dots = a(DOTS, WIN * D, WIN, D)
        dots_hi, dots_lo = (parts(ATT, x, WIN * D, WIN * D, WIN, D) for x in (0, 1))
        cuts = [slice(c * P, (c + 1) * P) for c in range(4)]

        def over_w(at, cut):
            return a(at, D)[:, cut].unsqueeze(1).broadcast_to([P, WIN, P])

        def by_t(cut):
            return dots[:, :, cut].rearrange("p w t -> p t w")

        V.need(AC.last(), PE.last(), V.last())
        G.need(AC.last())
        top = V.go(v.tensor_tensor(a(TOP, D), a(TOP, D), a(DOTS + (WIN - 1) * D, D), ALU.max))
        exps = []
        for c, cut in enumerate(cuts):
            ln = V if c % 2 else G
            ln.need(top)
            s = ln.go(ln.e.tensor_tensor(dots[:, :, cut], dots[:, :, cut], over_w(TOP, cut), ALU.subtract))
            AC.need(s)
            exps.append(AC.go(act.activation(dots[:, :, cut], dots[:, :, cut], ACT.Exp, scale=scale0)))
        att_done = []
        order = [1, 0, 3, 2]
        for c in order:
            cut = cuts[c]
            V.need(exps[c])
            V.need(V.go(v.tensor_reduce(a(SUM, D)[:, cut], by_t(cut), axis=AX, op=ALU.add)))
            s = V.go(v.reciprocal(a(SUM, D)[:, cut], a(SUM, D)[:, cut]))
            ln = V if c == 1 or c == 2 else G
            ln.need(s)
            s = ln.go(ln.e.tensor_tensor(dots[:, :, cut], dots[:, :, cut], over_w(SUM, cut), ALU.mult))
            att_done.append((c, s))
        for c, s in att_done:
            s = split(dots_hi[:, :, cuts[c]], dots_lo[:, :, cuts[c]], dots[:, :, cuts[c]], s,
                      low=G if c == 2 else V)
            PE.need(s)
        AV, PAIRS = K0, 4
        V.need(AC.last())
        with Turns(NT // 2, {PE: 2 * (2 * WIN + WIN // 2), V: 2 * WIN + 2, G: WIN, AC: 2}) as i:
            PE0, V0n, G0 = PE.n, V.n, G.n
            avs, pairs, outs, adds = [], [], [], []
            out_at = [5 * k + 13 if k < WIN - 2 else 4 * WIN + k + 1 for k in range(WIN)]
            sel_at = (37, 77)
            add_at = (WIN + 5, 2 * WIN + 2)

            sels = []
            for u in range(2):
                AC.need(PE.at(PE0 + sel_at[u]).before())
                sel = A[:, bass.ds(CONST + CONST_AT["selt"][0] + u * P + i * 2 * P, P)]
                sels.append(AC.go(act.activation(parts(SELT, u, P, P), sel, ACT.Copy)))
            def to_out():
                k = len(outs)
                tile = k // (WIN // 2)
                PE.need(pairs[k])
                if k % (WIN // 2) == 0:
                    PE.need(V.at(V0n + add_at[tile]).before())
                outs.append(PE.go(mm(bank[:, 4 + tile, :], a(W0 + 3 * P, P), a(AV + 2 * (k % PAIRS) * D, D),
                                     k % (WIN // 2), WIN // 2)))
                if k % (WIN // 2) == WIN // 2 - 1:
                    V.need(outs[-1])
                    x = A[:, bass.ds(X + tile * D + i * 2 * D, D)]
                    adds.append(V.go(v.scalar_tensor_tensor(x, bank[:, 4 + tile, :], bias0[:, 3:4], x,
                                                            ALU.add, ALU.add)))
                    assert adds[-1].n == V0n + add_at[tile]

            for m in range(2 * WIN):
                tile, w = m // WIN, m % WIN
                PE.need(sels[tile], avs[m - 4] if m >= 4 else V.at(V0n + 2 * WIN + 2 - 4 + m).before())
                for x in (0, 1):
                    s = PE.go(pe.matmul(bank[:, m % 4, :], lhsT=parts(SELT, tile, P, P),
                                        rhs=parts(ATT, x, WIN * D, WIN * D)[:, w * D:(w + 1) * D],
                                        start=x == 0, stop=x == 1))
                assert w < WIN - 1 or s.n == PE0 + sel_at[tile]
                k = m // 2
                V.need(s, outs[k - PAIRS] if k >= PAIRS else PE.at(PE0 + out_at[k - PAIRS]).before())
                avs.append(V.go(v.tensor_tensor(a(AV + m % (2 * PAIRS) * D, D), bank[:, m % 4, :],
                                                a(V0 + tile * KW + w, D, off=i * 2 * KW), ALU.mult)))
                if m % 2:
                    at = AV + 2 * (k % PAIRS) * D
                    G.need(avs[-1])
                    pairs.append(G.go(g.tensor_tensor(a(at, D), a(at, D), a(at + D, D), ALU.add)))
                    if m >= 5:
                        to_out()
            to_out()
            to_out()
            assert [s.n - PE0 for s in outs] == out_at
        boundary()

        def logits(to, product):
            for h in range(2):
                for c in range(DC):
                    s = product(bank[0:E0, 4 + h, :], c, h)
                AC.need(s)
                AC.go(act.activation(a(to + h * HALF, HALF)[0:E0, :], bank[0:E0, 4 + h, :], ACT.Copy))
            PE.need(AC.last())
            for t in range(NT):
                s = PE.go(pe.transpose(bank[:, 7, t * E0:(t + 1) * E0], a(to + t * P, P)[0:E0, :],
                                       const("ident")[0:E0, 0:E0]))
            return s

        use("experts", 4096 + 2048 + 3 * 2048, 8192 + 2 * 4096)
        XN = R
        STAGED = R + 6144
        XTS, EXS = (0, 0), (8192, 0)
        WREP, WCOL = R + 4096, R + 4096 + 64
        GATE = R + 4096 + 128
        LOG = GATE + 32
        TOP8, IDX = LOG + 64, LOG + 128
        TMP = LOG + 192
        LOT = DC * D
        gate_in = load("gate_in", GATE, dram["gate0"])
        exp_line = [Line(nc.sync, sem(f"expert_in{j}"), 16) for j in range(3)]

        def fetch(e, *after):
            return load("", STAGED + e % 3 * LOT, dram["expert0"][:, e * LOT:(e + 1) * LOT], *after,
                        line=exp_line[e % 3])

        exp_in = [fetch(e) for e in range(3)]
        ct_in = load("ct_in", CT, dram["ct"])
        norms = norms_of(XN)
        free = [None] * 4
        for t in range(NT):
            free[t % 4] = turned_split(a(XN + t * D, D), XTS, t, t % 4, free[t % 4], norms[t])
            xt_done = free[t % 4]
        PE.need(xt_done, gate_in)
        GS = (8192 + 4096, 0)
        gate_done = split(parts(GS, 0, 32, 32), parts(GS, 1, 32, 32), a(GATE, 32), gate_in)

        def split_expert(e, after):
            hi, lo = (parts((EXS[0] + e % 2 * 2 * LOT, 0), x, LOT, LOT) for x in (0, 1))
            done = split(hi, lo, a(STAGED + e % 3 * LOT, LOT), exp_in[e], after, low=G)
            if e + 3 < E0:
                exp_in.append(fetch(e + 3, done))
            return done

        ready = split_expert(0, None)

        PE.need(gate_done)
        s = used = logits(XN, lambda to, c, h: mm3(
            to, lambda x: parts(GS, x, 32, 32)[:, c * E0:(c + 1) * E0],
            lambda x: parts(XTS, x, DC * N, DC * N)[:, c * N + h * HALF:c * N + (h + 1) * HALF], c, DC))
        V.need(s)
        V.need(V.go(v.tensor_copy(a(LOG, 64), bank[:, 7, 0:64])))
        for t in range(NT):
            V.go(v.max(a(TOP8 + 8 * t, 8), a(LOG + 8 * t, 8)))
        V.need(V.last())
        for t in range(NT):
            V.go(v.max_index(a(IDX + 8 * t, 8).bitcast(U32), a(TOP8 + 8 * t, 8), a(LOG + 8 * t, 8)))
        top = a(TOP8, 64, NT, 8)
        s = V.go(v.tensor_tensor(a(TMP, NT), top[:, :, 1], top[:, :, 0], ALU.subtract))
        AC.need(s)
        s = AC.go(act.activation(a(TMP, NT), a(TMP, NT), ACT.Exp))
        V.need(s)
        V.need(V.go(v.tensor_scalar(a(TMP + 8, NT), a(TMP, NT), 1.0, None, ALU.add)))
        V.need(V.go(v.reciprocal(a(TMP + 8, NT), a(TMP + 8, NT))))
        V.need(V.go(v.tensor_tensor(a(TMP, NT), a(TMP, NT), a(TMP + 8, NT), ALU.mult)))
        V.need(V.go(v.tensor_copy(a(TMP + 16, 64), a(IDX, 64).bitcast(U32))))
        idx = a(TMP + 16, 64, NT, 8)
        pick = [a(TMP + 80 + 64 * j, 64, E0, NT) for j in range(2)]
        for j, weight in ((0, TMP + 8), (1, TMP)):
            V.need(V.go(v.tensor_tensor(pick[j], const("iota8").unsqueeze(2).broadcast_to([P, E0, NT]),
                                        idx[:, :, j].unsqueeze(1).broadcast_to([P, E0, NT]), ALU.is_equal)))
            V.need(V.go(v.tensor_tensor(pick[j], pick[j], a(weight, NT).unsqueeze(1).broadcast_to([P, E0, NT]),
                                        ALU.mult)))
        V.need(V.go(v.tensor_tensor(a(WREP, 64, E0, NT), pick[0], pick[1], ALU.add)))
        V.need(V.last())
        free = [free[t % 4] if t < 4 else None for t in range(NT)]
        for e in range(E0):
            nxt = split_expert(e + 1, used) if e + 1 < E0 else None
            PE.need(ready)
            for t in range(NT):
                PE.need(free[t] if e else V.last() if t == 7 else None)
                for c in range(DC):
                    s = mm3(bank[:, t, :], lambda x: parts(XTS, x, DC * N, DC * N)[:, c * N + t * P:c * N + t * P + P],
                            lambda x: parts((EXS[0] + e % 2 * 2 * LOT, c * D), x, LOT, D), c, DC)
                V.need(s)
                x = a(X + t * D, D)
                free[t] = V.go(v.scalar_tensor_tensor(x, bank[:, t, :], a(WREP + e * NT + t, 1), x,
                                                      ALU.mult, ALU.add))
                if e == E0 - 1:
                    measured(t)
            ready, used = nxt, s
        boundary()

        use("linear", 30720)
        F1 = R + 14336
        f1_in = load("ffn1_in", F1, dram["ffn1"])
        KE, KET, KV = R + 4096, F1 - 0 + 10784, R + 8192
        NMAX, KSUM = R + 13312, R + 13320
        assert KET + 4096 <= R + 30720
        ke = []
        for t in range(NT):
            V.need(None)
            s = V.go(v.tensor_reduce(a(NMAX + t, 1), a(C + t * D, D), axis=AX, op=ALU.max, negate=True))
            AC.need(s)
            ke.append(AC.go(act.activation(a(KE + t * D, D), a(C + t * D, D), ACT.Exp, bias=a(NMAX + t, 1),
                                           accum_out=a(KSUM + t, 1))))
        V.need(ke[-1])
        ksum = V.go(v.reciprocal(a(KSUM, NT), a(KSUM, NT)))
        NBIAS = SMALL + 80
        V.need(*roots)
        roots.clear()
        V.need(V.go(v.tensor_tensor(a(NBIAS, NT), a(MEAN, 2 * NT, NT, 2)[:, :, 0], a(RSTD, NT), ALU.mult)))
        bias = V.go(v.tensor_scalar(a(NBIAS, NT), a(NBIAS, NT), -1.0, None, ALU.mult))
        free = [None] * 8
        for t in range(NT):
            free[t % 2] = transposed(a(KE + t * D, D), KET, t, t % 2, free[t % 2], ke[t])
        PE.need(ct_in)
        for t in range(NT):
            PE.need(free[0], free[1], free[2 + t % 2])
            for c in range(DC):
                s = PE.go(mm(bank[:, 2 + t % 2, 0:P], a(KET + c * N + t * P, P), a(CT + c * N + t * P, P), c, DC))
            V.need(s, ksum)
            free[2 + t % 2] = V.go(v.scalar_tensor_tensor(a(KV + t * P, P), bank[:, 2 + t % 2, 0:P], a(KSUM + t, 1),
                                                          const("block8"), ALU.mult, ALU.mult))
        AC.need(bias)
        for t in range(NT):
            s = AC.go(act.activation(a(XN + t * D, D), a(X + t * D, D), ACT.Exp, scale=a(RSTD + t, 1),
                                     bias=a(NBIAS + t, 1)))
            at = CONST + CONST_AT["selw"][0] + P - 16 - 16 * (t % 2)
            PE.need(s)
            s = PE.go(mm(bank[t // 2 * 32:t // 2 * 32 + 32, 4, :], A[:, at:at + 32], a(XN + t * D, D), t % 2, 2))
        V.need(s)
        rsum = V.go(v.reciprocal(a(KE, D), bank[:, 4, :]))
        PE.need(rsum)

        def query(t):
            xq, at = a(XN + t * D, D), CONST + CONST_AT["selt"][0] + t * P
            PE.need(free[t % 2])
            s = PE.go(mm(bank[:, t % 2, :], A[:, at:at + P], a(KE, D)))
            V.need(s)
            free[t % 2] = V.go(v.tensor_tensor(xq, xq, bank[:, t % 2, :], ALU.mult))
            return free[t % 2]

        queries = [query(0)]
        for t in range(NT):
            if t + 1 < NT:
                queries.append(query(t + 1))
            PE.need(queries[t], free[2], free[3], free[6 + t % 2])
            s = PE.go(mm(bank[:, 6 + t % 2, :], a(KV + t * P, P), a(XN + t * D, D)))
            V.need(s)
            free[6 + t % 2] = V.go(v.tensor_tensor(a(X + t * D, D), bank[:, 6 + t % 2, :], a(X + t * D, D), ALU.add))
            measured(t)
        boundary()

        UP = F1
        FC1 = UP + DC * INT1
        EX1 = FC1 + DC * LAT1
        FC2 = EX1 + LAT1 // P * LAT1
        DOWN = FC2 + LAT1 // P * D
        GATE1 = DOWN + INT1 // P * D
        XN1 = C
        HT = R + 5120
        LT, LE, LN1 = R + 25120, R + 27168, R + 29216
        G_OFF = LN1 + 1024
        ln1_in = load("ln1_in", LN1, dram["ln1"])
        norms, xt_done = norm_all(XN1)
        PE.need(xt_done, f1_in)
        s = logits(LT, lambda to, c, h: PE.go(mm(to, a(GATE1 + c * 8, 8), a(XT + c * N + h * HALF, HALF), c, DC)))
        V.need(s)
        V.need(V.go(v.tensor_copy(a(G_OFF, 64), bank[:, 7, 0:64])))
        for t in range(NT):
            V.go(v.max(a(G_OFF + 64 + 8 * t, 8), a(G_OFF + 8 * t, 8)))
        V.need(V.last())
        top = a(G_OFF + 64, 64, NT, 8)
        RW = G_OFF + 128
        rw = V.go(v.tensor_tensor(a(RW, NT), top[:, :, 0], top[:, :, 1], ALU.add))
        G.need(ln1_in, norms[-1])
        for t in range(NT):
            G.go(g.tensor_tensor(a(X + t * D, D), a(X + t * D, D), a(LN1 + D, D), ALU.add))
        free = [None] * 8
        n = 0

        def product(dst, w_at, cols, j, src, k, h, evac):
            nonlocal n
            b = n % 7
            n += 1
            PE.need(free[b])
            for c in range(k):
                s = PE.go(mm(bank[:, b, :], a(w_at + c * cols + j * P, P), a(src + c * N + h * HALF, HALF), c, k))
            free[b] = evac(dst + j * N + h * HALF, b, s)

        def copied(to, b, s):
            AC.need(s)
            return AC.go(act.activation(a(to, HALF), bank[:, b, :], ACT.Copy))

        def relu_squared(to, b, s):
            AC.need(s)
            s = AC.go(act.activation(a(to, HALF), bank[:, b, :], ACT.Relu))
            V.need(s)
            return V.go(v.tensor_tensor(a(to, HALF), a(to, HALF), bank[:, b, :], ALU.mult))

        for j in range(LAT1 // P):
            for h in range(2):
                product(LT, FC1, LAT1, j, XT, DC, h, copied)
        lt_done = AC.last()
        for j in range(INT1 // P):
            for h in range(2):
                product(HT, UP, INT1, j, XT, DC, h, relu_squared)
        PE.need(lt_done)
        for j in range(LAT1 // P):
            for h in range(2):
                product(LE, EX1, LAT1, j, LT, LAT1 // P, h, copied)
        PE.need(V.last(), AC.last())
        free = [None] * 8
        for t in range(NT):
            b, y = 2 * (t % 4), a(XN1 + t * D, D)
            PE.need(free[b])
            for k in range(LAT1 // P):
                s = PE.go(mm(bank[:, b + 1, :], a(LE + k * N + t * P, P), a(FC2 + k * D, D), k, LAT1 // P))
            for k in range(INT1 // P):
                s = PE.go(mm(bank[:, b, :], a(HT + k * N + t * P, P), a(DOWN + k * D, D), k, INT1 // P))
            AC.need(s)
            s = AC.go(act.activation(y, bank[:, b, :], ACT.Copy))
            V.need(s, rw)
            free[b] = s = V.go(v.scalar_tensor_tensor(y, bank[:, b + 1, :], a(RW + t, 1), y, ALU.mult, ALU.add))
            s = normalise(y, y, t, s)
            G.need(s)
            s = G.go(g.tensor_tensor(y, y, a(LN1, D), ALU.mult))
            V.need(s)
            V.go(v.tensor_tensor(a(X + t * D, D), y, a(X + t * D, D), ALU.add))
            measured(t)
        boundary()

        use("grouped", 13312, 20480)
        STG_Q, STG_O, STG_KV = R, R + 2048, R + 4096
        QT, SC = XT, C + 2048
        PT, COS, SIN, MK, MNEG = (R + 6144 + x for x in (0, 2048, 3072, 4096, 5120))
        VN, KT = R + 12288, CONST + CONST_AT["selt"][0]
        POS, WRAP = PT, PT + 1024
        ROT, QC = C, C + 1024
        XTS, WQS, WOS, ATS = (0, 0), (8192, 0), (12288, 0), (16384, 0)
        LQ, LX, LA = DC * QH2 * D2, DC * N, QH2 * HALF
        scale2 = D2 ** -0.5
        a2 = dram["attn2"]
        cuts = {"q": (0, 2048), "kv": (2048, 3072), "o": (3072, 5120)}
        lines = {n: Line(nc.sync, sem(f"group_{n}_in"), 16) for n in ("q", "kv", "o")}

        def fetch_group(g, what, to):
            lo, hi = cuts[what]
            src = a2[bass.ds(g, 1)].rearrange("a p n -> (a p) n")[:, lo:hi]
            return lines[what].go(nc.sync.dma_start(a(to, hi - lo), src))

        rope_in = load("rope_in", STG_KV, dram["rope"])
        sem_i = Line(nc.sync, sem("int_in"), 16)
        sem_i.go(nc.sync.dma_start(a(POS, N).bitcast(I32), dram["pos"]))
        sem_m = Line(nc.sync, sem("mask_in"), 16)
        sem_m.go(nc.sync.dma_start(a(MK, N).bitcast(I32), dram["mask"]))
        q_in = fetch_group(0, "q", STG_Q)
        norms = norms_of(C)
        free = [None] * 4
        for t in range(NT):
            free[t % 4] = turned_split(a(C + t * D, D), XTS, t, t % 4, free[t % 4], norms[t])
        AC.need(q_in)
        V.need(sem_m.last(), sem_i.last(), free[3])
        s = V.go(v.tensor_scalar(a(MNEG, N), a(MK, N).bitcast(I32), 0.0, None, ALU.is_equal))
        V.need(s)
        V.need(V.go(v.tensor_scalar(a(MK, N), a(MNEG, N), -1.0, 1.0, ALU.mult, ALU.add)))
        V.go(v.tensor_scalar(a(MNEG, N), a(MNEG, N), NEG / scale2, None, ALU.mult))
        V.go(v.tensor_copy(a(POS, N), a(POS, N).bitcast(I32)))
        V.need(V.last())
        V.need(V.go(v.tensor_scalar(a(WRAP, N), a(POS, N), 0.0, float(MAXPOS), ALU.is_lt, ALU.mult)))
        V.need(V.go(v.tensor_tensor(a(POS, N), a(POS, N), a(WRAP, N), ALU.add)))
        V.need(V.go(v.tensor_scalar(a(POS, N), a(POS, N), 0.0, float(MAXPOS - 1), ALU.max, ALU.min)))
        PE.need(free[3])
        for c in range(MAXPOS // P):
            V.go(v.tensor_scalar(a(XT + c * N, N), a(POS, N), const("posid")[:, c:c + 1], None, ALU.is_equal))
        PE.need(V.last(), rope_in)
        for j, to in ((0, COS), (1, SIN)):
            for h in range(2):
                b = 2 * j + h
                for c in range(MAXPOS // P):
                    s = PE.go(mm(bank[:, 4 + b, :], a(STG_KV + c * 2 * D2 + j * D2, D2), a(XT + c * N + h * HALF, HALF),
                                 c, MAXPOS // P))
                AC.need(s)
                AC.go(act.activation(a(to + h * HALF, HALF), bank[:, 4 + b, :], ACT.Copy))

        def both(at, lot):
            return (parts(at, x, lot, lot) for x in (0, 1))

        boundary()
        kv_in = fetch_group(0, "kv", STG_KV)
        fetch_group(0, "o", STG_O)
        wq_done = split(*both(WQS, LQ), a(STG_Q, 2048), q_in)
        SP.need(wq_done)
        fetch_group(1, "q", STG_Q)
        NB = 4

        class Group:

            def __init__(self, kv):
                self.wk, self.wv = kv, kv + DC * D2
                self.free, self.turned_free, self.rot_free = [None] * NB, [None, None], [None, None]
                self.n = self.r = 0

            def take(self):
                self.n += 1
                PE.need(self.free[(self.n - 1) % NB])
                return (self.n - 1) % NB

            def rotary(self, b, s, to, h):
                r = self.r % 2
                self.r += 1
                rot, qc = a(ROT + r * HALF, HALF), a(QC + r * HALF, HALF)
                AC.need(s, self.rot_free[r])
                AC.go(act.activation(rot[0:64, :], bank[64:P, b, :], ACT.Copy))
                s1 = AC.go(act.activation(rot[64:P, :], bank[0:64, b, :], ACT.Copy))
                V.need(s1)
                s2 = self.free[b] = V.go(v.tensor_tensor(qc, bank[:, b, :], a(COS + h * HALF, HALF), ALU.mult))
                G.need(s1)
                s3 = G.go(g.tensor_tensor(rot, rot, a(SIN + h * HALF, HALF), ALU.mult))
                V.need(s3, s2)
                if len(to.shape) == 3:
                    qc, rot = (x.rearrange("p (b s) -> p b s", b=8) for x in (qc, rot))
                s = self.rot_free[r] = V.go(v.tensor_tensor(to, qc, rot, ALU.add))
                return s

            def k_rows(self, h, wk):
                b = self.take()
                for c in range(DC):
                    s = PE.go(mm(bank[:, b, :], a(wk + c * D2, D2), a(CT + c * N + h * HALF, HALF), c, DC))
                return self.rotary(b, s, a(KT + h * HALF, HALF), h)

            def q_rows(self, q, h, between=None):
                b = self.take()
                for c in range(DC):
                    s = mm3(bank[:, b, :], lambda x: parts(WQS, x, LQ, LQ)[:, c * QH2 * D2 + q * D2:][:, 0:D2],
                            lambda x: parts(XTS, x, LX, LX)[:, c * N + h * HALF:c * N + (h + 1) * HALF], c, DC)
                    if between:
                        between()
                return self.rotary(b, s, a(QT + h * QH2 * HALF, QH2 * HALF, 8, QH2, S)[:, :, q, :], h)

            def v_rows(self, h):
                b = self.take()
                for t in range(4):
                    for c in range(DC):
                        s = PE.go(mm(bank[:, b, t * P:(t + 1) * P], a(CT + c * N + (4 * h + t) * P, P),
                                     a(self.wv + c * D2, D2), c, DC))
                AC.need(s)
                s = self.free[b] = AC.go(act.activation(a(VN + h * HALF, HALF), bank[:, b, :], ACT.Copy))
                return s

            def scorer(self, h, *after):
                PE.need(*after)
                todo = [(bb, hp) for bb in range(8) for hp in range(2)]

                def four():
                    for bb, hp in todo[:4]:
                        at = (bb // 2 * 4 + hp * 2 + bb % 2) * 64
                        self.scored = PE.go(mm(bank[:, 4 + at // 512, at % 512:at % 512 + 64],
                                               a(QT + ((8 * h + bb) * QH2 + 2 * hp) * S, 2 * S),
                                               a(KT + (8 * h + bb) * S, S)))
                    del todo[:4]
                return four

            def softmax_exp(self, h):
                sc = SC + h * 1024
                mk, mn = (a(at + h * HALF, HALF, 4, P).unsqueeze(2).broadcast_to([P, 4, 2, P]) for at in (MK, MNEG))
                s4 = a(sc, 1024).rearrange("p (b h k) -> p b h k", b=4, h=2)
                rows, top = a(sc, 1024, 16, 64), a(SOFT + 32 * h, 16)
                V.need(self.scored)
                self.read = V.go(v.tensor_tensor(s4, bank[:, 4:6, :].rearrange("p a (b h k) -> p (a b) h k", b=2, h=2),
                                                 mk, ALU.mult))
                V.need(self.read)
                V.need(V.go(v.tensor_tensor(s4, s4, mn, ALU.add)))
                V.need(V.go(v.tensor_reduce(top, rows, axis=AX, op=ALU.max)))
                s = V.go(v.tensor_tensor(rows, rows, top.unsqueeze(2).broadcast_to([P, 16, 64]), ALU.subtract))
                AC.need(s)
                return AC.go(act.activation(rows, rows, ACT.Exp, scale=scale2))

            def softmax_scale(self, h, s):
                rows, tot = a(SC + h * 1024, 1024, 16, 64), a(SOFT + 32 * h + 16, 16)
                V.need(s)
                V.need(V.go(v.tensor_reduce(tot, rows, axis=AX, op=ALU.add)))
                s = V.go(v.reciprocal(tot, tot))
                G.need(s)
                return G.go(g.tensor_tensor(rows, rows, tot.unsqueeze(2).broadcast_to([P, 16, 64]), ALU.mult))

            def turn(self, h, att):
                for k in range(2):
                    PE.need(att, self.turned_free[k])
                    for j in range(4):
                        s = PE.go(pe.transpose(bank[:, 6 + k, j * P:(j + 1) * P],
                                               a(SC + h * 1024 + (4 * k + j) * P, P), const("ident")))
                    AC.need(s)
                    self.turned_free[k] = AC.go(act.activation(a(PT + h * 1024 + k * 512, 512), bank[:, 6 + k, :],
                                                               ACT.Copy))

            def apply(self, h, v_ready):
                out = []
                for k in range(2):
                    PE.need(v_ready, self.turned_free[k])
                    pair = (self.take(), self.take())
                    for bp in (2 * k, 2 * k + 1):
                        for b2, b in enumerate(pair):
                            rows = slice(b2 * 64, b2 * 64 + 64)
                            s = PE.go(mm(bank[:, b, (bp % 2) * 256:(bp % 2 + 1) * 256],
                                         a(VN + (4 * h + bp) * P, P)[rows, :],
                                         a(PT + h * 1024 + bp * 256, 256)[rows, :]))
                    for b2, b in enumerate(pair):
                        hi, lo = (parts(ATS, x, LA, LA, QH2, HALF)[:, :, 2 * k * P:(2 * k + 2) * P]
                                  .rearrange("p h (b c q) -> p b h c q", b=2, c=2)[:, :, :, b2, :] for x in (0, 1))
                        self.free[b] = split(hi, lo, bank[:, b, :].rearrange("p (b h q) -> p b h q", b=2, h=QH2), s)
                        out.append(self.free[b])
                return out

            def output(self, t, h, ready):
                PE.need(ready)
                b = self.take()
                for q in range(QH2):
                    s = mm3(bank[:, b, :], lambda x: parts(ATS, x, LA, LA)[:, q * HALF + t * P:q * HALF + (t + 1) * P],
                            lambda x: parts(WOS, x, LQ, LQ)[:, q * D:(q + 1) * D], q, QH2)
                x = a(X + (4 * h + t) * D, D)
                V.need(s)
                self.free[b] = V.go(v.tensor_tensor(x, bank[:, b, :], x, ALU.add))
                return s

        SOFT = SMALL + 700
        first = Group(STG_KV)
        PE.need(kv_in)
        for h in range(2):
            first.k_rows(h, STG_KV)
        PE.need(wq_done)
        for q in range(QH2):
            first.q_rows(q, 0)
        with Turns(G2 // 2, {**dict(zip(engines, GROUP_MARKS)), lines["q"]: 32, lines["kv"]: 32,
                             lines["o"]: 32}) as i:
            start = {ln: ln.last() for ln in engines}
            ahead = [nc.sync.snap((2 * i + x) % G2, min_val=0, max_val=G2 - 1) for x in (1, 2, 3)]
            for x in range(2):
                gr = Group(STG_KV + x * 1024)
                if x:
                    gr.free, gr.turned_free, gr.rot_free = last.free, last.turned_free, last.rot_free
                    gr.n, gr.r = last.n, last.r
                else:
                    gr.free = [start[V]] * NB
                    gr.turned_free, gr.rot_free = [start[AC]] * 2, [start[V]] * 2
                last = gr
                o_here = lines["o"].last()
                SP.need(PE.last())
                kv_next = fetch_group(ahead[x], "kv", STG_KV + (1 - x) * 1024)
                next_k = STG_KV + (1 - x) * 1024
                wo_done = split(*both(WOS, LQ), a(STG_O, 2048), o_here, PE.last())
                SP.need(wo_done)
                fetch_group(ahead[x], "o", STG_O)
                four = gr.scorer(0, *((read, next_k1) if x else (start[V],)))
                gr.q_rows(0, 1, four)
                e = gr.softmax_exp(0)
                gr.q_rows(1, 1)
                att0 = gr.softmax_scale(0, e)
                gr.q_rows(2, 1)
                q1 = gr.q_rows(3, 1)
                q_here = lines["q"].last()
                q_split = split(*both(WQS, LQ), a(STG_Q, 2048), q_here, PE.last(), low=G)
                SP.need(q_split)
                fetch_group(ahead[x + 1], "q", STG_Q)
                v0, v1 = gr.v_rows(0), gr.v_rows(1)
                gr.turn(0, att0)
                PE.need(kv_next)
                gr.k_rows(0, next_k)
                ats = gr.apply(0, v0)
                four = gr.scorer(1, q1, gr.read)
                PE.need(q_split)
                gr.q_rows(0, 0, four)
                e = gr.softmax_exp(1)
                PE.need(wo_done)
                gr.output(0, 0, ats[1])
                gr.output(1, 0, ats[1])
                att1 = gr.softmax_scale(1, e)
                gr.output(2, 0, ats[3])
                out0 = gr.output(3, 0, ats[3])
                gr.q_rows(1, 0)
                gr.turn(1, att1)
                gr.q_rows(2, 0)
                AC.need(out0)
                ats = gr.apply(1, v1)
                gr.q_rows(3, 0)
                next_k1 = gr.k_rows(1, next_k)
                for t in range(4):
                    gr.output(t, 1, ats[1] if t < 2 else ats[3])
                read = gr.read
        SP.need(*(lines[n].last() for n in lines))
        boundary()

        use("dense", 30720)
        WT2, CENT2 = R + 12288, C + 2048
        w2_in = load("weight2_in", WT2, dram["ffn2"][:, 0:DC * D])
        cent_in = load("cent_in", CENT2, dram["ffn2"][:, DC * D:])
        W3, WO3, SM3 = R, R + 9248, R + 8192
        XN2 = R + 19456
        DT, ASG, AHOT, RSEL, ONES, YD, QSEL = (R + 14336 + 512 * j for j in range(7))
        w3_in = load("attn3_in", W3, dram["attn3"])
        wo3_in = load("wo3_in", WO3, dram["wo3"])
        sm3_in = load("small3_in", SM3, dram["small3"])
        asg_line = Line(nc.sync, sem("assign_in"), 16)
        asg_in = asg_line.go(nc.sync.dma_start(a(ASG, D).bitcast(I32), dram["assign"]))
        norms, xt_done = norm_all(XN2)
        V.need(asg_in)
        V.go(v.memset(a(ONES, P), 1.0))
        V.need(V.go(v.tensor_copy(a(ASG, D), a(ASG, D).bitcast(I32))))
        V.need(V.go(v.tensor_scalar(a(AHOT, D), a(ASG, D), 0.0, float(NCL), ALU.is_lt, ALU.mult)))
        V.need(V.go(v.tensor_tensor(a(ASG, D), a(ASG, D), a(AHOT, D), ALU.add)))
        V.need(V.go(v.tensor_scalar(a(ASG, D), a(ASG, D), 0.0, float(NCL - 1), ALU.max, ALU.min)))
        ahot = V.go(v.tensor_scalar(a(AHOT, D), a(ASG, D), const("posid")[:, 0:1], None, ALU.is_equal))
        PE.need(xt_done, cent_in, w2_in)
        for t in range(NT):
            for c in range(DC):
                s = PE.go(mm(bank[:, 7, t * NCL:(t + 1) * NCL], a(XT + c * N + t * P, P), a(CENT2 + c * NCL, NCL),
                             c, DC))
        dt, top8 = a(DT, 512, NT, NCL), a(QSEL, NT)
        wide8 = top8.unsqueeze(2).broadcast_to([P, NT, NCL])
        b7 = bank[:, 7, :].rearrange("p (t n) -> p t n", t=NT)
        V.need(s)
        V.need(V.go(v.tensor_reduce(top8, b7, axis=AX, op=ALU.max)))
        s = V.go(v.tensor_tensor(dt, b7, wide8, ALU.subtract))
        AC.need(s)
        s = AC.go(act.activation(dt, dt, ACT.Exp, scale=10.0))
        V.need(s)
        V.need(V.go(v.tensor_reduce(top8, dt, axis=AX, op=ALU.add)))
        V.need(V.go(v.reciprocal(top8, top8)))
        V.need(V.go(v.tensor_tensor(dt, dt, wide8, ALU.mult)))
        hit = V.go(v.tensor_scalar(dt, dt, 0.01, None, ALU.is_gt))
        V.need(hit)
        qsel = V.go(v.tensor_reduce(top8, dt, axis=AX, op=ALU.max))
        PE.need(hit)
        for t in range(NT):
            s = PE.go(mm(bank[0:NCL, 6, 0:1], a(DT + t * NCL, NCL), a(ONES, 1), t, NT))
        V.need(s)
        s = V.go(v.tensor_scalar(a(QSEL + 16, 1)[0:NCL, :], bank[0:NCL, 6, 0:1], 0.0, None, ALU.is_gt))
        V.need(s)
        s = V.go(v.tensor_scalar(a(QSEL + 32, P)[0:NCL, :], a(ONES, P)[0:NCL, :], a(QSEL + 16, 1)[0:NCL, :], None,
                                 ALU.mult))
        PE.need(s, ahot)
        s = PE.go(mm(bank[:, 5, :], a(QSEL + 32, P)[0:NCL, :], a(AHOT, D)[0:NCL, :]))
        AC.need(s)
        rsel = AC.go(act.activation(a(RSEL, D), bank[:, 5, :], ACT.Copy))
        free = [None] * 4
        yfree = [None, None]
        YS = [YD, QSEL + 256]
        for t in range(NT):
            b, y = t % 4, a(YS[t % 2], D)
            PE.need(free[b])
            for c in range(DC):
                s = PE.go(mm(bank[:, b, :], a(XT + c * N + t * P, P), a(WT2 + c * D, D), c, DC))
            V.need(s)
            s = free[b] = V.go(v.tensor_tensor(y, bank[:, b, :], a(CENT2 + DC * NCL, D), ALU.add))
            G.need(s, rsel)
            s = G.go(g.tensor_tensor(y, y, a(RSEL, D), ALU.mult))
            V.need(s, qsel)
            x = a(X + t * D, D)
            V.go(v.scalar_tensor_tensor(x, y, a(QSEL + t, 1), x, ALU.mult, ALU.add))
            measured(t)
        FW, MIX, SI, BQK, BVB, BVS = R + 24576, R + 11296, R + 8736, R + 8760, R + 6144, R + 6656
        V.need(sm3_in)
        V.need(V.go(v.tensor_scalar(a(SI, 16), a(SM3 + 12, 16), 0.1, a(SM3 + 28, 1), ALU.mult, ALU.mult)))
        for T in range(DC):
            mix = a(MIX + T * P, P)
            s = V.go(v.tensor_tensor(mix.rearrange("p (a b) -> p a b", b=M3),
                                     const("block4").rearrange("p (a b) -> p a b", b=M3),
                                     a(SI + 4 * T, M3).unsqueeze(1).broadcast_to([P, P // M3, M3]), ALU.mult))
            V.need(s)
            V.go(v.tensor_tensor(mix, mix, const("ident"), ALU.add))
            V.go(v.tensor_scalar(a(BVB + T * P, P), a(ONES, P), a(SM3 + 8 + T, 1), None, ALU.mult))
        PE.need(V.last(), w3_in)
        free = [V.last()] * 8
        n = 0
        for w in range(3):
            for c in range(DC):
                PE.need(free[n % 4])
                for T in range(DC):
                    s = PE.go(mm(bank[:, n % 4, T * P:(T + 1) * P], a(W3 + w * 2048 + T * D + c * P, P),
                                 a(MIX + T * P, P)))
                AC.need(s)
                free[n % 4] = AC.go(act.activation(a(FW + w * 2048 + c * D, D), bank[:, n % 4, :], ACT.Copy))
                n += 1
        for j in range(8):
            s = PE.go(mm(bank[:, 6, j:j + 1], a(MIX + j % DC * P, P), a(SM3 + j, 1)))
        for T in range(DC):
            s = PE.go(mm(bank[:, 7, T * P:(T + 1) * P], a(BVB + T * P, P), a(MIX + T * P, P)))
        AC.need(s)
        AC.go(act.activation(a(BQK, 8), bank[:, 6, 0:8], ACT.Copy))
        AC.go(act.activation(a(BVS, D), bank[:, 7, :], ACT.Copy))
        boundary()

        QT3, KT3, VN3, OT = R + 12288, R + 16384, C, R + 20480
        XN3 = R + 20480
        VX, PT3, QX, PR = R + 24576, R + 26624, R + 28672, CT
        VD = XT
        W1 = R
        scale3 = 8 ** -0.5
        free = [None] * 8
        n = 0

        def feature_rows(w, src, dst):
            nonlocal n
            for T in range(DC):
                for h in range(2):
                    b = n % 8
                    n += 1
                    PE.need(free[b])
                    for c in range(DC):
                        s = PE.go(mm(bank[:, b, :], a(FW + w * 2048 + c * D + T * P, P), a(src + c * N + h * HALF, HALF),
                                     c, DC))
                    AC.need(s)
                    free[b] = AC.go(act.activation(a(dst + T * N + h * HALF, HALF), bank[:, b, :], ACT.Identity,
                                                   bias=a(BQK + 4 * w + T, 1)))

        norm3 = norms_of(XN3)
        feature_rows(1, CT, KT3)
        for t in range(NT):
            b = n % 8
            n += 1
            PE.need(free[b])
            for c in range(DC):
                s = PE.go(mm(bank[:, b, :], a(CT + c * N + t * P, P), a(FW + 4096 + c * D, D), c, DC))
            V.need(s)
            free[b] = V.go(v.tensor_tensor(a(VN3 + t * D, D), bank[:, b, :], a(BVS, D), ALU.add))
        vn_done = V.last()
        for t in range(NT):
            b = n % 8
            n += 1
            free[b] = transposed(a(XN3 + t * D, D), XT, t, b, free[b], norm3[t])
            G.need(norm3[t])
            G.go(g.tensor_tensor(a(X + t * D, D), a(X + t * D, D), a(SM3 + 29, D), ALU.add))
        PE.need(AC.last())
        feature_rows(0, XT, QT3)
        boundary()
        w1_in = load("w1_in", W1, dram["w1"])
        vd_line = Line(nc.sync, sem("v_copies"), 16)
        UN = 8

        def copy_v(T):
            for rep in range(2):
                for b2 in range(2):
                    dst = a(VD, 16 * P, NT, 2, P)[rep * S:(rep + 1) * S, :, b2, :]
                    src = A[b2 * S:(b2 + 1) * S, VN3:VN3 + NT * D].rearrange("p (t f) -> p t f", t=NT)
                    s = vd_line.go(nc.sync.dma_start(dst, src[:, :, bass.ds(T * P, P)]))
            return s

        def v_masked(q, vd_in, *after):
            G.need(vd_in, *after)
            return G.go(g.tensor_tensor(a(VX + q * D, D).rearrange("p (f m) -> p f m", m=M3),
                                        a(VD + q * D, D).rearrange("p (f m) -> p f m", m=M3),
                                        const("m_half").unsqueeze(1).broadcast_to([P, P, M3]), ALU.mult))

        class Unit:

            def __init__(self, u):
                self.u = u
                self.pr = PR + u % 4 * 1024
                self.qx, self.kx = QX + u % 2 * 1024, QX + u % 2 * 1024 + 512
                self.top, self.tot = SOFT + u % 2 * 16, SOFT + 32 + u % 2 * 16

            def wide(self, at):
                return a(at, 16).unsqueeze(2).broadcast_to([P, 16, S])

            def prepare(self, T, *after):
                AC.need(*after)
                G.need(*after)
                q, k = (a(at + self.u * P, P, 2, S, off=T * N)
                        for at in (QT3, KT3))
                for m in range(M3):
                    self.qx_done = AC.go(act.activation(a(self.qx, 512, 2, M3, S)[:, :, m, :], q, ACT.Copy,
                                                        scale=const("is_m")[:, m:m + 1]))
                self.kx_done = G.go(g.tensor_tensor(
                    a(self.kx, 512, 2, 4, S), k.unsqueeze(2).broadcast_to([P, 2, 4, S]),
                    const("is_h").unsqueeze(1).unsqueeze(3).broadcast_to([P, 2, 4, S]), ALU.mult))

            def score(self, *after):
                b = self.u % 2 * 2
                PE.need(*after)
                for b2 in range(2):
                    for mp in range(2):
                        to = bank[:, b + b2, :].rearrange("p (h m k) -> p h m k", h=4, m=2)[:, :, mp, :]
                        s = PE.go(mm(to, a(self.qx + (b2 * 4 + 2 * mp) * S, P), a(self.kx + b2 * 256, 256, 4, S)))
                self.scored = s
                scores = bank[:, b:b + 2, :].rearrange("p h (g k) -> p (h g) k", k=S)
                pr = a(self.pr, 1024, 16, S)
                V.need(s)
                V.need(V.go(v.tensor_reduce(a(self.top, 16), scores, axis=AX, op=ALU.max)))
                s = self.read = V.go(v.tensor_tensor(pr, scores, self.wide(self.top), ALU.subtract))
                AC.need(s)
                self.exp = AC.go(act.activation(pr, pr, ACT.Exp, scale=scale3))

            def divide(self, before):
                pr = a(self.pr, 1024, 16, S)
                V.need(self.exp, before)
                V.need(V.go(v.tensor_reduce(a(self.tot, 16), pr, axis=AX, op=ALU.add)))
                s = V.go(v.reciprocal(a(self.tot, 16), a(self.tot, 16)))
                G.need(s)
                self.done = G.go(g.tensor_tensor(pr, pr, self.wide(self.tot), ALU.mult))

            def turn(self, evac):
                for k in range(2):
                    PE.need(self.done, evac)
                    for h in range(4):
                        s = PE.go(pe.transpose(bank[:, 4 + k, h * P:(h + 1) * P],
                                               a(self.pr + (k * 4 + h) * P, P), const("ident")))
                    AC.need(s)
                    self.copied = AC.go(act.activation(a(PT3 + self.u % 2 * 1024 + k * 512, 512),
                                                       bank[:, 4 + k, :], ACT.Copy))

            def times_v(self, *after):
                PE.need(self.copied, *after)
                for b2 in range(2):
                    for h in range(4):
                        s = PE.go(mm(bank[32 * h:32 * h + 32, 6 + self.u % 2, b2 * P:(b2 + 1) * P],
                                     a(VX + (2 * self.u + b2) * P + 32 * h, 32),
                                     a(PT3 + self.u % 2 * 1024 + (b2 * 4 + h) * P, P)))
                return s

            def keep(self, T, s):
                o2 = bank[:, 6 + self.u % 2, 0:256].rearrange("p (b m r) -> p b m r", b=2, m=2)
                to = a(OT + self.u * P, P, 2, S, off=T * N)
                odd = const("is_odd")
                V.need(s)
                V.need(V.go(v.tensor_scalar(to, o2[:, :, 0, :], odd[:, 0:1], None, ALU.mult)))
                self.kept = V.go(v.scalar_tensor_tensor(to, o2[:, :, 1, :], odd[:, 1:2], to, ALU.mult, ALU.add))

        vd_in = copy_v(0)
        first = [Unit(0), Unit(1), Unit(2)]
        first[0].prepare(0)
        first[1].prepare(0)
        for q in range(3):
            v_masked(q, vd_in)
        first[0].score(first[0].qx_done, first[0].kx_done)
        first[0].divide(None)
        first[2].prepare(0, first[0].scored)
        first[1].score(first[1].qx_done, first[1].kx_done)
        v_masked(3, vd_in)
        with Turns(DC, {PE: 20 * UN, V: 6 * UN, G: 2 * UN + 4, AC: 7 * UN, vd_line: 64}) as T:
            nxt = (T + 1) % DC
            SP.need(G.last())
            vd_in = copy_v(nxt)
            v_start, ac_start, g_start = V.last(), AC.last(), G.last()
            units = dict(enumerate(first))
            units[0].done, units[1].exp = G.at(G.n - 2), ac_start
            units[2].qx_done, units[2].kx_done = ac_start, G.at(G.n - 1)
            vx = [G.at(G.n - 2)] * 3 + [g_start]
            for u in range(UN):
                w = u + 2
                units[u].turn(units[u - 1].copied if u else ac_start)
                units[u + 1].divide(units[u - 1].done if u else g_start)
                units[w + 1] = Unit((w + 1) % UN)
                units[w + 1].prepare(T if w + 1 < UN else nxt, units[u + 1].scored if u else PE.last())
                units[w].score(units[w].qx_done, units[w].kx_done, units[u].read if u > 1 else v_start)
                s = units[u].times_v(vx[u // 2], units[u - 2].kept if u > 1 else None)
                units[u].keep(T, s)
                if u % 2:
                    v_masked(u // 2, vd_in, s)
        PE.need(V.last(), wo3_in)
        G.need(G.last())
        V.need(G.last())
        free = [None] * 4
        for t in range(NT):
            b = t % 4
            PE.need(free[b])
            for c in range(DC):
                s = PE.go(mm(bank[:, b, :], a(OT + c * N + t * P, P), a(WO3 + c * D, D), c, DC))
            V.need(s)
            x = a(X + t * D, D)
            free[b] = V.go(v.tensor_tensor(x, bank[:, b, :], x, ALU.add))
            measured(t)
        boundary()

        C1, C2, W2, LOW = R + 7168, R + 9248, R + 12288, R + 19456
        RING = 3
        EQ, HS, HTS, TOPS = R + 20480, R + 20480 + RING * D, R + 20480 + 2 * RING * D, R + 20480 + 3 * RING * D
        c1_in = load("c1_in", C1, dram["c1"])
        c2_in = load("c2_in", C2, dram["c2"], part=RANK)
        w2_in = load("w2_in", W2, dram["w2"])
        norms, xt_done = norm_all(C)
        PE.need(xt_done, c1_in)
        for h in range(2):
            for c in range(DC):
                s = PE.go(mm(bank[0:RANK, 2 + h, :], a(C1 + c * RANK, RANK), a(XT + c * N + h * HALF, HALF), c, DC))
            AC.need(s)
            s = AC.go(act.activation(a(LOW + h * HALF, HALF)[0:RANK, :], bank[0:RANK, 2 + h, :], ACT.Copy))
        PE.need(s, c2_in, w1_in, w2_in)
        units = [(t, j) for t in range(NT) for j in range(4)]
        inter_read, h_read, hs_done, picked, turned, hts, outed = {}, {}, {}, {}, {}, {}, {}
        eq_done = {}
        stored = sem("stored")
        for u in range(len(units) + 2):
            if u < len(units):
                t, j = units[u]
                wd = min(D, INTER - j * D)
                nb = wd // BLK
                bi, bh, ring = u % 2, 2 + u % 2, u % RING
                eq = a(EQ + ring * D, wd)
                blocks = eq.rearrange("p (n k) -> p n k", k=BLK)
                tops = a(TOPS + ring * 32, nb)
                PE.need(inter_read.get(u - 2))
                s1 = PE.go(mm(bank[:, bi, 0:wd], a(LOW + t * P, P)[0:RANK, :], a(C2 + j * D, wd)[0:RANK, :]))
                PE.need(h_read.get(u - 2))
                for c in range(DC):
                    s2 = PE.go(mm(bank[:, bh, 0:wd], a(XT + c * N + t * P, P), a(W1 + c * INTER + j * D, wd), c, DC))
                hs_done[u] = s2
                inter = bank[:, bi, 0:wd].rearrange("p (n k) -> p n k", k=BLK)
                V.need(s1)
                V.need(V.go(v.tensor_reduce(tops, inter, axis=AX, op=ALU.max)))
                s = inter_read[u] = V.go(v.tensor_tensor(blocks, inter, tops.unsqueeze(2).broadcast_to([P, nb, BLK]),
                                                         ALU.is_equal))
                G.need(s)
                eq_done[u] = G.go(g.tensor_tensor(blocks, blocks, const("down32").unsqueeze(1)
                                                  .broadcast_to([P, nb, BLK]), ALU.mult))
            if 0 <= u - 1 < len(units):
                w = u - 1
                t, j = units[w]
                wd = min(D, INTER - j * D)
                nb = wd // BLK
                ring = w % RING
                eq = a(EQ + ring * D, wd)
                blocks = eq.rearrange("p (n k) -> p n k", k=BLK)
                tops = a(TOPS + ring * 32, nb)
                V.need(eq_done[w])
                V.need(V.go(v.tensor_reduce(tops, blocks, axis=AX, op=ALU.max)))
                s = V.go(v.tensor_tensor(blocks, blocks, tops.unsqueeze(2).broadcast_to([P, nb, BLK]), ALU.is_equal))
                V.need(s, hs_done[w], turned.get(w - RING))
                h_read[w] = V.go(v.scalar_tensor_tensor(a(HS + ring * D, wd), bank[:, 2 + w % 2, 0:wd], 0.0, eq,
                                                        ALU.max, ALU.mult))
            if 0 <= u - 2 < len(units):
                w = u - 2
                t, j = units[w]
                wd = min(D, INTER - j * D)
                ring = w % RING
                b = 4 + w % 2
                PE.need(h_read[w], hts.get(w - 2))
                for k in range(wd // P):
                    s = PE.go(pe.transpose(bank[:, b, k * P:(k + 1) * P], a(HS + ring * D + k * P, P), const("ident")))
                turned[w] = s
                AC.need(s, outed.get(w - RING))
                hts[w] = s = AC.go(act.activation(a(HTS + ring * D, wd), bank[:, b, 0:wd], ACT.Copy))
                PE.need(s)
                ob = 6 + t % 2
                if j == 0:
                    PE.need(outed.get(("x", t - 2)))
                for k in range(wd // P):
                    f = j * 4 + k
                    s = PE.go(mm(bank[:, ob, :], a(HTS + ring * D + k * P, P), a(W2 + f * D, D), f, NI))
                outed[w] = s
                if j == 3:
                    x = a(X + t * D, D)
                    V.need(s)
                    s = outed[("x", t)] = V.go(v.tensor_tensor(x, bank[:, ob, :], x, ALU.add))
                    SP.need(s)
                    nc.sync.dma_start(out[t * P:(t + 1) * P, :], x).then_inc(stored, 16)
        nc.sync.wait_ge(stored, 16 * NT)


def kernel(**inputs):
    import concourse.bacc as _bacc
    from concourse.bass_utils import run_bass_kernel_spmd as _run

    nc = _bacc.Bacc("TRN2", target_bir_lowering=False, num_devices=1)
    arrays = lay_out(inputs)
    dram = {n: nc.dram_tensor(f"in_{n}", v.shape, mybir.dt.from_np(v.dtype), kind="ExternalInput").ap()
            for n, v in arrays.items()}
    out = nc.dram_tensor("out", (N, D), F32, kind="ExternalOutput").ap()
    program(nc, dram, out)
    r = _run(nc, [{f"in_{n}": v for n, v in arrays.items()}], core_ids=[0])
    return r.results[0]["out"].reshape(B, S, D)
```
